# Optimizing a Trainium2 kernel written in Bass

```python
import numpy as np
import jax
import jax.numpy as jnp

def _softmax(x, axis=-1):
    return jax.nn.softmax(x, axis=axis)

def _gelu(x):
    return jax.nn.gelu(x, approximate=True)

def _silu(x):
    return jax.nn.silu(x)

def _sigmoid(x):
    return jax.nn.sigmoid(x)

def _layernorm(x, axis=-1, eps=1e-05):
    m = jnp.mean(x, axis=axis, keepdims=True)
    v = jnp.var(x, axis=axis, keepdims=True)
    return (x - m) / jnp.sqrt(v + eps)

def _scatter_add(tgt, idx, src, axis=0):
    return tgt.at[idx].add(src)

def _segment_sum(src, seg, n):
    return jax.ops.segment_sum(src, seg, n)
kernel_name = 'mk_adaln_ffn_d4_seqx_r4_ce993a'

def setup_inputs(seed: int=0):
    np.random.seed(seed)
    _w = jnp.asarray

    def _rec_inputs():
        import jax
        import jax.numpy as jnp
        _rk = jax.random.key(seed)
        x = -0.0002928 + 1 * jax.random.normal(jax.random.fold_in(_rk, 1), (2, 1024, 256), jnp.float32)
        _lenS = 1024 - jax.random.randint(jax.random.fold_in(_rk, 7), (2,), 0, max(1, 1024 // 4) + 1, jnp.int32)
        _lenS2 = 1024 - jax.random.randint(jax.random.fold_in(_rk, 8), (2,), 0, max(1, 1024 // 4) + 1, jnp.int32)
        fside_16xSxS_0 = -5.72187e-05 + 0.999849 * jax.random.normal(jax.random.fold_in(_rk, 11), (16, 1024, 1024), jnp.float32)
        cond_64 = -0.0265395 + 0.99382 * jax.random.normal(jax.random.fold_in(_rk, 13), (2, 64), jnp.float32)
        _validS = jnp.arange(1024)[None, :] < _lenS[:, None]
        _validS2 = jnp.arange(1024)[None, :] < _lenS2[:, None]
        _causal = jnp.tril(jnp.ones((1024, 1024), dtype=bool))
        mask_BxS_bk0 = jnp.logical_not(jnp.broadcast_to(_validS[:, :], (2, 1024)))
        mask_BxS_bf1 = jnp.ones((2, 1024), dtype=bool)
        return (x, fside_16xSxS_0, cond_64, mask_BxS_bk0, mask_BxS_bf1)
    x, fside_16xSxS_0, cond_64, mask_BxS_bk0, mask_BxS_bf1 = _rec_inputs()

    def _L0_cond_setup():
        import jax, jax.numpy as jnp
        import numpy as np
        B, N, DIM, H, DH = (2, 512, 256, 16, 64)
        INNER = H * DH
        EPS = 1e-05

        def layernorm(x, g):
            mean = jnp.mean(x, axis=-1, keepdims=True)
            var = jnp.var(x, axis=-1, keepdims=True)
            return (x - mean) * jax.lax.rsqrt(var + EPS) * g
        key = jax.random.key(seed)
        ks = jax.random.split(key, 10)
        x = jax.random.normal(ks[0], (B, N, DIM), dtype=jnp.float32)
        attn_bias = jax.random.normal(ks[1], (H, N, N), dtype=jnp.float32)
        mask = jax.random.randint(ks[2], (B, N), 0, 2).astype(bool)
        g_in = jnp.ones((DIM,), dtype=jnp.float32)
        null_attn_bias = jax.random.normal(ks[3], (H,), dtype=jnp.float32)
        null_kv = jax.random.normal(ks[4], (2, DH), dtype=jnp.float32)
        Wq = jax.random.normal(ks[5], (DIM, INNER), dtype=jnp.float32) * 0.02
        Wkv = jax.random.normal(ks[6], (DIM, 2 * DH), dtype=jnp.float32) * 0.02
        Wo = jax.random.normal(ks[7], (INNER, DIM), dtype=jnp.float32) * 0.02
        g_out = jnp.ones((DIM,), dtype=jnp.float32)
        return {'x': x, 'attn_bias': attn_bias, 'mask': mask, 'g_in': g_in, 'null_attn_bias': null_attn_bias, 'null_kv': null_kv, 'Wq': Wq, 'Wkv': Wkv, 'Wo': Wo, 'g_out': g_out}
    _L0_cond_all = _L0_cond_setup()
    _L0_cond_in = {k: v for k, v in _L0_cond_all.items() if k in ('g_in', 'null_attn_bias', 'Wq', 'Wkv', 'Wo', 'g_out')}
    del _L0_cond_all

    def _L0_ffn_setup():
        import jax, jax.numpy as jnp
        import numpy as np
        B, S, D, H, E = (8, 512, 256, 1024, 16)
        key = jax.random.key(seed)
        ks = jax.random.split(key, 4)
        sd = 1.0 / np.sqrt(D).astype(np.float32)
        sh = 1.0 / np.sqrt(H).astype(np.float32)
        return {'x': jax.random.normal(ks[0], (B, S, D), jnp.float32), 'Wg': jax.random.normal(ks[1], (D, E), jnp.float32) * sd, 'bg': jnp.zeros((E,), jnp.float32), 'W1': jax.random.normal(ks[2], (E, D, H), jnp.float32) * sd, 'b1': jnp.zeros((E, H), jnp.float32), 'W2': jax.random.normal(ks[3], (E, H, D), jnp.float32) * sh, 'b2': jnp.zeros((E, D), jnp.float32)}
    _L0_ffn_all = _L0_ffn_setup()
    _L0_ffn_in = {k: v for k, v in _L0_ffn_all.items() if k in ('Wg', 'bg', 'W1', 'b1', 'W2', 'b2')}
    del _L0_ffn_all

    def _L1_cond_setup():
        import jax, jax.numpy as jnp
        import numpy as np
        B, S, H = (4, 512, 256)
        E = 8
        M = 128
        K = 2
        N_SHARED = 2
        SM = M * N_SHARED
        G = 64
        GE_TEMP = 1.0
        ALPHA = 0.001
        SEQ_AUX = True
        NORM_TOPK = True
        COS_TEMP = 0.78
        CONS_ALPHA = 0.01
        LEAKY_SLOPE = 0.01
        EPS_COS = 1e-08

        def _leaky(x):
            return jnp.where(x >= 0, x, LEAKY_SLOPE * x)

        def _moe_forward(hidden_states, g, wt, wg, w_gate, w_up, w_down, sw_gate, sw_up, sw_down):
            b, s, h = hidden_states.shape
            x = hidden_states.reshape(-1, h)
            T = x.shape[0]
            logits_h = x @ wt.T
            logits_g = g @ wg.T
            logits_g = jnp.repeat(logits_g, s, axis=0)
            logits = (logits_h + logits_g / GE_TEMP) / (1.0 + 1.0 / GE_TEMP)
            scores = jax.nn.softmax(logits, axis=-1)
            topk_w, topk_idx = jax.lax.top_k(scores, K)
            if K > 1 and NORM_TOPK:
                topk_w = topk_w / (topk_w.sum(-1, keepdims=True) + 1e-20)
            onehot = jax.nn.one_hot(topk_idx.reshape(b, s * K), E, dtype=jnp.float32)
            ce = onehot.sum(1) / (s * K / E)
            aux_loss = (ce * scores.reshape(b, s, E).mean(1)).sum(1).mean() * ALPHA
            gp = _leaky(jnp.einsum('th,ehm->etm', x, w_gate))
            up = jnp.einsum('th,ehm->etm', x, w_up)
            y_all = jnp.einsum('etm,emh->eth', gp * up, w_down)
            y_sel = y_all[topk_idx, jnp.arange(T)[:, None], :]
            y = (y_sel * topk_w[..., None]).sum(1).reshape(b, s, h)
            p = _leaky(hidden_states @ sw_gate) * (hidden_states @ sw_up) @ sw_down
            y = y + p
            num = jnp.sum(y * p, -1)
            den = jnp.maximum(jnp.linalg.norm(y, axis=-1), EPS_COS) * jnp.maximum(jnp.linalg.norm(p, axis=-1), EPS_COS)
            closs = CONS_ALPHA * jnp.mean(num / den / (1.0 + COS_TEMP))
            return (y, aux_loss + closs)
        key = jax.random.key(seed)
        ks = jax.random.split(key, 12)
        sh = 1.0 / np.sqrt(H)
        sm = 1.0 / np.sqrt(M)
        ssm = 1.0 / np.sqrt(SM)
        sg = 1.0 / np.sqrt(G)
        return {'hidden_states': jax.random.normal(ks[0], (B, S, H), jnp.float32), 'g': jax.random.normal(ks[1], (B, G), jnp.float32), 'wt': jax.random.uniform(ks[2], (E, H), jnp.float32, -sh, sh), 'wg': jax.random.uniform(ks[3], (E, G), jnp.float32, -sg, sg), 'w_gate': jax.random.uniform(ks[4], (E, H, M), jnp.float32, -sh, sh), 'w_up': jax.random.uniform(ks[5], (E, H, M), jnp.float32, -sh, sh), 'w_down': jax.random.uniform(ks[6], (E, M, H), jnp.float32, -sm, sm), 'sw_gate': jax.random.uniform(ks[7], (H, SM), jnp.float32, -sh, sh), 'sw_up': jax.random.uniform(ks[8], (H, SM), jnp.float32, -sh, sh), 'sw_down': jax.random.uniform(ks[9], (SM, H), jnp.float32, -ssm, ssm)}
    _L1_cond_all = _L1_cond_setup()
    _L1_cond_in = {k: v for k, v in _L1_cond_all.items() if k in ('wt', 'wg', 'w_gate', 'w_up', 'w_down', 'sw_gate', 'sw_up', 'sw_down')}
    del _L1_cond_all

    def _L1_ffn_setup():
        import jax, jax.numpy as jnp
        import numpy as np
        S, B, H, F, E, K = (512, 2, 256, 512, 8, 2)

        def _moe_forward(hidden_states, router_w, w1, b1, w2, b2):
            s, b, h = hidden_states.shape
            T = s * b
            x = hidden_states.reshape(T, h)
            logits = jnp.einsum('th,eh->te', x, router_w)
            topk_logits, topk_idx = jax.lax.top_k(logits, K)
            probs = jax.nn.softmax(topk_logits, axis=-1)
            combine = jnp.zeros((T, E), dtype=x.dtype)
            combine = combine.at[jnp.arange(T)[:, None], topk_idx].add(probs.astype(x.dtype))
            hmid = jnp.einsum('th,efh->etf', x, w1) + b1[:, None, :]
            hmid = jax.nn.gelu(hmid, approximate=False)
            y = jnp.einsum('etf,ehf->eth', hmid, w2) + b2[:, None, :]
            out = jnp.einsum('eth,te->th', y, combine)
            return out.reshape(s, b, h)
        key = jax.random.key(seed)
        ks = jax.random.split(key, 6)
        std = 0.02
        return {'hidden_states': jax.random.normal(ks[0], (S, B, H), dtype=jnp.float32), 'router_w': jax.random.normal(ks[1], (E, H), dtype=jnp.float32) * std, 'w1': jax.random.normal(ks[2], (E, F, H), dtype=jnp.float32) * (1.0 / np.sqrt(H)), 'b1': jnp.zeros((E, F), dtype=jnp.float32), 'w2': jax.random.normal(ks[3], (E, H, F), dtype=jnp.float32) * (1.0 / np.sqrt(F)), 'b2': jnp.zeros((E, H), dtype=jnp.float32)}
    _L1_ffn_all = _L1_ffn_setup()
    _L1_ffn_in = {k: v for k, v in _L1_ffn_all.items() if k in ('router_w', 'w1', 'b1', 'w2', 'b2')}
    del _L1_ffn_all

    def _L2_cond_setup():
        import jax, jax.numpy as jnp
        import numpy as np
        DIM = 256
        HEADS = 16
        DIM_HEAD = 64
        SCALE = 8.0

        def ln(x, g, eps=1e-05):
            mean = x.mean(axis=-1, keepdims=True)
            var = ((x - mean) ** 2).mean(axis=-1, keepdims=True)
            return (x - mean) * jax.lax.rsqrt(var + eps) * g

        def l2norm(t):
            n = jnp.maximum(jnp.linalg.norm(t, axis=-1, keepdims=True), 1e-12)
            return t / n

        def rel_pos_bias(n, w0, b0, g0, w1, b1, g1, w2, b2, dtype):
            pos = jnp.arange(-n + 1, n, dtype=dtype)[:, None]
            h = jax.nn.silu(ln(pos @ w0 + b0, g0))
            h = jax.nn.silu(ln(h @ w1 + b1, g1))
            h = h @ w2 + b2
            i = jnp.arange(n)
            idx = i[:, None] - i[None, :] + n - 1
            bias = h[idx]
            return jnp.transpose(bias, (2, 0, 1))
        key = jax.random.key(seed)
        ks = jax.random.split(key, 16)
        b, n = (2, 512)
        inner = HEADS * DIM_HEAD
        s = 0.02
        return {'x': jax.random.normal(ks[0], (b, n, DIM), jnp.float32), 'mask': jnp.ones((b, n), dtype=bool), 'g_norm': jnp.ones((DIM,), jnp.float32), 'Wq': jax.random.normal(ks[1], (DIM, inner), jnp.float32) * s, 'Wkv': jax.random.normal(ks[2], (DIM, 2 * DIM_HEAD), jnp.float32) * s, 'q_scale': jnp.ones((DIM_HEAD,), jnp.float32), 'k_scale': jnp.ones((DIM_HEAD,), jnp.float32), 'null_kv': jax.random.normal(ks[3], (2, DIM_HEAD), jnp.float32), 'null_attn_bias': jax.random.normal(ks[4], (HEADS,), jnp.float32), 'w0': jax.random.normal(ks[5], (1, DIM), jnp.float32) * s, 'b0': jnp.zeros((DIM,), jnp.float32), 'g0': jnp.ones((DIM,), jnp.float32), 'w1': jax.random.normal(ks[6], (DIM, DIM), jnp.float32) * s, 'b1': jnp.zeros((DIM,), jnp.float32), 'g1': jnp.ones((DIM,), jnp.float32), 'w2': jax.random.normal(ks[7], (DIM, HEADS), jnp.float32) * s, 'b2': jnp.zeros((HEADS,), jnp.float32), 'Wout': jax.random.normal(ks[8], (inner, DIM), jnp.float32) * s, 'g_out': jnp.ones((DIM,), jnp.float32)}
    _L2_cond_all = _L2_cond_setup()
    _L2_cond_in = {k: v for k, v in _L2_cond_all.items() if k in ('g_norm', 'Wq', 'Wkv', 'q_scale', 'k_scale', 'null_attn_bias', 'w0', 'b0', 'g0', 'w1', 'b1', 'g1', 'w2', 'b2', 'Wout', 'g_out')}
    del _L2_cond_all

    def _L2_ffn_setup():
        import jax, jax.numpy as jnp
        import numpy as np
        B, T, D = (2, 512, 256)
        DCD = 1024
        RET = 128
        NEXP = 1024
        NKEYS = 64
        H = 4
        KPH = 8
        key = jax.random.key(seed)
        ks = jax.random.split(key, 10)
        s = lambda k, shape, scale: jax.random.normal(k, shape, jnp.float32) * scale
        return {'hidden_states': jax.random.normal(ks[0], (B, T, D), jnp.float32), 'Wg': s(ks[1], (D, DCD), 0.02), 'bg': jnp.zeros((DCD,), jnp.float32), 'Wu': s(ks[2], (D, DCD), 0.02), 'bu': jnp.zeros((DCD,), jnp.float32), 'Wd': s(ks[3], (DCD, D), 0.02), 'bd': jnp.zeros((D,), jnp.float32), 'Wq': s(ks[4], (D, RET * H), 0.02), 'keys': s(ks[5], (H, NKEYS, 2, RET // 2), 0.02), 'down_embed': s(ks[6], (NEXP, D), 0.02), 'up_embed': s(ks[7], (NEXP, D), 0.02)}
    _L2_ffn_all = _L2_ffn_setup()
    _L2_ffn_in = {k: v for k, v in _L2_ffn_all.items() if k in ('Wg', 'bg', 'Wu', 'bu', 'Wd', 'bd', 'Wq', 'keys', 'down_embed', 'up_embed')}
    del _L2_ffn_all

    def _L3_cond_setup():
        import jax, jax.numpy as jnp
        import numpy as np
        B, S, H = (4, 512, 256)
        E = 8
        M = 128
        K = 2
        N_SHARED = 2
        SM = M * N_SHARED
        G = 64
        GE_TEMP = 1.0
        ALPHA = 0.001
        SEQ_AUX = True
        NORM_TOPK = True
        COS_TEMP = 0.78
        CONS_ALPHA = 0.01
        LEAKY_SLOPE = 0.01
        EPS_COS = 1e-08

        def _leaky(x):
            return jnp.where(x >= 0, x, LEAKY_SLOPE * x)

        def _moe_forward(hidden_states, g, wt, wg, w_gate, w_up, w_down, sw_gate, sw_up, sw_down):
            b, s, h = hidden_states.shape
            x = hidden_states.reshape(-1, h)
            T = x.shape[0]
            logits_h = x @ wt.T
            logits_g = g @ wg.T
            logits_g = jnp.repeat(logits_g, s, axis=0)
            logits = (logits_h + logits_g / GE_TEMP) / (1.0 + 1.0 / GE_TEMP)
            scores = jax.nn.softmax(logits, axis=-1)
            topk_w, topk_idx = jax.lax.top_k(scores, K)
            if K > 1 and NORM_TOPK:
                topk_w = topk_w / (topk_w.sum(-1, keepdims=True) + 1e-20)
            onehot = jax.nn.one_hot(topk_idx.reshape(b, s * K), E, dtype=jnp.float32)
            ce = onehot.sum(1) / (s * K / E)
            aux_loss = (ce * scores.reshape(b, s, E).mean(1)).sum(1).mean() * ALPHA
            gp = _leaky(jnp.einsum('th,ehm->etm', x, w_gate))
            up = jnp.einsum('th,ehm->etm', x, w_up)
            y_all = jnp.einsum('etm,emh->eth', gp * up, w_down)
            y_sel = y_all[topk_idx, jnp.arange(T)[:, None], :]
            y = (y_sel * topk_w[..., None]).sum(1).reshape(b, s, h)
            p = _leaky(hidden_states @ sw_gate) * (hidden_states @ sw_up) @ sw_down
            y = y + p
            num = jnp.sum(y * p, -1)
            den = jnp.maximum(jnp.linalg.norm(y, axis=-1), EPS_COS) * jnp.maximum(jnp.linalg.norm(p, axis=-1), EPS_COS)
            closs = CONS_ALPHA * jnp.mean(num / den / (1.0 + COS_TEMP))
            return (y, aux_loss + closs)
        key = jax.random.key(seed)
        ks = jax.random.split(key, 12)
        sh = 1.0 / np.sqrt(H)
        sm = 1.0 / np.sqrt(M)
        ssm = 1.0 / np.sqrt(SM)
        sg = 1.0 / np.sqrt(G)
        return {'hidden_states': jax.random.normal(ks[0], (B, S, H), jnp.float32), 'g': jax.random.normal(ks[1], (B, G), jnp.float32), 'wt': jax.random.uniform(ks[2], (E, H), jnp.float32, -sh, sh), 'wg': jax.random.uniform(ks[3], (E, G), jnp.float32, -sg, sg), 'w_gate': jax.random.uniform(ks[4], (E, H, M), jnp.float32, -sh, sh), 'w_up': jax.random.uniform(ks[5], (E, H, M), jnp.float32, -sh, sh), 'w_down': jax.random.uniform(ks[6], (E, M, H), jnp.float32, -sm, sm), 'sw_gate': jax.random.uniform(ks[7], (H, SM), jnp.float32, -sh, sh), 'sw_up': jax.random.uniform(ks[8], (H, SM), jnp.float32, -sh, sh), 'sw_down': jax.random.uniform(ks[9], (SM, H), jnp.float32, -ssm, ssm)}
    _L3_cond_all = _L3_cond_setup()
    _L3_cond_in = {k: v for k, v in _L3_cond_all.items() if k in ('wt', 'wg', 'w_gate', 'w_up', 'w_down', 'sw_gate', 'sw_up', 'sw_down')}
    del _L3_cond_all

    def _L3_ffn_setup():
        import jax, jax.numpy as jnp
        import numpy as np
        B, T, D, F, E = (2, 256, 256, 1024, 8)
        EPS = 1e-06
        key = jax.random.key(seed)
        k = jax.random.split(key, 5)
        scale = 0.02
        return {'x': jax.random.normal(k[0], (B, T, D), dtype=jnp.float32), 'rms_w': jnp.ones((D,), dtype=jnp.float32), 'gate_w': jax.random.normal(k[1], (E, D), dtype=jnp.float32) * scale, 'W1': jax.random.normal(k[2], (E, D, F), dtype=jnp.float32) * scale, 'b1': jnp.zeros((E, F), dtype=jnp.float32), 'W2': jax.random.normal(k[3], (E, F, D), dtype=jnp.float32) * scale, 'b2': jnp.zeros((E, D), dtype=jnp.float32)}
    _L3_ffn_all = _L3_ffn_setup()
    _L3_ffn_in = {k: v for k, v in _L3_ffn_all.items() if k in ('rms_w', 'gate_w', 'W1', 'b1', 'W2', 'b2')}
    del _L3_ffn_all
    return {'x': x, 'fside_16xSxS_0': fside_16xSxS_0, 'cond_64': cond_64, 'mask_BxS_bk0': mask_BxS_bk0, 'mask_BxS_bf1': mask_BxS_bf1, 'L0_cond_g_in': _L0_cond_in['g_in'], 'L0_cond_null_attn_bias': _L0_cond_in['null_attn_bias'], 'L0_cond_Wq': _L0_cond_in['Wq'], 'L0_cond_Wkv': _L0_cond_in['Wkv'], 'L0_cond_Wo': _L0_cond_in['Wo'], 'L0_cond_g_out': _L0_cond_in['g_out'], 'L0_ffn_Wg': _L0_ffn_in['Wg'], 'L0_ffn_bg': _L0_ffn_in['bg'], 'L0_ffn_W1': _L0_ffn_in['W1'], 'L0_ffn_b1': _L0_ffn_in['b1'], 'L0_ffn_W2': _L0_ffn_in['W2'], 'L0_ffn_b2': _L0_ffn_in['b2'], 'L1_cond_wt': _L1_cond_in['wt'], 'L1_cond_wg': _L1_cond_in['wg'], 'L1_cond_w_gate': _L1_cond_in['w_gate'], 'L1_cond_w_up': _L1_cond_in['w_up'], 'L1_cond_w_down': _L1_cond_in['w_down'], 'L1_cond_sw_gate': _L1_cond_in['sw_gate'], 'L1_cond_sw_up': _L1_cond_in['sw_up'], 'L1_cond_sw_down': _L1_cond_in['sw_down'], 'L1_ffn_router_w': _L1_ffn_in['router_w'], 'L1_ffn_w1': _L1_ffn_in['w1'], 'L1_ffn_b1': _L1_ffn_in['b1'], 'L1_ffn_w2': _L1_ffn_in['w2'], 'L1_ffn_b2': _L1_ffn_in['b2'], 'L2_cond_g_norm': _L2_cond_in['g_norm'], 'L2_cond_Wq': _L2_cond_in['Wq'], 'L2_cond_Wkv': _L2_cond_in['Wkv'], 'L2_cond_q_scale': _L2_cond_in['q_scale'], 'L2_cond_k_scale': _L2_cond_in['k_scale'], 'L2_cond_null_attn_bias': _L2_cond_in['null_attn_bias'], 'L2_cond_w0': _L2_cond_in['w0'], 'L2_cond_b0': _L2_cond_in['b0'], 'L2_cond_g0': _L2_cond_in['g0'], 'L2_cond_w1': _L2_cond_in['w1'], 'L2_cond_b1': _L2_cond_in['b1'], 'L2_cond_g1': _L2_cond_in['g1'], 'L2_cond_w2': _L2_cond_in['w2'], 'L2_cond_b2': _L2_cond_in['b2'], 'L2_cond_Wout': _L2_cond_in['Wout'], 'L2_cond_g_out': _L2_cond_in['g_out'], 'L2_ffn_Wg': _L2_ffn_in['Wg'], 'L2_ffn_bg': _L2_ffn_in['bg'], 'L2_ffn_Wu': _L2_ffn_in['Wu'], 'L2_ffn_bu': _L2_ffn_in['bu'], 'L2_ffn_Wd': _L2_ffn_in['Wd'], 'L2_ffn_bd': _L2_ffn_in['bd'], 'L2_ffn_Wq': _L2_ffn_in['Wq'], 'L2_ffn_keys': _L2_ffn_in['keys'], 'L2_ffn_down_embed': _L2_ffn_in['down_embed'], 'L2_ffn_up_embed': _L2_ffn_in['up_embed'], 'L3_cond_wt': _L3_cond_in['wt'], 'L3_cond_wg': _L3_cond_in['wg'], 'L3_cond_w_gate': _L3_cond_in['w_gate'], 'L3_cond_w_up': _L3_cond_in['w_up'], 'L3_cond_w_down': _L3_cond_in['w_down'], 'L3_cond_sw_gate': _L3_cond_in['sw_gate'], 'L3_cond_sw_up': _L3_cond_in['sw_up'], 'L3_cond_sw_down': _L3_cond_in['sw_down'], 'L3_ffn_rms_w': _L3_ffn_in['rms_w'], 'L3_ffn_gate_w': _L3_ffn_in['gate_w'], 'L3_ffn_W1': _L3_ffn_in['W1'], 'L3_ffn_b1': _L3_ffn_in['b1'], 'L3_ffn_W2': _L3_ffn_in['W2'], 'L3_ffn_b2': _L3_ffn_in['b2']}

def reference(x, fside_16xSxS_0, cond_64, mask_BxS_bk0, mask_BxS_bf1, L0_cond_g_in, L0_cond_null_attn_bias, L0_cond_Wq, L0_cond_Wkv, L0_cond_Wo, L0_cond_g_out, L0_ffn_Wg, L0_ffn_bg, L0_ffn_W1, L0_ffn_b1, L0_ffn_W2, L0_ffn_b2, L1_cond_wt, L1_cond_wg, L1_cond_w_gate, L1_cond_w_up, L1_cond_w_down, L1_cond_sw_gate, L1_cond_sw_up, L1_cond_sw_down, L1_ffn_router_w, L1_ffn_w1, L1_ffn_b1, L1_ffn_w2, L1_ffn_b2, L2_cond_g_norm, L2_cond_Wq, L2_cond_Wkv, L2_cond_q_scale, L2_cond_k_scale, L2_cond_null_attn_bias, L2_cond_w0, L2_cond_b0, L2_cond_g0, L2_cond_w1, L2_cond_b1, L2_cond_g1, L2_cond_w2, L2_cond_b2, L2_cond_Wout, L2_cond_g_out, L2_ffn_Wg, L2_ffn_bg, L2_ffn_Wu, L2_ffn_bu, L2_ffn_Wd, L2_ffn_bd, L2_ffn_Wq, L2_ffn_keys, L2_ffn_down_embed, L2_ffn_up_embed, L3_cond_wt, L3_cond_wg, L3_cond_w_gate, L3_cond_w_up, L3_cond_w_down, L3_cond_sw_gate, L3_cond_sw_up, L3_cond_sw_down, L3_ffn_rms_w, L3_ffn_gate_w, L3_ffn_W1, L3_ffn_b1, L3_ffn_W2, L3_ffn_b2):
    import jax
    import jax.numpy as jnp

    def _L0_cond_ref(x, attn_bias, mask, g_in, null_attn_bias, null_kv, Wq, Wkv, Wo, g_out):
        import jax, jax.numpy as jnp
        import numpy as np
        B, N, DIM, H, DH = (2, 512, 256, 16, 64)
        INNER = H * DH
        EPS = 1e-05

        def layernorm(x, g):
            mean = jnp.mean(x, axis=-1, keepdims=True)
            var = jnp.var(x, axis=-1, keepdims=True)
            return (x - mean) * jax.lax.rsqrt(var + EPS) * g
        b, n, _ = x.shape
        scale = DH ** (-0.5)
        xn = layernorm(x, g_in)
        q = (xn @ Wq).reshape(b, n, H, DH).transpose(0, 2, 1, 3) * scale
        kv = xn @ Wkv
        k, v = (kv[..., :DH], kv[..., DH:])
        nk = jnp.broadcast_to(null_kv[0], (b, 1, DH))
        nv = jnp.broadcast_to(null_kv[1], (b, 1, DH))
        k = jnp.concatenate([nk, k], axis=1)
        v = jnp.concatenate([nv, v], axis=1)
        sim = jnp.einsum('bhid,bjd->bhij', q, k)
        null_col = jnp.broadcast_to(null_attn_bias[:, None, None], (H, n, 1))
        bias = jnp.concatenate([null_col, attn_bias], axis=-1)
        sim = sim + bias
        neg = -jnp.finfo(sim.dtype).max
        j = n + 1
        causal_mask = jnp.triu(jnp.ones((n, j), dtype=bool), k=j - n + 1)
        sim = jnp.where(causal_mask, neg, sim)
        mask_p = jnp.pad(mask, ((0, 0), (1, 0)), constant_values=True)
        sim = jnp.where(mask_p[:, None, None, :], sim, neg)
        attn = jax.nn.softmax(sim, axis=-1)
        out = jnp.einsum('bhij,bjd->bhid', attn, v)
        out = out.transpose(0, 2, 1, 3).reshape(b, n, INNER)
        out = out @ Wo
        return layernorm(out, g_out)

    def _L0_ffn_ref(x, Wg, bg, W1, b1, W2, b2):
        import jax, jax.numpy as jnp
        import numpy as np
        B, S, D, H, E = (8, 512, 256, 1024, 16)
        d = x.shape[-1]
        xf = x.reshape(-1, d)
        n_tok = xf.shape[0]
        n_exp = Wg.shape[1]
        cap = -(-n_tok // n_exp)
        score = jax.nn.softmax(xf @ Wg + bg, axis=-1)
        gate = jnp.max(score, axis=-1)
        idx = jnp.argmax(score, axis=-1)
        onehot = jax.nn.one_hot(idx, n_exp, dtype=jnp.int32)
        pos = jnp.sum((jnp.cumsum(onehot, axis=0) - 1) * onehot, axis=-1)
        keep = pos < cap
        safe_pos = jnp.where(keep, pos, cap - 1)
        buf = jnp.zeros((n_exp, cap, d), x.dtype).at[idx, safe_pos].add(jnp.where(keep[:, None], xf, 0.0))
        h = jax.nn.relu(jnp.einsum('ecd,edh->ech', buf, W1) + b1[:, None, :])
        y = jnp.einsum('ech,ehd->ecd', h, W2) + b2[:, None, :]
        out = y[idx, safe_pos] * gate[:, None]
        out = jnp.where(keep[:, None], out, 0.0)
        return out.reshape(x.shape)

    def _L1_cond_ref(hidden_states, g, wt, wg, w_gate, w_up, w_down, sw_gate, sw_up, sw_down):
        import jax, jax.numpy as jnp
        import numpy as np
        B, S, H = (4, 512, 256)
        E = 8
        M = 128
        K = 2
        N_SHARED = 2
        SM = M * N_SHARED
        G = 64
        GE_TEMP = 1.0
        ALPHA = 0.001
        SEQ_AUX = True
        NORM_TOPK = True
        COS_TEMP = 0.78
        CONS_ALPHA = 0.01
        LEAKY_SLOPE = 0.01
        EPS_COS = 1e-08

        def _leaky(x):
            return jnp.where(x >= 0, x, LEAKY_SLOPE * x)

        def _moe_forward(hidden_states, g, wt, wg, w_gate, w_up, w_down, sw_gate, sw_up, sw_down):
            b, s, h = hidden_states.shape
            x = hidden_states.reshape(-1, h)
            T = x.shape[0]
            logits_h = x @ wt.T
            logits_g = g @ wg.T
            logits_g = jnp.repeat(logits_g, s, axis=0)
            logits = (logits_h + logits_g / GE_TEMP) / (1.0 + 1.0 / GE_TEMP)
            scores = jax.nn.softmax(logits, axis=-1)
            topk_w, topk_idx = jax.lax.top_k(scores, K)
            if K > 1 and NORM_TOPK:
                topk_w = topk_w / (topk_w.sum(-1, keepdims=True) + 1e-20)
            onehot = jax.nn.one_hot(topk_idx.reshape(b, s * K), E, dtype=jnp.float32)
            ce = onehot.sum(1) / (s * K / E)
            aux_loss = (ce * scores.reshape(b, s, E).mean(1)).sum(1).mean() * ALPHA
            gp = _leaky(jnp.einsum('th,ehm->etm', x, w_gate))
            up = jnp.einsum('th,ehm->etm', x, w_up)
            y_all = jnp.einsum('etm,emh->eth', gp * up, w_down)
            y_sel = y_all[topk_idx, jnp.arange(T)[:, None], :]
            y = (y_sel * topk_w[..., None]).sum(1).reshape(b, s, h)
            p = _leaky(hidden_states @ sw_gate) * (hidden_states @ sw_up) @ sw_down
            y = y + p
            num = jnp.sum(y * p, -1)
            den = jnp.maximum(jnp.linalg.norm(y, axis=-1), EPS_COS) * jnp.maximum(jnp.linalg.norm(p, axis=-1), EPS_COS)
            closs = CONS_ALPHA * jnp.mean(num / den / (1.0 + COS_TEMP))
            return (y, aux_loss + closs)
        y, _ = _moe_forward(hidden_states, g, wt, wg, w_gate, w_up, w_down, sw_gate, sw_up, sw_down)
        return y

    def _L1_ffn_ref(hidden_states, router_w, w1, b1, w2, b2):
        import jax, jax.numpy as jnp
        import numpy as np
        S, B, H, F, E, K = (512, 2, 256, 512, 8, 2)

        def _moe_forward(hidden_states, router_w, w1, b1, w2, b2):
            s, b, h = hidden_states.shape
            T = s * b
            x = hidden_states.reshape(T, h)
            logits = jnp.einsum('th,eh->te', x, router_w)
            topk_logits, topk_idx = jax.lax.top_k(logits, K)
            probs = jax.nn.softmax(topk_logits, axis=-1)
            combine = jnp.zeros((T, E), dtype=x.dtype)
            combine = combine.at[jnp.arange(T)[:, None], topk_idx].add(probs.astype(x.dtype))
            hmid = jnp.einsum('th,efh->etf', x, w1) + b1[:, None, :]
            hmid = jax.nn.gelu(hmid, approximate=False)
            y = jnp.einsum('etf,ehf->eth', hmid, w2) + b2[:, None, :]
            out = jnp.einsum('eth,te->th', y, combine)
            return out.reshape(s, b, h)
        return _moe_forward(hidden_states, router_w, w1, b1, w2, b2)

    def _L2_cond_ref(x, mask, g_norm, Wq, Wkv, q_scale, k_scale, null_kv, null_attn_bias, w0, b0, g0, w1, b1, g1, w2, b2, Wout, g_out):
        import jax, jax.numpy as jnp
        import numpy as np
        DIM = 256
        HEADS = 16
        DIM_HEAD = 64
        SCALE = 8.0

        def ln(x, g, eps=1e-05):
            mean = x.mean(axis=-1, keepdims=True)
            var = ((x - mean) ** 2).mean(axis=-1, keepdims=True)
            return (x - mean) * jax.lax.rsqrt(var + eps) * g

        def l2norm(t):
            n = jnp.maximum(jnp.linalg.norm(t, axis=-1, keepdims=True), 1e-12)
            return t / n

        def rel_pos_bias(n, w0, b0, g0, w1, b1, g1, w2, b2, dtype):
            pos = jnp.arange(-n + 1, n, dtype=dtype)[:, None]
            h = jax.nn.silu(ln(pos @ w0 + b0, g0))
            h = jax.nn.silu(ln(h @ w1 + b1, g1))
            h = h @ w2 + b2
            i = jnp.arange(n)
            idx = i[:, None] - i[None, :] + n - 1
            bias = h[idx]
            return jnp.transpose(bias, (2, 0, 1))
        b, n, _ = x.shape
        xn = ln(x, g_norm)
        q = (xn @ Wq).reshape(b, n, HEADS, DIM_HEAD).transpose(0, 2, 1, 3)
        kv = xn @ Wkv
        k, v = (kv[..., :DIM_HEAD], kv[..., DIM_HEAD:])
        nk = jnp.broadcast_to(null_kv[0], (b, 1, DIM_HEAD))
        nv = jnp.broadcast_to(null_kv[1], (b, 1, DIM_HEAD))
        k = jnp.concatenate([nk, k], axis=1)
        v = jnp.concatenate([nv, v], axis=1)
        q = l2norm(q) * q_scale
        k = l2norm(k) * k_scale
        sim = jnp.einsum('bhid,bjd->bhij', q, k) * SCALE
        bias = rel_pos_bias(n, w0, b0, g0, w1, b1, g1, w2, b2, q.dtype)
        null_bias = jnp.broadcast_to(null_attn_bias[:, None, None], (HEADS, n, 1))
        attn_bias = jnp.concatenate([null_bias, bias], axis=-1)
        sim = sim + attn_bias
        neg = -jnp.finfo(sim.dtype).max
        causal = jnp.triu(jnp.ones((n, n + 1), dtype=bool), k=2)
        sim = jnp.where(causal, neg, sim)
        m = jnp.pad(mask, ((0, 0), (1, 0)), constant_values=True)[:, None, None, :]
        sim = jnp.where(m, sim, neg)
        attn = jax.nn.softmax(sim, axis=-1)
        out = jnp.einsum('bhij,bjd->bhid', attn, v)
        out = out.transpose(0, 2, 1, 3).reshape(b, n, HEADS * DIM_HEAD)
        return ln(out @ Wout, g_out)

    def _L2_ffn_ref(hidden_states, Wg, bg, Wu, bu, Wd, bd, Wq, keys, down_embed, up_embed):
        import jax, jax.numpy as jnp
        import numpy as np
        B, T, D = (2, 512, 256)
        DCD = 1024
        RET = 128
        NEXP = 1024
        NKEYS = 64
        H = 4
        KPH = 8
        b, t, d = hidden_states.shape
        q = (hidden_states @ Wq).reshape(b, t, 2, H, RET // 2)
        sim = jnp.einsum('btphn,hkpn->pbthk', q, keys)
        sc, ix = jax.lax.top_k(sim, KPH)
        sx, sy = (sc[0], sc[1])
        ixx, ixy = (ix[0], ix[1])
        all_sc = (sx[..., :, None] + sy[..., None, :]).reshape(b, t, H, KPH * KPH)
        all_ix = (ixx[..., :, None] * NKEYS + ixy[..., None, :]).reshape(b, t, H, KPH * KPH)
        scores, pk = jax.lax.top_k(all_sc, KPH)
        idx = jnp.take_along_axis(all_ix, pk, axis=-1)
        de = down_embed[idx]
        ue = up_embed[idx]
        w = jnp.einsum('btd,bthkd->bthk', hidden_states, de)
        w = jax.nn.silu(w) * jax.nn.softmax(scores, axis=-1)
        experts_states = jnp.einsum('bthk,bthkd->btd', w, ue)
        mlp = jax.nn.silu(hidden_states @ Wg + bg) * (hidden_states @ Wu + bu) @ Wd + bd
        return mlp + experts_states

    def _L3_cond_ref(hidden_states, g, wt, wg, w_gate, w_up, w_down, sw_gate, sw_up, sw_down):
        import jax, jax.numpy as jnp
        import numpy as np
        B, S, H = (4, 512, 256)
        E = 8
        M = 128
        K = 2
        N_SHARED = 2
        SM = M * N_SHARED
        G = 64
        GE_TEMP = 1.0
        ALPHA = 0.001
        SEQ_AUX = True
        NORM_TOPK = True
        COS_TEMP = 0.78
        CONS_ALPHA = 0.01
        LEAKY_SLOPE = 0.01
        EPS_COS = 1e-08

        def _leaky(x):
            return jnp.where(x >= 0, x, LEAKY_SLOPE * x)

        def _moe_forward(hidden_states, g, wt, wg, w_gate, w_up, w_down, sw_gate, sw_up, sw_down):
            b, s, h = hidden_states.shape
            x = hidden_states.reshape(-1, h)
            T = x.shape[0]
            logits_h = x @ wt.T
            logits_g = g @ wg.T
            logits_g = jnp.repeat(logits_g, s, axis=0)
            logits = (logits_h + logits_g / GE_TEMP) / (1.0 + 1.0 / GE_TEMP)
            scores = jax.nn.softmax(logits, axis=-1)
            topk_w, topk_idx = jax.lax.top_k(scores, K)
            if K > 1 and NORM_TOPK:
                topk_w = topk_w / (topk_w.sum(-1, keepdims=True) + 1e-20)
            onehot = jax.nn.one_hot(topk_idx.reshape(b, s * K), E, dtype=jnp.float32)
            ce = onehot.sum(1) / (s * K / E)
            aux_loss = (ce * scores.reshape(b, s, E).mean(1)).sum(1).mean() * ALPHA
            gp = _leaky(jnp.einsum('th,ehm->etm', x, w_gate))
            up = jnp.einsum('th,ehm->etm', x, w_up)
            y_all = jnp.einsum('etm,emh->eth', gp * up, w_down)
            y_sel = y_all[topk_idx, jnp.arange(T)[:, None], :]
            y = (y_sel * topk_w[..., None]).sum(1).reshape(b, s, h)
            p = _leaky(hidden_states @ sw_gate) * (hidden_states @ sw_up) @ sw_down
            y = y + p
            num = jnp.sum(y * p, -1)
            den = jnp.maximum(jnp.linalg.norm(y, axis=-1), EPS_COS) * jnp.maximum(jnp.linalg.norm(p, axis=-1), EPS_COS)
            closs = CONS_ALPHA * jnp.mean(num / den / (1.0 + COS_TEMP))
            return (y, aux_loss + closs)
        y, _ = _moe_forward(hidden_states, g, wt, wg, w_gate, w_up, w_down, sw_gate, sw_up, sw_down)
        return y

    def _L3_ffn_ref(x, rms_w, gate_w, W1, b1, W2, b2):
        import jax, jax.numpy as jnp
        import numpy as np
        B, T, D, F, E = (2, 256, 256, 1024, 8)
        EPS = 1e-06
        ms = jnp.mean(x * x, axis=-1, keepdims=True)
        xn = x * jax.lax.rsqrt(ms + EPS) * rms_w
        logits = jnp.einsum('btd,ed->bte', xn, gate_w)
        scores = jax.nn.softmax(logits, axis=-1)
        top1_idx = jnp.argmax(scores, axis=-1)
        top1_score = jnp.max(scores, axis=-1)
        out = jnp.zeros_like(xn)
        for e in range(E):
            h = jax.nn.silu(jnp.einsum('btd,df->btf', xn, W1[e]) + b1[e])
            ye = jnp.einsum('btf,fd->btd', h, W2[e]) + b2[e]
            out = jnp.where((top1_idx == e)[..., None], ye, out)
        return out * top1_score[..., None]
    x = x + _L0_ffn_ref(_L0_cond_ref(x, fside_16xSxS_0, mask_BxS_bk0, L0_cond_g_in, L0_cond_null_attn_bias, cond_64, L0_cond_Wq, L0_cond_Wkv, L0_cond_Wo, L0_cond_g_out), L0_ffn_Wg, L0_ffn_bg, L0_ffn_W1, L0_ffn_b1, L0_ffn_W2, L0_ffn_b2)
    x = x + _L1_ffn_ref(_L1_cond_ref(x, cond_64, L1_cond_wt, L1_cond_wg, L1_cond_w_gate, L1_cond_w_up, L1_cond_w_down, L1_cond_sw_gate, L1_cond_sw_up, L1_cond_sw_down), L1_ffn_router_w, L1_ffn_w1, L1_ffn_b1, L1_ffn_w2, L1_ffn_b2)
    x = x + _L2_ffn_ref(_L2_cond_ref(x, mask_BxS_bf1, L2_cond_g_norm, L2_cond_Wq, L2_cond_Wkv, L2_cond_q_scale, L2_cond_k_scale, cond_64, L2_cond_null_attn_bias, L2_cond_w0, L2_cond_b0, L2_cond_g0, L2_cond_w1, L2_cond_b1, L2_cond_g1, L2_cond_w2, L2_cond_b2, L2_cond_Wout, L2_cond_g_out), L2_ffn_Wg, L2_ffn_bg, L2_ffn_Wu, L2_ffn_bu, L2_ffn_Wd, L2_ffn_bd, L2_ffn_Wq, L2_ffn_keys, L2_ffn_down_embed, L2_ffn_up_embed)
    x = x + _L3_ffn_ref(_L3_cond_ref(x, cond_64, L3_cond_wt, L3_cond_wg, L3_cond_w_gate, L3_cond_w_up, L3_cond_w_down, L3_cond_sw_gate, L3_cond_sw_up, L3_cond_sw_down), L3_ffn_rms_w, L3_ffn_gate_w, L3_ffn_W1, L3_ffn_b1, L3_ffn_W2, L3_ffn_b2)
    return x

_drawn_inputs = setup_inputs


def setup_inputs(seed=0):
    import zlib

    import numpy as np

    out = dict(_drawn_inputs(seed))
    spreads = {'L0_cond_g_in': (1.0, 0.2),
     'L0_cond_g_out': (1.0, 0.2),
     'L0_ffn_bg': (0.0, 0.354),
     'L0_ffn_b1': (0.0, 0.694),
     'L0_ffn_b2': (0.0, 0.549),
     'L1_ffn_b1': (0.0, 0.1),
     'L1_ffn_b2': (0.0, 0.1),
     'L2_cond_g_norm': (1.0, 0.6),
     'L2_cond_q_scale': (1.0, 0.6),
     'L2_cond_k_scale': (1.0, 0.6),
     'L2_cond_b0': (0.0, 0.8),
     'L2_cond_g0': (1.0, 0.6),
     'L2_cond_b1': (0.0, 0.8),
     'L2_cond_g1': (1.0, 0.6),
     'L2_cond_b2': (0.0, 0.8),
     'L2_cond_g_out': (1.0, 0.6),
     'L2_ffn_bg': (0.0, 0.634),
     'L2_ffn_bu': (0.0, 0.623),
     'L2_ffn_bd': (0.0, 0.1),
     'L3_ffn_rms_w': (1.0, 0.6),
     'L3_ffn_b1': (0.0, 0.8),
     'L3_ffn_b2': (0.0, 0.416)}
    factors = {'L2_cond_null_attn_bias': 5.538,
     'L2_cond_w0': 8.0,
     'L2_cond_w1': 8.0,
     'L2_cond_w2': 8.0,
     'L2_ffn_Wq': 8.0,
     'L2_ffn_keys': 8.0,
     'L2_ffn_down_embed': 4.96,
     'L2_ffn_up_embed': 4.619,
     'L3_cond_wt': 3.047,
     'L3_cond_wg': 2.906,
     'L3_cond_w_gate': 2.726,
     'L3_ffn_W1': 2.7}
    for name, (base, spread) in spreads.items():
        noise = np.random.default_rng([zlib.crc32(name.encode()), seed]).standard_normal(out[name].shape)
        drawn = base * np.exp(spread * noise) if base else spread * noise
        out[name] = jnp.asarray(drawn.astype(out[name].dtype))
    for name, factor in factors.items():
        out[name] = (out[name] * factor).astype(out[name].dtype)
    return out
```

```python
from contextlib import ExitStack

import concourse.bass as bass
from concourse import mybir

F32 = mybir.dt.float32
BF16 = mybir.dt.bfloat16
U8 = mybir.dt.uint8
I32 = mybir.dt.int32
U32 = mybir.dt.uint32
ALU = mybir.AluOpType
ACT = mybir.ActivationFunctionType
AX = mybir.AxisListType.X

P = 128
B, S, D = 2, 1024, 256
T = B * S
NT = T // P
TB = S // P
KD = D // P
H, DH = 16, 64
NP = H // 2
INNER = H * DH
LN_EPS = 1e-5
RMS_EPS = 1e-6
NORM_FLOOR = 1e-12
MASKED = -1e38
BANK = 512


class Steps:

    def __init__(self, sem, names, ahead=4):
        self.sem, self.names, self.ahead = sem, names.split(), ahead

    def open(self, eng):
        eng.sem_inc(self.sem, self.ahead * len(self.names))

    def after(self, name, t):
        return (t + self.ahead) * len(self.names) + self.names.index(name) + 1


class Phase:

    def __init__(self, nc, pool):
        self.nc, self.pool, self.used, self.stack = nc, pool, 0, ExitStack()

    def __enter__(self):
        return self

    def sb(self, name, shape, dt=F32):
        return self.stack.enter_context(self.nc.sbuf_tensor(self.name(name), shape, dt))

    def ps(self, name, shape, dt=F32):
        return self.stack.enter_context(self.nc.psum_tensor(self.name(name), shape, dt))

    def name(self, name):
        self.pool["n"] += 1
        return f"{name}_{self.pool['n']}"

    def sem(self):
        self.used += 1
        return self.pool["sems"][self.used - 1]

    def steps(self, names, ahead=4):
        return Steps(self.sem(), names, ahead)

    def __exit__(self, kind, value, tb):
        self.stack.close()
        if kind is None:
            first = self.pool["first"]
            self.nc.all_engine_barrier(sems_to_clear=range(first, first + self.used))
        return False


def tiles(eng, n, body):
    with eng.Fori(0, n // 2) as i:
        body(i * 2, 0)
        body(i * 2 + 1, 1)


def skewed(eng, n, a, b, b_first=False):

    def pair(i, j):
        steps = [lambda: a(i, (j + 1) % 2), lambda: b(i - 1, j % 2)]
        for step in reversed(steps) if b_first else steps:
            step()

    a(0, 0)
    if n > 2:
        with eng.Fori(0, n // 2 - 1) as i:
            pair(i * 2 + 1, 0)
            pair(i * 2 + 2, 1)
    pair(n - 1, 0)
    b(n - 1, 1)


def row(ap, width, offset=0):
    return bass.AP(ap.tensor, ap.offset + offset, [[0, P], [1, width]])


def bc(ap, shape):
    return ap.unsqueeze(2).to_broadcast(shape)


def setup(nc, pool, c, x_in):
    with Phase(nc, pool) as ph:
        loaded, zeroed = ph.sem(), ph.sem()
        made = ph.sem()
        block = ph.stack.enter_context(nc.Block())

        @block.sync
        def _(sp):
            sp.dma_start(c["x"][:], x_in.rearrange("b (t p) d -> p (b t) d", p=P)).then_inc(loaded, 16)
            sp.wait_ge(loaded, 16)

        @block.gpsimd
        def _(pool_eng):
            pool_eng.memset(c["ident"][:], 0.0).then_inc(zeroed, 1)
            pool_eng.memset(c["ones"][:], 1.0).then_inc(zeroed, 1)
            pool_eng.memset(c["eps"][:, 0:1], LN_EPS).then_inc(zeroed, 1)
            pool_eng.memset(c["eps"][:, 1:2], RMS_EPS).then_inc(zeroed, 1)
            pool_eng.wait_ge(zeroed, 4)
            pool_eng.affine_select(out=c["ident"][:], in_=c["ident"][:], compare_op=ALU.not_equal, fill=1.0,
                                   base=0, pattern=[[-1, P]], channel_multiplier=1).then_inc(made, 1)
            pool_eng.wait_ge(made, 1)
            pool_eng.tensor_copy(c["ident16"][:], c["ident"][:]).then_inc(made, 1)


def qkv_phase(nc, pool, c, att, g, wq, wkv, null_bias, q_scale=None, k_scale=None):
    normal = q_scale is not None
    HN = H + 1
    QK = INNER + DH
    with Phase(nc, pool) as ph:
        w = ph.sb("w", [P, KD, INNER + 2 * DH])
        gt = ph.sb("gt", [P, D])
        table = ph.sb("table", [P, QK])
        nb_row = ph.sb("nb_row", [P, H])
        qnk = ph.sb("qnk", [P, INNER])
        qnk_sum = ph.sb("qnk_sum", [P, H])
        stats = ph.sb("stats", [P, 2, 6])
        mv = ph.sb("mv", [P, 2, 2])
        sd = ph.sb("sd", [P, 2, 1])
        rstd = ph.sb("rstd", [P, 2, 1])
        xc = ph.sb("xc", [P, 2, D])
        xn = ph.sb("xn", [P, 2, D])
        xnT = ph.sb("xnT", [P, 2, KD, P])
        qs = ph.sb("qs", [P, 2, INNER + 2 * DH])
        if normal:
            sq = ph.sb("sq", [P, QK])
            qn = ph.sb("qn", [P, QK])
            n2 = ph.sb("n2", [P, HN])
            nr = ph.sb("nr", [P, HN])
            rn = ph.sb("rn", [P, HN])
        ps_x = ph.ps("ps_x", [P, 2, BANK])
        ps_q = ph.ps("ps_q", [P, 3 * BANK])
        ps_t = ph.ps("ps_t", [P, 3 * BANK])

        weights, tabled = ph.sem(), ph.sem()
        dve_a = ph.steps("stats waited moments rstd centred xn")
        act_a = ph.steps("sd xnT")
        pe_a = ph.steps("xT qkv")
        dve_b = ph.steps("sumsq floor rn qn qs kdup nullsum null kT" if normal else "qs kdup nullsum null kT")
        gp_b = ph.steps("qnk")
        act_b = ph.steps("v sq norm qT" if normal else "v qT")
        pe_b = ph.steps("qT")
        block = ph.stack.enter_context(nc.Block())

        @block.sync
        def _(sp):
            sp.dma_start(w[:, :, 0:INNER], wq.rearrange("(k p) n -> p k n", p=P)).then_inc(weights, 16)
            sp.dma_start(w[:, :, INNER:], wkv.rearrange("(k p) n -> p k n", p=P)).then_inc(weights, 16)
            sp.dma_start(gt[:], row(g, D)).then_inc(weights, 16)
            sp.dma_start(nb_row[:], row(null_bias, H)).then_inc(weights, 16)
            if normal:
                sp.dma_start(table[:, 0:INNER].rearrange("p (h n) -> p h n", h=H),
                             bass.AP(q_scale.tensor, q_scale.offset, [[0, P], [0, H], [1, DH]])).then_inc(weights, 16)
                sp.dma_start(table[:, INNER:QK], row(k_scale, DH)).then_inc(weights, 16)

        n_loads = 16 * (6 if normal else 4)

        @block.vector
        def _(dve):
            dve_a.open(dve)
            dve_b.open(dve)
            dve.wait_ge(weights, n_loads)
            if normal:
                dve.tensor_scalar(table[:, 0:INNER], table[:, 0:INNER], 8.0, None, ALU.mult).then_inc(tabled, 1)
            else:
                dve.memset(table[:, 0:INNER], DH ** -0.5).then_inc(tabled, 1)
                dve.memset(table[:, INNER:QK], 1.0).then_inc(tabled, 1)
            dve.wait_ge(tabled, 1 if normal else 2)

            def a(t, u):
                x_t = c["x"][:, bass.ds(t, 1), :].rearrange("p a d -> p (a d)")
                dve.bn_stats(stats[:, u, :], x_t).then_inc(dve_a.sem, 1)
                dve.wait_ge(dve_a.sem, dve_a.after("stats", t))
                dve.sem_inc(dve_a.sem, 1)
                dve.bn_aggr(mv[:, u, :], stats[:, u, :]).then_inc(dve_a.sem, 1)
                dve.wait_ge(act_a.sem, act_a.after("sd", t))
                dve.reciprocal(rstd[:, u, :], sd[:, u, :]).then_inc(dve_a.sem, 1)
                dve.wait_ge(dve_a.sem, dve_a.after("rstd", t))
                dve.tensor_scalar(xc[:, u, :], x_t, mv[:, u, 0:1], rstd[:, u, 0:1], ALU.subtract,
                                  ALU.mult).then_inc(dve_a.sem, 1)
                dve.wait_ge(dve_a.sem, dve_a.after("centred", t))
                dve.wait_ge(pe_a.sem, pe_a.after("xT", t - 2))
                dve.tensor_tensor(xn[:, u, :], xc[:, u, :], gt[:], ALU.mult).then_inc(dve_a.sem, 1)

            def b(t, u):
                if normal:
                    dve.wait_ge(act_b.sem, act_b.after("sq", t))
                    dve.tensor_reduce(n2[:], sq[:].rearrange("p (h n) -> p h n", n=DH), AX,
                                      ALU.add).then_inc(dve_b.sem, 1)
                    dve.wait_ge(act_b.sem, act_b.after("norm", t))
                    dve.tensor_scalar(nr[:], nr[:], NORM_FLOOR, None, ALU.max).then_inc(dve_b.sem, 1)
                    dve.wait_ge(dve_b.sem, dve_b.after("floor", t))
                    dve.reciprocal(rn[:], nr[:]).then_inc(dve_b.sem, 1)
                    dve.wait_ge(dve_b.sem, dve_b.after("rn", t))
                    dve.tensor_tensor(qn[:].rearrange("p (h n) -> p h n", n=DH),
                                      ps_q[:, 0:QK].rearrange("p (h n) -> p h n", n=DH),
                                      bc(rn[:], [P, HN, DH]), ALU.mult).then_inc(dve_b.sem, 1)
                    dve.wait_ge(dve_b.sem, dve_b.after("qn", t))
                dve.wait_ge(pe_a.sem, pe_a.after("qkv", t))
                dve.wait_ge(act_b.sem, act_b.after("v", t))
                dve.wait_ge(pe_b.sem, pe_b.after("qT", t - 2))
                dve.wait_ge(gp_b.sem, gp_b.after("qnk", t - 2))
                dve.tensor_tensor(qs[:, u, 0:QK], qn[:] if normal else ps_q[:, 0:QK], table[:],
                                  ALU.mult).then_inc(dve_b.sem, 1)
                dve.wait_ge(dve_b.sem, dve_b.after("qs", t))
                dve.tensor_copy(qs[:, u, QK:QK + DH], qs[:, u, INNER:QK]).then_inc(dve_b.sem, 1)
                dve.wait_ge(gp_b.sem, gp_b.after("qnk", t))
                dve.tensor_reduce(qnk_sum[:], qnk[:].rearrange("p (h n) -> p h n", n=DH), AX,
                                  ALU.add).then_inc(dve_b.sem, 1)
                dve.wait_ge(dve_b.sem, dve_b.after("nullsum", t))
                dve.scalar_tensor_tensor(att["nsn"][:, bass.ds(t, 1), :].rearrange("p a h -> p (a h)"), qnk_sum[:], -1.0,
                                         nb_row[:], ALU.mult, ALU.subtract).then_inc(dve_b.sem, 1)
                dve.wait_ge(pe_b.sem, pe_b.after("qT", t))
                dve.tensor_copy(att["kT"][:, bass.ds(t * P, P)], ps_t[:, INNER:INNER + P]).then_inc(dve_b.sem, 1)

            skewed(dve, NT, a, b)

        @block.gpsimd
        def _(gp):
            gp_b.open(gp)

            def null_products(t, u):
                gp.wait_ge(dve_b.sem, dve_b.after("qs", t))
                gp.wait_ge(dve_b.sem, dve_b.after("nullsum", t - 1))
                gp.tensor_tensor(qnk[:].rearrange("p (h n) -> p h n", n=DH),
                                 qs[:, u, 0:INNER].rearrange("p (h n) -> p h n", n=DH),
                                 att["nk"][:].unsqueeze(1).to_broadcast([P, H, DH]), ALU.mult).then_inc(gp_b.sem, 1)

            tiles(gp, NT, null_products)

        @block.scalar
        def _(act):
            act_a.open(act)
            act_b.open(act)

            def a(t, u):
                act.wait_ge(dve_a.sem, dve_a.after("moments", t))
                act.activation(sd[:, u, :], mv[:, u, 1:2], ACT.Sqrt, bias=c["eps"][:, 0:1]).then_inc(act_a.sem, 1)
                act.wait_ge(pe_a.sem, pe_a.after("xT", t))
                act.wait_ge(pe_a.sem, pe_a.after("qkv", t - 2))
                act.activation(xnT[:, u].rearrange("p k n -> p (k n)"), ps_x[:, u, 0:D], ACT.Copy).then_inc(act_a.sem, 1)

            def b(t, u):
                act.wait_ge(pe_a.sem, pe_a.after("qkv", t))
                act.activation(att["v"][:, bass.ds(t, 1), :], ps_q[:, QK:QK + DH].unsqueeze(1), ACT.Copy).then_inc(act_b.sem, 1)
                if normal:
                    act.wait_ge(dve_b.sem, dve_b.after("sumsq", t - 1))
                    act.activation(sq[:], ps_q[:, 0:QK], ACT.Square).then_inc(act_b.sem, 1)
                if normal:
                    act.wait_ge(dve_b.sem, dve_b.after("sumsq", t))
                    act.activation(nr[:], n2[:], ACT.Sqrt).then_inc(act_b.sem, 1)
                act.wait_ge(pe_b.sem, pe_b.after("qT", t))
                act.activation(att["qo"][:, bass.ds(t, 1)].rearrange("p a q n -> p (a q n)"), ps_t[:, 0:INNER],
                               ACT.Copy).then_inc(act_b.sem, 1)

            skewed(act, NT, a, b)

        @block.tensor
        def _(pe):
            pe_a.open(pe)
            pe_b.open(pe)
            pe.wait_ge(weights, n_loads)

            def a(t, u):
                pe.wait_ge(dve_a.sem, dve_a.after("xn", t))
                pe.wait_ge(act_a.sem, act_a.after("xnT", t - 2))
                for k in range(KD):
                    ins = pe.transpose(ps_x[:, u, k * P:(k + 1) * P], xn[:, u, k * P:(k + 1) * P], c["ident"][:])
                ins.then_inc(pe_a.sem, 1)
                pe.wait_ge(act_a.sem, act_a.after("xnT", t))
                pe.wait_ge(dve_b.sem, dve_b.after("qs", t - 1))
                pe.wait_ge(act_b.sem, act_b.after("v", t - 1))
                for lo in range(0, INNER + 2 * DH, BANK):
                    hi = min(lo + BANK, INNER + 2 * DH)
                    for k in range(KD):
                        ins = pe.matmul(ps_q[:, lo:hi], xnT[:, u, k, :], w[:, k, lo:hi], start=(k == 0),
                                        stop=(k == KD - 1))
                ins.then_inc(pe_a.sem, 1)

            def b(t, u):
                pe.wait_ge(dve_b.sem, dve_b.after("kdup", t))
                pe.wait_ge(dve_b.sem, dve_b.after("kT", t - 1))
                pe.wait_ge(act_b.sem, act_b.after("qT", t - 1))
                for k in range(NP + 1):
                    ins = pe.transpose(ps_t[:, k * P:(k + 1) * P], qs[:, u, k * P:(k + 1) * P], c["ident"][:])
                ins.then_inc(pe_b.sem, 1)

            skewed(pe, NT, a, b)


def null_phase(nc, pool, c, att, null_kv, mask, k_scale=None):
    with Phase(nc, pool) as ph:
        m8 = ph.sb("m8", [P, B, S], U8)
        raw = ph.sb("raw", [P, DH])
        ks = ph.sb("ks", [P, DH])
        sq = ph.sb("sq", [P, DH])
        nrm = ph.sb("nrm", [P, 4])
        loaded, masked, step, rooted, triangle = (ph.sem() for _ in range(5))
        block = ph.stack.enter_context(nc.Block())
        normal = k_scale is not None
        n_loads = 16 * (4 if normal else 3)

        @block.sync
        def _(sp):
            sp.dma_start(m8[:].rearrange("p b s -> p (b s)"), row(mask, B * S)).then_inc(loaded, 16)
            sp.dma_start(raw[:], row(null_kv, DH)).then_inc(loaded, 16)
            sp.dma_start(att["nv"][:], row(null_kv, DH, DH)).then_inc(loaded, 16)
            if normal:
                sp.dma_start(ks[:], row(k_scale, DH)).then_inc(loaded, 16)
            sp.wait_ge(loaded, n_loads)

        @block.vector
        def _(dve):
            dve.wait_ge(loaded, n_loads)
            dve.tensor_scalar(att["km"][:], m8[:], -1.0, -MASKED, ALU.add, ALU.mult).then_inc(masked, 1)
            if normal:
                dve.tensor_tensor(sq[:], raw[:], raw[:], ALU.mult).then_inc(step, 1)
                dve.wait_ge(step, 1)
                dve.tensor_reduce(nrm[:, 0:1], sq[:], AX, ALU.add).then_inc(step, 1)
                dve.wait_ge(rooted, 1)
                dve.tensor_scalar(nrm[:, 2:3], nrm[:, 1:2], NORM_FLOOR, None, ALU.max).then_inc(step, 1)
                dve.wait_ge(step, 3)
                dve.reciprocal(nrm[:, 3:4], nrm[:, 2:3]).then_inc(step, 1)
                dve.wait_ge(step, 4)
                dve.scalar_tensor_tensor(att["nk"][:], raw[:], nrm[:, 3:4], ks[:], ALU.mult, ALU.mult).then_inc(step, 1)
            else:
                dve.tensor_copy(att["nk"][:], raw[:]).then_inc(step, 1)

        @block.scalar
        def _(act):
            if normal:
                act.wait_ge(step, 2)
                act.activation(nrm[:, 1:2], nrm[:, 0:1], ACT.Sqrt).then_inc(rooted, 1)

        @block.gpsimd
        def _(gp):
            gp.wait_ge(masked, 1)
            gp.affine_select(out=att["dm"][:].rearrange("p (m j) -> p m j", j=P),
                             in_=att["km"][:].rearrange("p b (m j) -> p (b m) j", j=P), compare_op=ALU.is_ge,
                             fill=MASKED, base=0, pattern=[[0, NT], [-1, P]], channel_multiplier=1).then_inc(triangle, 1)
            gp.wait_ge(triangle, 1)


def core_phase(nc, pool, c, att, bias_src, bias_made=None):
    with Phase(nc, pool) as ph:
        stage = ph.sb("stage", [P, 2, B, P])
        bias = ph.sb("bias", [P, 2, S])
        prob = ph.sb("prob", [P, 2, S])
        pT = ph.sb("pT", [P, 2, S])
        nsn = ph.sb("nsn", [P, 4])
        nmax = ph.sb("nmax", [P, 4])
        rsum = ph.sb("rsum", [P, 4])
        p0 = ph.sb("p0", [P, 4])
        tot = ph.sb("tot", [P, 4])
        rinv = ph.sb("rinv", [P, 4])
        ot = ph.sb("ot", [P, 4, DH])
        ps_s = ph.ps("ps_s", [P, 2, 2 * BANK])
        ps_pt = ph.ps("ps_pt", [P, 2, BANK])
        ps_o = ph.ps("ps_o", [P, 2, BANK])

        zeroed = ph.sem()
        bias_in = [ph.sem(), ph.sem()]
        gp_s = ph.steps("even odd")
        pe_a = ph.steps("scores", 8)
        dve_a = ph.steps("null waited neg", 8)
        act_a = ph.steps("exp p0", 8)
        pe_b = ph.steps("t0 t1 pv", 8)
        act_b = ph.steps("pt0", 8)
        dve_b = ph.steps("pt1", 8)
        fin = ph.steps("tot rinv ot0 ot1 o0 o1", 8)
        block = ph.stack.enter_context(nc.Block())

        def units(eng, qt, a, b, b_first=False, pair=None):

            def both(p_a, v_a, p_b, v_b):
                if b_first:
                    b(qt, p_b, v_b)
                a(qt, p_a, v_a)
                if not b_first:
                    b(qt, p_b, v_b)

            a(qt, 0, 0)
            with eng.Fori(0, NP - 1) as p:
                for v in range(3):
                    both(p, v + 1, p, v)
                both(p + 1, 0, p, 3)
            for v in range(3):
                both(NP - 1, v + 1, NP - 1, v)
            b(qt, NP - 1, 3)

        def unit(qt, p, v):
            return (p + qt * NP) * 4 + v

        @block.sync
        def _(sp):
            if bias_made is not None:
                sp.wait_ge(bias_made, 16)
            for qt in range(TB):
                with sp.Fori(0, NP) as p:
                    for hp in range(2):
                        sp.wait_ge(dve_a.sem, dve_a.after("neg", unit(qt, p, 2 * hp + 1) - 4))
                        sp.dma_start(bias[:, hp, 0:(qt + 1) * P], bias_src(p * 2 + hp, qt)).then_inc(bias_in[hp], 16)

        @block.gpsimd
        def _(gp):
            gp_s.open(gp)
            gp.memset(stage[:], 0.0).then_inc(zeroed, 1)
            gp.wait_ge(zeroed, 1)
            for qt in range(TB):
                with gp.Fori(0, NP) as p:
                    for hp in range(2):
                        gp.wait_ge(pe_a.sem, pe_a.after("scores", unit(qt, p, 2 * hp + 1) - 4))
                        half = slice(hp * DH, (hp + 1) * DH)
                        gp.tensor_copy(stage[half, hp],
                                       att["qo"][half, qt:NT:TB, bass.ds(p, 1), :].rearrange("d b a n -> d b (a n)")
                                       ).then_inc(gp_s.sem, 1)

        @block.tensor
        def _(pe):
            pe_a.open(pe)
            pe_b.open(pe)

            def a(qt, p, v):
                n, hp, b, u = unit(qt, p, v), v // 2, v % 2, v % 2
                W = (qt + 1) * P
                pe.wait_ge(gp_s.sem, gp_s.after("odd" if hp else "even", p + qt * NP))
                pe.wait_ge(dve_a.sem, dve_a.after("neg", n - 2))
                q_t = stage[:, hp, b, :]
                for lo in range(0, W, BANK):
                    hi = min(lo + BANK, W)
                    last = min(hi, qt * P)
                    if last > lo:
                        pe.matmul(ps_s[:, u, lo:last], c["ident16"][:], att["km"][:, b, lo:last], start=True,
                                  stop=False, skip_group_check=True)
                    if hi == W:
                        pe.matmul(ps_s[:, u, W - P:W], c["ident16"][:], att["dm"][:, b * S + W - P:b * S + W],
                                  start=last <= lo, stop=False, skip_group_check=True)
                    ins = pe.matmul(ps_s[:, u, lo:hi], q_t, att["kT"][:, b * S + lo:b * S + hi], start=False,
                                    stop=True, skip_group_check=True)
                ins.then_inc(pe_a.sem, 1)

            def b(qt, p, v):
                n, hp, b_, u = unit(qt, p, v), v // 2, v % 2, v % 2
                n_blocks = qt + 1
                first = (n_blocks + 1) // 2
                pe.wait_ge(act_a.sem, act_a.after("exp", n))
                pe.wait_ge(act_b.sem, act_b.after("pt0", n - 1))
                for k in range(first):
                    ins = pe.transpose(ps_pt[:, 0, k * P:(k + 1) * P], prob[:, u, k * P:(k + 1) * P], c["ident"][:])
                ins.then_inc(pe_b.sem, 1 if first < n_blocks else 2)
                if first < n_blocks:
                    pe.wait_ge(dve_b.sem, dve_b.after("pt1", n - 1))
                    for k in range(first, n_blocks):
                        ins = pe.transpose(ps_pt[:, 1, (k - first) * P:(k - first + 1) * P],
                                           prob[:, u, k * P:(k + 1) * P], c["ident"][:])
                    ins.then_inc(pe_b.sem, 1)
                pe.wait_ge(act_b.sem, act_b.after("pt0", n))
                pe.wait_ge(fin.sem, fin.after("ot1", (p + qt * NP) * 2 + hp - 2))
                for k in range(n_blocks):
                    if k == first:
                        pe.wait_ge(dve_b.sem, dve_b.after("pt1", n))
                    ins = pe.matmul(ps_o[:, hp, b_ * DH:(b_ + 1) * DH], pT[:, u, k * P:(k + 1) * P],
                                    att["v"][:, b_ * TB + k, :], start=(k == 0), stop=(k == n_blocks - 1))
                ins.then_inc(pe_b.sem, 1)

            for qt in range(TB):
                units(pe, qt, a, b)

        @block.vector
        def _(dve):
            dve_a.open(dve)
            dve_b.open(dve)
            fin.open(dve)

            def a(qt, p, v):
                n, hp, u = unit(qt, p, v), v // 2, v % 2
                head_p = p + qt * NP
                b = v % 2
                dve.wait_ge(act_a.sem, act_a.after("p0", n - 4))
                dve.tensor_copy(nsn[:, v:v + 1], att["nsn"][:, b * TB + qt, bass.ds(p * 2 + hp, 1)]).then_inc(dve_a.sem, 1)
                dve.wait_ge(pe_a.sem, pe_a.after("scores", n))
                dve.wait_ge(dve_a.sem, dve_a.after("null", n))
                dve.wait_ge(bias_in[hp], (head_p + 1) * 16)
                dve.wait_ge(pe_b.sem, pe_b.after("t1", n - 2))
                W = (qt + 1) * P
                dve.sem_inc(dve_a.sem, 1)
                dve.tensor_tensor_reduce(out=prob[:, u, 0:W], in0=ps_s[:, u, 0:W], in1=bias[:, hp, 0:W], scale=-1.0,
                                         scalar=nsn[:, v:v + 1], op0=ALU.add, op1=ALU.min,
                                         accum_out=nmax[:, v:v + 1]).then_inc(dve_a.sem, 1)

            def b(qt, p, v):
                n, hp, u = unit(qt, p, v), v // 2, v % 2
                n_blocks = qt + 1
                first = (n_blocks + 1) // 2
                if first < n_blocks:
                    dve.wait_ge(pe_b.sem, pe_b.after("t1", n))
                    dve.wait_ge(pe_b.sem, pe_b.after("pv", n - 2))
                    dve.tensor_copy(pT[:, u, first * P:n_blocks * P], ps_pt[:, 1, 0:(n_blocks - first) * P]
                                    ).then_inc(dve_b.sem, 1)
                else:
                    dve.sem_inc(dve_b.sem, 1)
                if v % 2 == 0:
                    return
                h = (p + qt * NP) * 2 + hp
                two = slice(2 * hp, 2 * hp + 2)
                dve.wait_ge(act_a.sem, act_a.after("p0", n))
                dve.tensor_tensor(tot[:, two], rsum[:, two], p0[:, two], ALU.add).then_inc(fin.sem, 1)
                dve.wait_ge(fin.sem, fin.after("tot", h))
                dve.reciprocal(rinv[:, two], tot[:, two]).then_inc(fin.sem, 1)
                dve.wait_ge(pe_b.sem, pe_b.after("pv", n))
                for b_ in range(2):
                    w = 2 * hp + b_
                    dve.scalar_tensor_tensor(ot[:, w, :], att["nv"][:], p0[:, w:w + 1],
                                             ps_o[:, hp, b_ * DH:(b_ + 1) * DH], ALU.mult, ALU.add).then_inc(fin.sem, 1)
                dve.wait_ge(fin.sem, fin.after("ot1", h))
                for b_ in range(2):
                    w = 2 * hp + b_
                    dve.tensor_scalar(att["qo"][:, b_ * TB + qt, bass.ds(p, 1), hp * DH:(hp + 1) * DH],
                                      ot[:, w:w + 1, :], rinv[:, w:w + 1], None, ALU.mult).then_inc(fin.sem, 1)

            for qt in range(TB):
                units(dve, qt, a, b)
            dve.wait_ge(fin.sem, fin.after("o1", TB * H - 1))

        @block.scalar
        def _(act):
            act_a.open(act)
            act_b.open(act)

            def a(qt, p, v):
                n, u = unit(qt, p, v), v % 2
                W = (qt + 1) * P
                act.wait_ge(dve_a.sem, dve_a.after("neg", n))
                act.activation(prob[:, u, 0:W], prob[:, u, 0:W], ACT.Exp, bias=nmax[:, v:v + 1], scale=-1.0,
                               accum_out=rsum[:, v:v + 1]).then_inc(act_a.sem, 1)
                act.activation(p0[:, v:v + 1], nsn[:, v:v + 1], ACT.Exp, bias=nmax[:, v:v + 1],
                               scale=-1.0).then_inc(act_a.sem, 1)

            def b(qt, p, v):
                n, u = unit(qt, p, v), v % 2
                first = (qt + 2) // 2
                act.wait_ge(pe_b.sem, pe_b.after("t0", n))
                act.wait_ge(pe_b.sem, pe_b.after("pv", n - 2))
                act.activation(pT[:, u, 0:first * P], ps_pt[:, 0, 0:first * P], ACT.Copy).then_inc(act_b.sem, 1)

            for qt in range(TB):
                units(act, qt, a, b, b_first=True)


def out_phase(nc, pool, c, att, wo, g):
    with Phase(nc, pool) as ph:
        w = ph.sb("w", [P, NP, D])
        gt = ph.sb("gt", [P, D])
        o = ph.sb("o", [P, 2, INNER])
        oT = ph.sb("oT", [P, 2, INNER])
        stats = ph.sb("stats", [P, 2, 6])
        mv = ph.sb("mv", [P, 2, 2])
        sd = ph.sb("sd", [P, 2, 1])
        rstd = ph.sb("rstd", [P, 2, 1])
        yc = ph.sb("yc", [P, 2, D])
        ps_t = ph.ps("ps_t", [P, 2, 2 * BANK])
        ps_y = ph.ps("ps_y", [P, 2, BANK])
        weights = ph.sem()
        gp_a = ph.steps("o")
        pe_a = ph.steps("oT")
        act_a = ph.steps("oT")
        dve_a = ph.steps("oT")
        pe_b = ph.steps("y")
        dve_b = ph.steps("stats waited moments rstd centred y")
        act_b = ph.steps("sd")
        block = ph.stack.enter_context(nc.Block())

        @block.sync
        def _(sp):
            sp.dma_start(w[:], wo.rearrange("(k p) n -> p k n", p=P)).then_inc(weights, 16)
            sp.dma_start(gt[:], row(g, D)).then_inc(weights, 16)

        @block.gpsimd
        def _(gp):
            gp_a.open(gp)

            def stage(t, u):
                gp.wait_ge(pe_a.sem, pe_a.after("oT", t - 2))
                gp.tensor_copy(o[:, u, :], att["qo"][:, bass.ds(t, 1)].rearrange("p a q n -> p (a q n)")
                               ).then_inc(gp_a.sem, 1)

            tiles(gp, NT, stage)

        @block.tensor
        def _(pe):
            pe_a.open(pe)
            pe_b.open(pe)
            pe.wait_ge(weights, 32)

            def a(t, u):
                pe.wait_ge(gp_a.sem, gp_a.after("o", t))
                pe.wait_ge(act_a.sem, act_a.after("oT", t - 2))
                pe.wait_ge(dve_a.sem, dve_a.after("oT", t - 2))
                for k in range(NP):
                    ins = pe.transpose(ps_t[:, u, k * P:(k + 1) * P], o[:, u, k * P:(k + 1) * P], c["ident"][:])
                ins.then_inc(pe_a.sem, 1)

            def b(t, u):
                pe.wait_ge(act_a.sem, act_a.after("oT", t))
                pe.wait_ge(dve_a.sem, dve_a.after("oT", t))
                pe.wait_ge(dve_b.sem, dve_b.after("centred", t - 2))
                for k in range(NP):
                    ins = pe.matmul(ps_y[:, u, 0:D], oT[:, u, k * P:(k + 1) * P], w[:, k, :], start=(k == 0),
                                    stop=(k == NP - 1))
                ins.then_inc(pe_b.sem, 1)

            skewed(pe, NT, a, b)

        @block.vector
        def _(dve):
            dve_a.open(dve)
            dve_b.open(dve)
            dve.wait_ge(weights, 32)

            def a(t, u):
                dve.wait_ge(pe_a.sem, pe_a.after("oT", t))
                dve.wait_ge(pe_b.sem, pe_b.after("y", t - 2))
                dve.tensor_copy(oT[:, u, BANK:], ps_t[:, u, BANK:]).then_inc(dve_a.sem, 1)

            def b(t, u):
                dve.wait_ge(pe_b.sem, pe_b.after("y", t))
                dve.bn_stats(stats[:, u, :], ps_y[:, u, 0:D]).then_inc(dve_b.sem, 1)
                dve.wait_ge(dve_b.sem, dve_b.after("stats", t))
                dve.sem_inc(dve_b.sem, 1)
                dve.bn_aggr(mv[:, u, :], stats[:, u, :]).then_inc(dve_b.sem, 1)
                dve.wait_ge(act_b.sem, act_b.after("sd", t))
                dve.reciprocal(rstd[:, u, :], sd[:, u, :]).then_inc(dve_b.sem, 1)
                dve.wait_ge(dve_b.sem, dve_b.after("rstd", t))
                dve.tensor_scalar(yc[:, u, :], ps_y[:, u, 0:D], mv[:, u, 0:1], rstd[:, u, 0:1], ALU.subtract,
                                  ALU.mult).then_inc(dve_b.sem, 1)
                dve.wait_ge(dve_b.sem, dve_b.after("centred", t))
                dve.tensor_tensor(c["cur"][:, bass.ds(t, 1), :].rearrange("p a d -> p (a d)"), yc[:, u, :], gt[:],
                                  ALU.mult).then_inc(dve_b.sem, 1)

            skewed(dve, NT, a, b)

        @block.scalar
        def _(act):
            act_a.open(act)
            act_b.open(act)

            def a(t, u):
                act.wait_ge(pe_a.sem, pe_a.after("oT", t))
                act.wait_ge(pe_b.sem, pe_b.after("y", t - 2))
                act.activation(oT[:, u, 0:BANK], ps_t[:, u, 0:BANK], ACT.Copy).then_inc(act_a.sem, 1)

            def b(t, u):
                act.wait_ge(dve_b.sem, dve_b.after("moments", t))
                act.activation(sd[:, u, :], mv[:, u, 1:2], ACT.Sqrt, bias=c["eps"][:, 0:1]).then_inc(act_b.sem, 1)

            skewed(act, NT, a, b)

N_SLOT_TILES = {1: NT + 8, 2: 2 * NT + 8}


def interleaved(eng, n, a1, b, a2):

    def step(t, u):
        a1(t, u)
        b(t - 1, 1 - u)
        a2(t, u)

    a1(0, 0)
    a2(0, 0)
    with eng.Fori(0, n // 2 - 1) as i:
        step(i * 2 + 1, 1)
        step(i * 2 + 2, 0)
    step(n - 1, 1)
    b(n - 1, 1)


def loaded(t, u, n_dmas):
    return (t - u + 2) * (8 * n_dmas)


def logits_phase(nc, pool, c, r, src, gate_w, bias, cond=None, halve=False, shared=None, rms=None):
    E = gate_w.shape[1]
    with Phase(nc, pool) as ph:
        w = ph.sb("w", [P, KD, E])
        lb = ph.sb("lb", [P, B, E])
        xs = ph.sb("xs", [P, 2, D])
        xT = ph.sb("xT", [P, 2, KD, P])
        if cond is not None:
            cw = ph.sb("cw", [64, E])
            cg = ph.sb("cg", [64, B])
            cgb = ph.sb("cgb", [64, B, P])
        if shared is not None:
            wg = ph.sb("wg", [P, KD, D])
            wu = ph.sb("wu", [P, KD, D])
            wd = ph.sb("wd", [P, KD, D])
            small = ph.sb("small", [P, 2, D])
            lr = ph.sb("lr", [P, 2, D])
            hT = ph.sb("hT", [P, 2, D])
        if rms is not None:
            gt = ph.sb("gt", [P, D])
            sq = ph.sb("sq", [P, 2, D])
            ms = ph.sb("ms", [P, 2, 4])
        ps_x = ph.ps("ps_x", [P, 2, BANK])
        ps_l = ph.ps("ps_l", [P, 1, BANK])
        if shared is not None:
            ps_g = ph.ps("ps_g", [P, 2, BANK])
            ps_u = ph.ps("ps_u", [P, 2, BANK])
            ps_y = ph.ps("ps_y", [P, 1, BANK])

        weights, biased, cb, rep = ph.sem(), ph.sem(), ph.sem(), ph.sem()
        gp_a = ph.steps("x")
        pe_x = ph.steps("xT")
        act_x = ph.steps("xT")
        pe_l = ph.steps("logits")
        dve_l = ph.steps("logits")
        pe_s = ph.steps("gate up")
        act_s = ph.steps("hundredth")
        dve_s = ph.steps("leaky h")
        pe_y = ph.steps("y")
        act_y = ph.steps("y")
        act_n = ph.steps("ms root")
        dve_n = ph.steps("rinv scaled xn")
        block = ph.stack.enter_context(nc.Block())
        loads = [(w[:], gate_w.rearrange("(k p) n -> p k n", p=P))]
        if bias is not None:
            loads += [(lb[:, b, :], row(bias, E)) for b in range(B)]
        if cond is not None:
            loads += [(cw[:], cond[1])]
            loads += [(cg[:, b:b + 1], bass.AP(cond[0].tensor, cond[0].offset + 64 * b, [[1, 64], [1, 1]])) for b in range(B)]
        if shared is not None:
            loads += [(s[:], d.rearrange("(k p) n -> p k n", p=P)) for s, d in zip((wg, wu, wd), shared)]
        if rms is not None:
            loads += [(gt[:], row(rms, D))]

        @block.sync
        def _(sp):
            for dst, src_ in loads:
                sp.dma_start(dst, src_).then_inc(weights, 16)
            sp.wait_ge(weights, 16 * len(loads))

        @block.gpsimd
        def _(gp):
            gp_a.open(gp)

            def stage(t, u):
                gp.wait_ge(pe_x.sem, pe_x.after("xT", t - 2))
                if rms is not None:
                    gp.wait_ge(dve_n.sem, dve_n.after("xn", t))
                gp.tensor_copy(xs[:, u, :], src[:, bass.ds(t, 1), :].rearrange("p a d -> p (a d)")).then_inc(gp_a.sem, 1)

            tiles(gp, NT, stage)

        @block.tensor
        def _(pe):
            for s in (pe_x, pe_l, pe_s, pe_y):
                s.open(pe)
            pe.wait_ge(weights, 16 * len(loads))
            if cond is not None:
                pe.wait_ge(rep, 2)
                for b in range(B):
                    ins = pe.matmul(ps_l[:, 0, b * E:(b + 1) * E], cgb[:, b, :], cw[:], start=True, stop=True)
                ins.then_inc(cb, 1)
                pe.wait_ge(biased, 1)

            def a1(t, u):
                pe.wait_ge(gp_a.sem, gp_a.after("x", t))
                pe.wait_ge(act_x.sem, act_x.after("xT", t - 2))
                for k in range(KD):
                    ins = pe.transpose(ps_x[:, u, k * P:(k + 1) * P], xs[:, u, k * P:(k + 1) * P], c["ident"][:])
                ins.then_inc(pe_x.sem, 1)

            def a2(t, u):
                pe.wait_ge(act_x.sem, act_x.after("xT", t))
                pe.wait_ge(dve_l.sem, dve_l.after("logits", t - 1))
                for k in range(KD):
                    ins = pe.matmul(ps_l[:, 0, 0:E], xT[:, u, k, :], w[:, k, :], start=(k == 0), stop=(k == KD - 1))
                ins.then_inc(pe_l.sem, 1)
                if shared is not None:
                    for ww, ps, used in ((wg, ps_g, "leaky"), (wu, ps_u, "h")):
                        pe.wait_ge(dve_s.sem, dve_s.after(used, t - 2))
                        for m in range(D // P):
                            for k in range(KD):
                                ins = pe.matmul(ps[:, u, m * P:(m + 1) * P], ww[:, k, m * P:(m + 1) * P], xT[:, u, k, :],
                                                start=(k == 0), stop=(k == KD - 1))
                        ins.then_inc(pe_s.sem, 1)

            def b(t, u):
                if shared is None:
                    return
                pe.wait_ge(dve_s.sem, dve_s.after("h", t))
                pe.wait_ge(act_y.sem, act_y.after("y", t - 1))
                for m in range(D // P):
                    ins = pe.matmul(ps_y[:, 0, 0:D], hT[:, u, m * P:(m + 1) * P], wd[:, m, :], start=(m == 0),
                                    stop=(m == D // P - 1))
                ins.then_inc(pe_y.sem, 1)

            interleaved(pe, NT, a1, b, a2)

        @block.scalar
        def _(act):
            for s in (act_x, act_s, act_y, act_n):
                s.open(act)

            def norm(t, u):
                if rms is None:
                    return
                act.wait_ge(dve_n.sem, dve_n.after("xn", t - 2))
                act.activation(sq[:, u, :], src[:, bass.ds(t, 1), :].rearrange("p a d -> p (a d)"), ACT.Square,
                               scale=float(D) ** -0.5, accum_out=ms[:, u, 0:1]).then_inc(act_n.sem, 1)
                act.wait_ge(act_n.sem, act_n.after("ms", t))
                act.activation(ms[:, u, 1:2], ms[:, u, 0:1], ACT.Sqrt, bias=c["eps"][:, 1:2]).then_inc(act_n.sem, 1)

            def xT_out(t, u):
                act.wait_ge(pe_x.sem, pe_x.after("xT", t))
                act.wait_ge(pe_l.sem, pe_l.after("logits", t - 2))
                if shared is not None:
                    act.wait_ge(pe_s.sem, pe_s.after("up", t - 2))
                act.activation(xT[:, u].rearrange("p k n -> p (k n)"), ps_x[:, u, 0:D], ACT.Copy).then_inc(act_x.sem, 1)

            def hundredth(t, u):
                act.wait_ge(pe_s.sem, pe_s.after("gate", t))
                act.wait_ge(dve_s.sem, dve_s.after("leaky", t - 2))
                act.activation(small[:, u, :], ps_g[:, u, 0:D], ACT.Copy, scale=0.01).then_inc(act_s.sem, 1)

            def y_out(t, u):
                act.wait_ge(pe_y.sem, pe_y.after("y", t))
                act.activation(r["acc"][:, bass.ds(t, 1), :], ps_y[:, 0:1, 0:D], ACT.Copy).then_inc(act_y.sem, 1)

            if shared is not None:
                interleaved(act, NT, xT_out, y_out, hundredth)
            else:
                skewed(act, NT, norm, xT_out)

        @block.vector
        def _(dve):
            for s in (dve_l, dve_s, dve_n):
                s.open(dve)
            dve.wait_ge(weights, 16 * len(loads))
            if cond is not None:
                for b in range(B):
                    dve.tensor_copy(cgb[:, b, :], cg[:, b:b + 1].to_broadcast([64, P])).then_inc(rep, 1)
                dve.wait_ge(cb, 1)
                dve.tensor_copy(lb[:].rearrange("p b e -> p (b e)"), ps_l[:, 0, 0:B * E]).then_inc(biased, 1)
                dve.wait_ge(biased, 1)

            def norm(t, u):
                if rms is None:
                    return
                x_t = src[:, bass.ds(t, 1), :].rearrange("p a d -> p (a d)")
                dve.wait_ge(act_n.sem, act_n.after("root", t))
                dve.reciprocal(ms[:, u, 2:3], ms[:, u, 1:2]).then_inc(dve_n.sem, 1)
                dve.wait_ge(dve_n.sem, dve_n.after("rinv", t))
                dve.tensor_scalar(sq[:, u, :], x_t, ms[:, u, 2:3], None, ALU.mult).then_inc(dve_n.sem, 1)
                dve.wait_ge(dve_n.sem, dve_n.after("scaled", t))
                dve.tensor_tensor(x_t, sq[:, u, :], gt[:], ALU.mult).then_inc(dve_n.sem, 1)

            def b(t, u):
                dve.wait_ge(pe_l.sem, pe_l.after("logits", t))
                l_t = r["logits"][:, bass.ds(t, 1), 0:E].rearrange("p a e -> p (a e)")
                dve.tensor_copy(l_t, ps_l[:, 0, 0:E]).then_inc(dve_l.sem, 1)
                if shared is not None:
                    dve.wait_ge(act_s.sem, act_s.after("hundredth", t))
                    dve.tensor_tensor(lr[:, u, :], small[:, u, :], ps_g[:, u, 0:D], ALU.max).then_inc(dve_s.sem, 1)
                    dve.wait_ge(dve_s.sem, dve_s.after("leaky", t))
                    dve.wait_ge(pe_s.sem, pe_s.after("up", t))
                    dve.wait_ge(pe_y.sem, pe_y.after("y", t - 2))
                    dve.tensor_tensor(hT[:, u, :], lr[:, u, :], ps_u[:, u, 0:D], ALU.mult).then_inc(dve_s.sem, 1)

            skewed(dve, NT, norm, b)
            if bias is not None or cond is not None:
                dve.wait_ge(dve_l.sem, dve_l.after("logits", NT - 1))
                for b_ in range(B):
                    l_b = r["logits"][:, b_ * TB:(b_ + 1) * TB, 0:E]
                    dve.tensor_tensor(l_b, l_b, lb[:, b_, :].unsqueeze(1).to_broadcast([P, TB, E]), ALU.add).then_inc(biased, 1)
                if halve:
                    dve.wait_ge(biased, 3)
                    l_a = r["logits"][:, :, 0:E]
                    dve.tensor_scalar(l_a, l_a, 0.5, None, ALU.mult).then_inc(biased, 1)


def choose_phase(nc, pool, c, r, E, choices, dispatch_src, xs_dram, capacity=None, softmax_all=True, dma_done=None):
    n_slots = E * P if capacity else N_SLOT_TILES[choices] * P
    with Phase(nc, pool) as ph:
        L = r["logits"][:, :, 0:E]
        iota_i = ph.sb("iota_i", [P, NT, E], I32)
        iota = ph.sb("iota", [P, NT, E])
        far = ph.sb("far", [P, NT, E])
        mx = ph.sb("mx", [P, 2, NT])
        idx = ph.sb("idx", [P, 2, NT])
        oh = ph.sb("oh", [P, 2, NT, E])
        ex = ph.sb("ex", [P, NT, E])
        z = ph.sb("z", [P, 4, NT])
        m16 = ph.sb("m16", [P, NT * E], BF16)
        msum = ph.sb("msum", [P, NT, E])
        tri = ph.sb("tri", [P, P], BF16)
        ones16 = ph.sb("ones16", [P, P], BF16)
        cum = ph.sb("cum", [P, 2, NT + 1, E])
        rank = ph.sb("rank", [P, NT, E])
        cnt_i = ph.sb("cnt_i", [P, 2, E], I32)
        ends = ph.sb("ends", [P, 3, E + 1])
        sel = ph.sb("sel", [P, NT, E])
        slot_f = ph.sb("slot_f", [P, 4, NT])
        n_slot_tiles = n_slots // P
        tmap = ph.sb("tmap", [P, n_slot_tiles, E])
        tio_i = ph.sb("tio_i", [P, n_slot_tiles, E], I32)
        tio = ph.sb("tio", [P, n_slot_tiles, E])
        tsum = ph.sb("tsum", [P, n_slot_tiles])
        ps_r = ph.ps("ps_r", [P, BANK])
        ps_t = ph.ps("ps_t", [P, BANK])
        made, v, prefix, exped, slots_ready = (ph.sem() for _ in range(5))
        block = ph.stack.enter_context(nc.Block())
        count = {"v": 0}

        @block.gpsimd
        def _(gp):
            gp.iota(iota_i[:], pattern=[[0, NT], [1, E]], base=0, channel_multiplier=0).then_inc(made, 1)
            gp.iota(tio_i[:], pattern=[[1, n_slot_tiles], [0, E]], base=0, channel_multiplier=0).then_inc(made, 1)
            gp.memset(tri[:], 1.0).then_inc(made, 1)
            gp.memset(ones16[:], 1.0).then_inc(made, 1)
            gp.wait_ge(made, 4)
            gp.affine_select(out=tri[:], in_=tri[:], compare_op=ALU.is_gt, fill=0.0, base=0, pattern=[[1, P]],
                             channel_multiplier=-1).then_inc(made, 1)
            gp.wait_ge(slots_ready, 1)
            for t in range(NT):
                for k in range(choices):
                    gp.indirect_dma_start(out=xs_dram[0:n_slots, :],
                                          out_offset=bass.IndirectOffsetOnAxis(ap=r["slot_out"][:, k, t:t + 1], axis=0),
                                          in_=dispatch_src[:, t, :], in_offset=None, bounds_check=n_slots - 1,
                                          oob_is_err=False).then_inc(dma_done["sem"], 16)
            dma_done["count"] += 16 * NT * choices
            gp.wait_ge(dma_done["sem"], dma_done["count"])

        @block.tensor
        def _(pe):
            pe.wait_ge(made, 5)
            pe.wait_ge(prefix, 1)
            pe.matmul(ps_r[:, 0:NT * E], tri[:], m16[:], start=True, stop=True).then_inc(prefix, 1)
            pe.matmul(ps_t[:, 0:NT * E], ones16[:], m16[:], start=True, stop=True).then_inc(prefix, 1)

        @block.scalar
        def _(act):
            act.wait_ge(exped, 1)
            act.activation(ex[:], ex[:], ACT.Exp).then_inc(exped, 1)
            if choices == 2:
                act.activation(z[:, 1, :], z[:, 1, :], ACT.Exp).then_inc(exped, 1)

        @block.vector
        def _(dve):
            def then(ins):
                count["v"] += 1
                ins.then_inc(v, 1)
                dve.wait_ge(v, count["v"])

            wide = [P, NT, E]
            dve.wait_ge(made, 2)
            then(dve.tensor_copy(iota[:], iota_i[:]))
            then(dve.tensor_copy(tio[:], tio_i[:]))
            for k in range(choices):
                if k == 1:
                    then(dve.scalar_tensor_tensor(sel[:], oh[:, 0], -3e38, L, ALU.mult, ALU.add))
                Lk = L if k == 0 else sel[:]
                then(dve.tensor_reduce(mx[:, k, :], Lk, AX, ALU.max))
                then(dve.tensor_tensor(far[:], Lk, bc(mx[:, k, :], wide), ALU.is_lt))
                then(dve.scalar_tensor_tensor(far[:], far[:], float(E), iota[:], ALU.mult, ALU.add))
                then(dve.tensor_reduce(idx[:, k, :], far[:], AX, ALU.min))
                then(dve.tensor_tensor(oh[:, k], iota[:], bc(idx[:, k, :], wide), ALU.is_equal))
            then(dve.tensor_tensor(ex[:], L, bc(mx[:, 0, :], wide), ALU.subtract))
            if choices == 2:
                then(dve.tensor_tensor(z[:, 1, :], mx[:, 1, :], mx[:, 0, :], ALU.subtract))
            dve.sem_inc(exped, 1)
            if choices == 2:
                then(dve.tensor_tensor(msum[:], oh[:, 0], oh[:, 1], ALU.add))
                then(dve.tensor_copy(m16[:], msum[:].rearrange("p t e -> p (t e)")))
            else:
                then(dve.tensor_copy(m16[:], oh[:, 0].rearrange("p t e -> p (t e)")))
            dve.sem_inc(prefix, 1)
            dve.wait_ge(exped, choices + 1)
            if softmax_all:
                then(dve.tensor_reduce(z[:, 0, :], ex[:], AX, ALU.add))
            if choices == 1:
                then(dve.reciprocal(r["wt"][:, 0, :], z[:, 0, :]))
            else:
                if softmax_all:
                    then(dve.tensor_scalar(z[:, 2, :], z[:, 1, :], 1.0, None, ALU.add))
                    then(dve.scalar_tensor_tensor(z[:, 2, :], z[:, 0, :], 1e-20, z[:, 2, :], ALU.mult, ALU.add))
                else:
                    then(dve.tensor_scalar(z[:, 2, :], z[:, 1, :], 1.0, None, ALU.add))
                then(dve.reciprocal(r["wt"][:, 0, :], z[:, 2, :]))
                then(dve.tensor_tensor(r["wt"][:, 1, :], z[:, 1, :], r["wt"][:, 0, :], ALU.mult))
            dve.wait_ge(prefix, 3)
            then(dve.memset(cum[:, 0, 0, :], 0.0))
            then(dve.memset(cum[:, 1, 0, :], 0.0))
            then(dve.tensor_copy(cum[:, 0, 1:, :], ps_t[:, 0:NT * E].rearrange("p (t e) -> p t e", e=E)))
            at, shift = 0, 1
            while shift < NT:
                then(dve.tensor_copy(cum[:, 1 - at, 1:shift + 1, :], cum[:, at, 1:shift + 1, :]))
                then(dve.tensor_tensor(cum[:, 1 - at, shift + 1:, :], cum[:, at, shift + 1:, :],
                                       cum[:, at, 1:NT + 1 - shift, :], ALU.add))
                at, shift = 1 - at, shift * 2
            then(dve.tensor_tensor(rank[:], ps_r[:, 0:NT * E].rearrange("p (t e) -> p t e", e=E), cum[:, at, 0:NT, :], ALU.add))
            if capacity:
                then(dve.tensor_tensor(sel[:], oh[:, 0], rank[:], ALU.mult))
                then(dve.tensor_reduce(slot_f[:, 0, :], sel[:], AX, ALU.add))
                then(dve.tensor_scalar(slot_f[:, 1, :], slot_f[:, 0, :], float(capacity), None, ALU.is_lt))
                then(dve.tensor_tensor(r["wt"][:, 0, :], r["wt"][:, 0, :], slot_f[:, 1, :], ALU.mult))
                then(dve.tensor_scalar(slot_f[:, 0, :], slot_f[:, 0, :], float(capacity - 1), None, ALU.min))
                then(dve.scalar_tensor_tensor(slot_f[:, 0, :], idx[:, 0, :], float(P), slot_f[:, 0, :], ALU.mult, ALU.add))
                then(dve.tensor_copy(r["slot"][:, 0, :], slot_f[:, 0, :]))
                then(dve.tensor_scalar(slot_f[:, 2, :], slot_f[:, 1, :], -float(n_slots), float(n_slots), ALU.mult, ALU.add))
                then(dve.tensor_tensor(slot_f[:, 3, :], slot_f[:, 2, :], slot_f[:, 0, :], ALU.add))
                then(dve.tensor_copy(r["slot_out"][:, 0, :], slot_f[:, 3, :]))
                dve.sem_inc(slots_ready, 1)
                return
            then(dve.tensor_scalar(ends[:, 2, 0:E], cum[:, at, NT, :], float(P - 1), None, ALU.add))
            then(dve.tensor_copy(cnt_i[:, 0, :], ends[:, 2, 0:E]))
            then(dve.tensor_scalar(cnt_i[:, 1, :], cnt_i[:, 0, :], 7, None, ALU.arith_shift_right))
            then(dve.memset(ends[:, 0, 0:1], 0.0))
            then(dve.memset(ends[:, 1, 0:1], 0.0))
            then(dve.tensor_copy(ends[:, 0, 1:], cnt_i[:, 1, :]))
            a2, shift = 0, 1
            while shift < E:
                then(dve.tensor_copy(ends[:, 1 - a2, 1:shift + 1], ends[:, a2, 1:shift + 1]))
                then(dve.tensor_tensor(ends[:, 1 - a2, shift + 1:], ends[:, a2, shift + 1:], ends[:, a2, 1:E + 1 - shift], ALU.add))
                a2, shift = 1 - a2, shift * 2
            then(dve.tensor_scalar(ends[:, 2, 0:E], ends[:, a2, 0:E], float(P), None, ALU.mult))
            then(dve.tensor_tensor(rank[:], rank[:], ends[:, 2, 0:E].unsqueeze(1).to_broadcast(wide), ALU.add))
            for k in range(choices):
                then(dve.tensor_tensor(sel[:], oh[:, k], rank[:], ALU.mult))
                then(dve.tensor_reduce(slot_f[:, k, :], sel[:], AX, ALU.add))
                then(dve.tensor_copy(r["slot"][:, k, :], slot_f[:, k, :]))
                then(dve.tensor_copy(r["slot_out"][:, k, :], slot_f[:, k, :]))
            dve.sem_inc(slots_ready, 1)
            then(dve.tensor_tensor(tmap[:], tio[:], ends[:, a2, 1:].unsqueeze(1).to_broadcast([P, n_slot_tiles, E]), ALU.is_ge))
            then(dve.tensor_reduce(tsum[:], tmap[:], AX, ALU.add))
            then(dve.tensor_scalar(tsum[:], tsum[:], float(E - 1), None, ALU.min))
            then(dve.tensor_copy(r["tile_expert"][:, 0:n_slot_tiles], tsum[:]))


def mlp_experts_phase(nc, pool, c, r, n_tiles, by_map, func, w1, b1, w2, b2, xs_dram, ys_dram):
    E, _, F = w1.shape
    FC = F // P
    n_dmas = 5
    with Phase(nc, pool) as ph:
        xs = ph.sb("xs", [P, 2, D])
        xT = ph.sb("xT", [P, 2, D])
        w1s = ph.sb("w1s", [P, 2, KD, F])
        w2s = ph.sb("w2s", [P, 2, FC, D])
        b1s = ph.sb("b1s", [P, 2, FC])
        b2s = ph.sb("b2s", [P, 2, D])
        hT = ph.sb("hT", [P, 2, F])
        ys = ph.sb("ys", [P, 2, D])
        nbank = (F + BANK - 1) // BANK
        per = BANK // P
        ps_x = ph.ps("ps_x", [P, 2, BANK])
        ps_h = ph.ps("ps_h", [P, 4, BANK])
        ps_y = ph.ps("ps_y", [P, 2, BANK])
        loads = [ph.sem(), ph.sem()]
        stores = [ph.sem(), ph.sem()]
        pe_x = ph.steps("xT")
        dve_x = ph.steps("xT")
        pe_h = ph.steps(" ".join(f"h{m}" for m in range(nbank)))
        act_h = ph.steps(" ".join(f"h{m}" for m in range(nbank)))
        pe_y = ph.steps("y")
        dve_y = ph.steps("y")
        block = ph.stack.enter_context(nc.Block())

        @block.sync
        def _(sp):
            def load(t, u):
                sp.wait_ge(pe_y.sem, pe_y.after("y", t - 2))
                sp.wait_ge(dve_y.sem, dve_y.after("y", t - 2))
                e = sp.value_load(r["tile_expert"][0:1, bass.ds(t, 1)], min_val=0, max_val=E - 1) if by_map else t
                sp.dma_start(xs[:, u, :], xs_dram[bass.ds(t * P, P), :]).then_inc(loads[u], 16)
                sp.dma_start(w1s[:, u], w1[bass.ds(e, 1)].rearrange("a (k p) f -> p (a k) f", p=P)).then_inc(loads[u], 16)
                sp.dma_start(b1s[:, u, :], b1[bass.ds(e, 1)].rearrange("a p f -> p (a f)")).then_inc(loads[u], 16)
                sp.dma_start(w2s[:, u], w2[bass.ds(e, 1)].rearrange("a (k p) n -> p (a k) n", p=P)).then_inc(loads[u], 16)
                sp.dma_start(b2s[:, u, :], b2[bass.ds(e, 1), :].to_broadcast([P, D])).then_inc(loads[u], 16)

            def store(t, u):
                sp.wait_ge(dve_y.sem, dve_y.after("y", t))
                sp.dma_start(ys_dram[bass.ds(t * P, P), :], ys[:, u, :]).then_inc(stores[u], 16)

            for u in range(2):
                sp.sem_inc(stores[u], 16)
            skewed(sp, n_tiles, load, store)
            for u in range(2):
                sp.wait_ge(stores[u], 8 * n_tiles + 16)

        @block.tensor
        def _(pe):
            for s in (pe_x, pe_h, pe_y):
                s.open(pe)

            def a1(t, u):
                pe.wait_ge(loads[u], loaded(t, u, n_dmas))
                pe.wait_ge(dve_x.sem, dve_x.after("xT", t - 2))
                for k in range(KD):
                    ins = pe.transpose(ps_x[:, u, k * P:(k + 1) * P], xs[:, u, k * P:(k + 1) * P], c["ident"][:])
                ins.then_inc(pe_x.sem, 1)

            def a2(t, u):
                pe.wait_ge(dve_x.sem, dve_x.after("xT", t))
                for f in range(FC):
                    bank = u * 2 + f // per
                    if f % per == 0:
                        pe.wait_ge(act_h.sem, act_h.after(f"h{f // per}", t - 2))
                    o = ps_h[:, bank, (f % per) * P:(f % per + 1) * P]
                    for k in range(KD):
                        ins = pe.matmul(o, w1s[:, u, k, f * P:(f + 1) * P], xT[:, u, k * P:(k + 1) * P],
                                        start=(k == 0), stop=(k == KD - 1))
                    if f % per == per - 1:
                        ins.then_inc(pe_h.sem, 1)

            def b(t, u):
                pe.wait_ge(dve_y.sem, dve_y.after("y", t - 2))
                for f in range(FC):
                    if f % per == 0:
                        pe.wait_ge(act_h.sem, act_h.after(f"h{f // per}", t))
                    ins = pe.matmul(ps_y[:, u, 0:D], hT[:, u, f * P:(f + 1) * P], w2s[:, u, f, :], start=(f == 0),
                                    stop=(f == FC - 1))
                ins.then_inc(pe_y.sem, 1)

            interleaved(pe, n_tiles, a1, b, a2)

        @block.scalar
        def _(act):
            act_h.open(act)

            def h(t, u):
                act.wait_ge(pe_y.sem, pe_y.after("y", t - 2))
                for f in range(FC):
                    if f % per == 0:
                        act.wait_ge(pe_h.sem, pe_h.after(f"h{f // per}", t))
                    o = ps_h[:, u * 2 + f // per, (f % per) * P:(f % per + 1) * P]
                    ins = act.activation(hT[:, u, f * P:(f + 1) * P], o, func, bias=b1s[:, u, f:f + 1])
                    if f % per == per - 1:
                        ins.then_inc(act_h.sem, 1)

            tiles(act, n_tiles, h)

        @block.vector
        def _(dve):
            dve_x.open(dve)
            dve_y.open(dve)

            def a(t, u):
                dve.wait_ge(pe_x.sem, pe_x.after("xT", t))
                dve.wait_ge(pe_h.sem, pe_h.after(f"h{nbank - 1}", t - 2))
                dve.tensor_copy(xT[:, u, :], ps_x[:, u, 0:D]).then_inc(dve_x.sem, 1)

            def b(t, u):
                dve.wait_ge(pe_y.sem, pe_y.after("y", t))
                dve.wait_ge(stores[u], loaded(t, u, 1))
                dve.tensor_tensor(ys[:, u, :], ps_y[:, u, 0:D], b2s[:, u, :], ALU.add).then_inc(dve_y.sem, 1)

            skewed(dve, n_tiles, a, b)


def glu_experts_phase(nc, pool, c, r, n_tiles, w_gate, w_up, w_down, xs_dram, ys_dram):
    E, _, M = w_gate.shape
    n_dmas = 4
    with Phase(nc, pool) as ph:
        xs = ph.sb("xs", [P, 2, D])
        xT = ph.sb("xT", [P, 2, D])
        wg = ph.sb("wg", [P, 2, KD, M])
        wu = ph.sb("wu", [P, 2, KD, M])
        wd = ph.sb("wd", [P, 2, D])
        small = ph.sb("small", [P, 2, P])
        lr = ph.sb("lr", [P, 2, P])
        hT = ph.sb("hT", [P, 2, P])
        ys = ph.sb("ys", [P, 2, D])
        ps_x = ph.ps("ps_x", [P, 2, BANK])
        ps_g = ph.ps("ps_g", [P, 2, BANK])
        ps_u = ph.ps("ps_u", [P, 2, BANK])
        ps_y = ph.ps("ps_y", [P, 2, BANK])
        loads = [ph.sem(), ph.sem()]
        stores = [ph.sem(), ph.sem()]
        pe_x = ph.steps("xT")
        act_x = ph.steps("xT")
        pe_h = ph.steps("gate up")
        act_h = ph.steps("hundredth")
        dve_h = ph.steps("leaky h")
        pe_y = ph.steps("y")
        dve_y = ph.steps("y")
        block = ph.stack.enter_context(nc.Block())

        @block.sync
        def _(sp):
            def load(t, u):
                sp.wait_ge(pe_y.sem, pe_y.after("y", t - 2))
                e = sp.value_load(r["tile_expert"][0:1, bass.ds(t, 1)], min_val=0, max_val=E - 1)
                sp.dma_start(xs[:, u, :], xs_dram[bass.ds(t * P, P), :]).then_inc(loads[u], 16)
                sp.dma_start(wg[:, u], w_gate[bass.ds(e, 1)].rearrange("a (k p) f -> p (a k) f", p=P)).then_inc(loads[u], 16)
                sp.dma_start(wu[:, u], w_up[bass.ds(e, 1)].rearrange("a (k p) f -> p (a k) f", p=P)).then_inc(loads[u], 16)
                sp.dma_start(wd[:, u], w_down[bass.ds(e, 1)].rearrange("a p n -> p (a n)")).then_inc(loads[u], 16)

            def store(t, u):
                sp.wait_ge(dve_y.sem, dve_y.after("y", t))
                sp.dma_start(ys_dram[bass.ds(t * P, P), :], ys[:, u, :]).then_inc(stores[u], 16)

            for u in range(2):
                sp.sem_inc(stores[u], 16)
            skewed(sp, n_tiles, load, store)
            for u in range(2):
                sp.wait_ge(stores[u], 8 * n_tiles + 16)

        @block.tensor
        def _(pe):
            for s in (pe_x, pe_h, pe_y):
                s.open(pe)

            def a1(t, u):
                pe.wait_ge(loads[u], loaded(t, u, n_dmas))
                pe.wait_ge(act_x.sem, act_x.after("xT", t - 2))
                for k in range(KD):
                    ins = pe.transpose(ps_x[:, u, k * P:(k + 1) * P], xs[:, u, k * P:(k + 1) * P], c["ident"][:])
                ins.then_inc(pe_x.sem, 1)

            def a2(t, u):
                pe.wait_ge(act_x.sem, act_x.after("xT", t))
                pe.wait_ge(dve_h.sem, dve_h.after("leaky", t - 2))
                for k in range(KD):
                    ins = pe.matmul(ps_g[:, u, 0:P], wg[:, u, k, :], xT[:, u, k * P:(k + 1) * P], start=(k == 0),
                                    stop=(k == KD - 1))
                ins.then_inc(pe_h.sem, 1)
                pe.wait_ge(dve_h.sem, dve_h.after("h", t - 2))
                for k in range(KD):
                    ins = pe.matmul(ps_u[:, u, 0:P], wu[:, u, k, :], xT[:, u, k * P:(k + 1) * P], start=(k == 0),
                                    stop=(k == KD - 1))
                ins.then_inc(pe_h.sem, 1)

            def b(t, u):
                pe.wait_ge(dve_h.sem, dve_h.after("h", t))
                pe.wait_ge(dve_y.sem, dve_y.after("y", t - 2))
                pe.matmul(ps_y[:, u, 0:D], hT[:, u, :], wd[:, u, :], start=True, stop=True).then_inc(pe_y.sem, 1)

            interleaved(pe, n_tiles, a1, b, a2)

        @block.scalar
        def _(act):
            act_x.open(act)
            act_h.open(act)

            def x(t, u):
                act.wait_ge(pe_x.sem, pe_x.after("xT", t))
                act.wait_ge(pe_h.sem, pe_h.after("up", t - 2))
                act.activation(xT[:, u, :], ps_x[:, u, 0:D], ACT.Copy).then_inc(act_x.sem, 1)

            def hundredth(t, u):
                act.wait_ge(pe_h.sem, pe_h.after("gate", t))
                act.wait_ge(dve_h.sem, dve_h.after("leaky", t - 2))
                act.activation(small[:, u, :], ps_g[:, u, 0:P], ACT.Copy, scale=0.01).then_inc(act_h.sem, 1)

            skewed(act, n_tiles, x, hundredth)

        @block.vector
        def _(dve):
            dve_h.open(dve)
            dve_y.open(dve)

            def h(t, u):
                dve.wait_ge(act_h.sem, act_h.after("hundredth", t))
                dve.tensor_tensor(lr[:, u, :], small[:, u, :], ps_g[:, u, 0:P], ALU.max).then_inc(dve_h.sem, 1)
                dve.wait_ge(dve_h.sem, dve_h.after("leaky", t))
                dve.wait_ge(pe_h.sem, pe_h.after("up", t))
                dve.wait_ge(pe_y.sem, pe_y.after("y", t - 2))
                dve.tensor_tensor(hT[:, u, :], lr[:, u, :], ps_u[:, u, 0:P], ALU.mult).then_inc(dve_h.sem, 1)

            def y(t, u):
                dve.wait_ge(pe_y.sem, pe_y.after("y", t))
                dve.wait_ge(stores[u], loaded(t, u, 1))
                dve.tensor_copy(ys[:, u, :], ps_y[:, u, 0:D]).then_inc(dve_y.sem, 1)

            tiles(dve, n_tiles, lambda t, u: (h(t, u), y(t, u)))


def combine_phase(nc, pool, c, r, choices, ys_dram, n_slots, dst, base=None, dma_done=None):
    with Phase(nc, pool) as ph:
        yg = ph.sb("yg", [P, choices, NT, D])
        v = ph.sem()
        block = ph.stack.enter_context(nc.Block())
        G = 4
        start = dma_done["count"]

        @block.gpsimd
        def _(gp):
            for t in range(NT):
                for k in range(choices):
                    gp.indirect_dma_start(out=yg[:, k, t, :], out_offset=None, in_=ys_dram[0:n_slots, :],
                                          in_offset=bass.IndirectOffsetOnAxis(ap=r["slot"][:, k, t:t + 1], axis=0),
                                          bounds_check=n_slots - 1, oob_is_err=False).then_inc(dma_done["sem"], 16)
            gp.wait_ge(dma_done["sem"], start + 16 * NT * choices)

        @block.vector
        def _(dve):
            n = 0
            dve.wait_ge(dma_done["sem"], start + 16 * NT * choices)
            for k in range(choices):
                for g in range(0, NT, G):
                    y = yg[:, k, g:g + G, :]
                    dve.tensor_tensor(y, y, bc(r["wt"][:, k, g:g + G], [P, G, D]), ALU.mult).then_inc(v, 1)
                    n += 1
            for k in range(choices):
                for g in range(0, NT, G):
                    dve.wait_ge(v, n)
                    d = dst[:, g:g + G, :]
                    other = base[:, g:g + G, :] if k == 0 and base is not None else d
                    if k == 0 and base is None:
                        dve.tensor_copy(d, yg[:, k, g:g + G, :]).then_inc(v, 1)
                    else:
                        dve.tensor_tensor(d, other, yg[:, k, g:g + G, :], ALU.add).then_inc(v, 1)
                    if g == NT - G:
                        n += NT // G
        dma_done["count"] = start + 16 * NT * choices


def bias_table_phase(nc, pool, c, w, table_dram, spread_dram, spread_done):
    NTP = S // P
    with Phase(nc, pool) as ph:
        pos_i = ph.sb("pos_i", [P, NTP], I32)
        pos = ph.sb("pos", [P, NTP])
        rows = {n: ph.sb(n, [P, D]) for n in ("w0", "b0", "g0", "b1", "g1")}
        w1 = ph.sb("w1", [P, KD, D])
        w2 = ph.sb("w2", [P, KD, H])
        b2 = ph.sb("b2", [H, 1])
        h = ph.sb("h", [P, NTP, D])
        hT = ph.sb("hT", [P, KD, S])
        stats = ph.sb("stats", [P, NTP, 6])
        mv = ph.sb("mv", [P, NTP, 2])
        sd = ph.sb("sd", [P, NTP])
        rstd = ph.sb("rstd", [P, NTP])
        table = ph.sb("table", [H, S + P])
        ps_t = ph.ps("ps_t", [P, KD, S])
        ps_h = ph.ps("ps_h", [P, NTP, D])
        loaded, made, v, spread, moments, rooted, normed, silued, turned, out_t, product, stored = (ph.sem() for _ in range(12))
        block = ph.stack.enter_context(nc.Block())
        n_loads = 16 * 8
        count = {"v": 0}

        @block.sync
        def _(sp):
            for n in rows:
                sp.dma_start(rows[n][:], row(w[n], D)).then_inc(loaded, 16)
            sp.dma_start(w1[:], w["w1"].rearrange("(k p) n -> p k n", p=P)).then_inc(loaded, 16)
            sp.dma_start(w2[:], w["w2"].rearrange("(k p) n -> p k n", p=P)).then_inc(loaded, 16)
            sp.dma_start(b2[:], w["b2"].rearrange("(h a) -> h a", a=1)).then_inc(loaded, 16)
            sp.wait_ge(product, 2)
            sp.wait_ge(v, 1)
            sp.dma_start(table_dram, table[:]).then_inc(stored, 16)
            sp.wait_ge(stored, 16)
            sp.dma_start(spread_dram, bass.AP(table_dram.tensor, table_dram.offset + P - 1,
                                              [[S + P, H], [-1, P], [1, S]])).then_inc(spread_done, 16)

        @block.gpsimd
        def _(gp):
            gp.iota(pos_i[:], pattern=[[-P, NTP]], base=S - 1, channel_multiplier=-1).then_inc(made, 1)

        @block.vector
        def _(dve):
            def then(ins):
                count["v"] += 1
                ins.then_inc(v, 1)
                dve.wait_ge(v, count["v"])

            def norm(gain, n):
                for t in range(NTP):
                    ins = dve.bn_stats(stats[:, t, :], h[:, t, :])
                then(ins)
                for t in range(NTP):
                    ins = dve.bn_aggr(mv[:, t, :], stats[:, t, :])
                ins.then_inc(moments, 1)
                dve.wait_ge(rooted, n)
                then(dve.reciprocal(rstd[:], sd[:]))
                for t in range(NTP):
                    ins = dve.tensor_scalar(h[:, t, :], h[:, t, :], mv[:, t, 0:1], rstd[:, t:t + 1], ALU.subtract, ALU.mult)
                then(ins)
                dve.tensor_tensor(h[:], h[:], rows[gain][:].unsqueeze(1).to_broadcast([P, NTP, D]),
                                  ALU.mult).then_inc(normed, 1)

            then(dve.memset(table[:, S:], 0.0))
            dve.wait_ge(made, 1)
            then(dve.tensor_copy(pos[:], pos_i[:]))
            dve.wait_ge(loaded, n_loads)
            for t in range(NTP):
                ins = dve.scalar_tensor_tensor(h[:, t, :], rows["w0"][:], pos[:, t:t + 1], rows["b0"][:], ALU.mult, ALU.add)
            then(ins)
            norm("g0", 1)
            dve.wait_ge(turned, 1)
            dve.tensor_copy(hT[:, 1, :], ps_t[:, 1, :]).then_inc(out_t, 1)
            dve.wait_ge(product, 1)
            then(dve.tensor_tensor(h[:], ps_h[:], rows["b1"][:].unsqueeze(1).to_broadcast([P, NTP, D]), ALU.add))
            norm("g1", 2)
            dve.wait_ge(turned, 2)
            dve.tensor_copy(hT[:, 1, :], ps_t[:, 1, :]).then_inc(out_t, 1)

        @block.scalar
        def _(act):
            for n in (1, 2):
                act.wait_ge(moments, n)
                act.activation(sd[:], mv[:, :, 1], ACT.Sqrt, bias=c["eps"][:, 0:1]).then_inc(rooted, 1)
                act.wait_ge(normed, n)
                act.activation(h[:], h[:], ACT.Silu).then_inc(silued, 1)
                act.wait_ge(turned, n)
                act.activation(hT[:, 0, :], ps_t[:, 0, :], ACT.Copy).then_inc(out_t, 1)
            act.wait_ge(spread, 1)
            act.wait_ge(loaded, n_loads)
            act.activation(table[:, 0:S], ps_h[0:H].rearrange("p a d -> p (a d)")[:, 0:S], ACT.Identity,
                           bias=b2[:, 0:1]).then_inc(product, 1)

        @block.tensor
        def _(pe):
            pe.wait_ge(loaded, n_loads)
            for n in (1, 2):
                pe.wait_ge(silued, n)
                for k in range(KD):
                    for t in range(NTP):
                        ins = pe.transpose(ps_t[:, k, t * P:(t + 1) * P], h[:, t, k * P:(k + 1) * P], c["ident"][:])
                ins.then_inc(turned, 1)
                pe.wait_ge(out_t, 2 * n)
                if n == 1:
                    for t in range(NTP):
                        for k in range(KD):
                            ins = pe.matmul(ps_h[:, t, :], hT[:, k, t * P:(t + 1) * P], w1[:, k, :], start=(k == 0),
                                            stop=(k == KD - 1))
                    ins.then_inc(product, 1)
                else:
                    flat = ps_h[0:H].rearrange("p a d -> p (a d)")
                    for lo in range(0, S, BANK):
                        for k in range(KD):
                            ins = pe.matmul(flat[:, lo:lo + BANK], w2[:, k, :], hT[:, k, lo:lo + BANK], start=(k == 0),
                                            stop=(k == KD - 1))
                    ins.then_inc(spread, 1)


def woven(eng, n, step):
    step(0, None, None, 0)
    step(1, 0, None, 1)
    with eng.Fori(0, n // 2 - 1) as i:
        step(i * 2 + 2, i * 2 + 1, i * 2, 0)
        step(i * 2 + 3, i * 2 + 2, i * 2 + 1, 1)
    step(None, n - 1, n - 2, 0)
    step(None, None, n - 1, 1)


def product_key_phase(nc, pool, c, w):
    HR, NK, TOP = 4, 64, 8
    NE = 1024
    NA = NE // NK
    FC = NE // P
    with Phase(nc, pool) as ph:
        wq = ph.sb("wq", [P, KD, 4 * P])
        kbd = ph.sb("kbd", [P, 4, P])
        wg = ph.sb("wg", [P, KD, NE])
        wu = ph.sb("wu", [P, KD, NE])
        wd = ph.sb("wd", [P, FC, D])
        down = ph.sb("down", [P, KD, NE])
        up = ph.sb("up", [P, FC, D])
        bg = ph.sb("bg", [P, FC])
        bu = ph.sb("bu", [P, FC])
        bd = ph.sb("bd", [P, D])
        xs = ph.sb("xs", [P, 2, 2, D])
        xT = ph.sb("xT", [P, 2, 2, KD, P])
        qT = ph.sb("qT", [P, 4 * P])
        sim = ph.sb("sim", [P, 2, HR, NK])
        s8 = ph.sb("s8", [P, 2, HR, TOP])
        top = ph.sb("top", [P, HR])
        s8x = ph.sb("s8x", [P, HR, TOP])
        simx = ph.sb("simx", [P, HR, NA])
        cand = ph.sb("cand", [P, HR, TOP, TOP])
        t8 = ph.sb("t8", [P, 2, HR, TOP])
        e8 = ph.sb("e8", [P, 2, HR, TOP])
        ss = ph.sb("ss", [P, 2, HR, NE])
        es = ph.sb("es", [P, 2, HR, NE])
        sum8 = ph.sb("sum8", [P, HR])
        rinv = ph.sb("rinv", [P, HR])
        kept = ph.sb("kept", [P, NE])
        inside = ph.sb("inside", [P, HR])
        rest = ph.sb("rest", [P, HR])
        rest1 = ph.sb("rest1", [P, 1])
        co = ph.sb("co", [P, 2, NE])
        sw = ph.sb("sw", [P, NE])
        gm = ph.sb("gm", [P, NE])
        gT = ph.sb("gT", [P, NE])
        sg = ph.sb("sg", [P, NE])
        hT = ph.sb("hT", [P, NE])
        yb = ph.sb("yb", [P, D])
        ps_x = ph.ps("ps_x", [P, 2, KD, P])
        ps_q = ph.ps("ps_q", [P, BANK])
        ps_s = ph.ps("ps_s", [P, BANK])
        ps_w = ph.ps("ps_w", [P, 2 * BANK])
        ps_gu = ph.ps("ps_gu", [P, 2, BANK])
        ps_y = ph.ps("ps_y", [P, BANK])

        weights, zeroed = ph.sem(), ph.sem()
        gp_x = ph.steps("x")
        pe_x = ph.steps("xT")
        act_x = ph.steps("xT")
        pe_a = ph.steps("q sim")
        act_a = ph.steps("qT e8 es")
        dve_a = ph.steps("sim ready s8 top s8x simx cand ready2 t8")
        gp_a = ph.steps("ss")
        dve_m = ph.steps("sum8 rinv " + " ".join(f"wait{h} kept{h} co{h}" for h in range(HR)) + " rest restr rest1 co")
        pe_b = ph.steps("w gu0 gu1 gu2 gu3 gT y")
        act_b = ph.steps("sw sg0 sg1 sg2 sg3 gT")
        dve_b = ph.steps("gm h0 h1 h2 h3 gT yb x")
        block = ph.stack.enter_context(nc.Block())
        loads = [(wq[:], w["Wq"].rearrange("(k p) n -> p k n", p=P)), (wg[:], w["Wg"].rearrange("(k p) n -> p k n", p=P)),
                 (wu[:], w["Wu"].rearrange("(k p) n -> p k n", p=P)), (wd[:], w["Wd"].rearrange("(k p) n -> p k n", p=P)),
                 (down[:], w["downT"].rearrange("(k p) n -> p k n", p=P)), (up[:], w["up"].rearrange("(k p) n -> p k n", p=P)),
                 (bg[:], w["bgT"]), (bu[:], w["buT"]), (bd[:], row(w["bd"], D))]
        for q in range(2):
            for h in range(HR):
                half = slice((h % 2) * NK, (h % 2 + 1) * NK)
                loads.append((kbd[half, q * 2 + h // 2, half], w["keysT"][q, h]))
        n_loads = 16 * len(loads)

        def number(ta, tb):
            return ta if ta is not None else tb + 2

        @block.sync
        def _(sp):
            sp.wait_ge(zeroed, 1)
            for dst, src in loads:
                sp.dma_start(dst, src).then_inc(weights, 16)
            sp.wait_ge(weights, n_loads)

        @block.gpsimd
        def _(gp):
            gp_x.open(gp)
            gp_a.open(gp)
            gp.memset(kbd[:], 0.0).then_inc(zeroed, 1)

            def step(ta, tm, tb, u):
                if ta is not None or tb is not None:
                    s = number(ta, tb)
                    gp.wait_ge(pe_x.sem, pe_x.after("xT", s - 2))
                    for k, t in enumerate((ta, tb)):
                        if t is not None:
                            ins = gp.tensor_copy(xs[:, u, k, :], c["cur"][:, bass.ds(t, 1), :].rearrange("p a d -> p (a d)"))
                    ins.then_inc(gp_x.sem, 1)
                if ta is not None:
                    gp.wait_ge(dve_a.sem, dve_a.after("simx", ta))
                    gp.wait_ge(dve_m.sem, dve_m.after(f"kept{HR - 1}", ta - 2))
                    gp.wait_ge(act_a.sem, act_a.after("es", ta - 2))
                    gp.tensor_tensor(ss[:, u].rearrange("p h (a b) -> p h a b", b=NK),
                                     simx[:].unsqueeze(3).to_broadcast([P, HR, NA, NK]),
                                     sim[:, 1].unsqueeze(2).to_broadcast([P, HR, NA, NK]), ALU.add).then_inc(gp_a.sem, 1)

            woven(gp, NT, step)

        @block.tensor
        def _(pe):
            for s in (pe_x, pe_a, pe_b):
                s.open(pe)
            pe.wait_ge(weights, n_loads)

            def step(ta, tm, tb, u):
                if ta is not None or tb is not None:
                    s = number(ta, tb)
                    pe.wait_ge(gp_x.sem, gp_x.after("x", s))
                    pe.wait_ge(act_x.sem, act_x.after("xT", s - 1))
                    for j, t in enumerate((ta, tb)):
                        if t is not None:
                            for k in range(KD):
                                ins = pe.transpose(ps_x[:, j, k, :], xs[:, u, j, k * P:(k + 1) * P], c["ident"][:])
                    ins.then_inc(pe_x.sem, 1)
                    pe.wait_ge(act_x.sem, act_x.after("xT", s))
                if ta is not None:
                    pe.wait_ge(act_a.sem, act_a.after("qT", ta - 1))
                    for m in range(4):
                        for k in range(KD):
                            ins = pe.matmul(ps_q[:, m * P:(m + 1) * P], wq[:, k, m * P:(m + 1) * P], xT[:, u, 0, k, :],
                                            start=(k == 0), stop=(k == KD - 1))
                    ins.then_inc(pe_a.sem, 1)
                if tb is not None:
                    pe.wait_ge(act_b.sem, act_b.after("gT", tb - 1))
                    pe.wait_ge(dve_b.sem, dve_b.after("gT", tb - 1))
                    for lo in range(0, NE, BANK):
                        for k in range(KD):
                            ins = pe.matmul(ps_w[:, lo:lo + BANK], xT[:, u, 1, k, :], down[:, k, lo:lo + BANK],
                                            start=(k == 0), stop=(k == KD - 1))
                    ins.then_inc(pe_b.sem, 1)
                if ta is not None:
                    pe.wait_ge(act_a.sem, act_a.after("qT", ta))
                    pe.wait_ge(dve_a.sem, dve_a.after("sim", ta - 1))
                    for m in range(4):
                        ins = pe.matmul(ps_s[:, m * P:(m + 1) * P], qT[:, m * P:(m + 1) * P], kbd[:, m, :], start=True, stop=True)
                    ins.then_inc(pe_a.sem, 1)
                if tb is not None:
                    for q in range(4):
                        if q < 2:
                            pe.wait_ge(dve_b.sem, dve_b.after(f"h{q + 2}", tb - 1))
                        else:
                            pe.wait_ge(dve_b.sem, dve_b.after(f"h{q - 2}", tb))
                        for j, ww in enumerate((wg, wu)):
                            for f in range(2):
                                fc = 2 * q + f
                                for k in range(KD):
                                    ins = pe.matmul(ps_gu[:, q % 2, (2 * j + f) * P:(2 * j + f + 1) * P],
                                                    ww[:, k, fc * P:(fc + 1) * P], xT[:, u, 1, k, :], start=(k == 0),
                                                    stop=(k == KD - 1))
                        ins.then_inc(pe_b.sem, 1)
                    pe.wait_ge(dve_b.sem, dve_b.after("gm", tb))
                    for k in range(FC):
                        ins = pe.transpose(ps_w[:, k * P:(k + 1) * P], gm[:, k * P:(k + 1) * P], c["ident"][:])
                    ins.then_inc(pe_b.sem, 1)
                    pe.wait_ge(dve_b.sem, dve_b.after("h3", tb))
                    pe.wait_ge(dve_b.sem, dve_b.after("yb", tb - 1))
                    for k in range(FC):
                        pe.matmul(ps_y[:, 0:D], hT[:, k * P:(k + 1) * P], wd[:, k, :], start=(k == 0), stop=False)
                    pe.wait_ge(act_b.sem, act_b.after("gT", tb))
                    pe.wait_ge(dve_b.sem, dve_b.after("gT", tb))
                    for k in range(FC):
                        ins = pe.matmul(ps_y[:, 0:D], gT[:, k * P:(k + 1) * P], up[:, k, :], start=False, stop=(k == FC - 1))
                    ins.then_inc(pe_b.sem, 1)

            woven(pe, NT, step)

        @block.scalar
        def _(act):
            for s in (act_x, act_a, act_b):
                s.open(act)
            act.wait_ge(weights, n_loads)

            def step(ta, tm, tb, u):
                if ta is not None or tb is not None:
                    s = number(ta, tb)
                    act.wait_ge(pe_x.sem, pe_x.after("xT", s))
                    js = [j for j, t in enumerate((ta, tb)) if t is not None]
                    lo, hi = js[0], js[-1] + 1
                    act.activation(xT[:, u, lo:hi].rearrange("p j k n -> p (j k n)"),
                                   ps_x[:, lo:hi].rearrange("p j k n -> p (j k n)"), ACT.Copy).then_inc(act_x.sem, 1)
                if ta is not None:
                    act.wait_ge(pe_a.sem, pe_a.after("q", ta))
                    act.wait_ge(pe_a.sem, pe_a.after("sim", ta - 1))
                    act.activation(qT[:], ps_q[:], ACT.Copy).then_inc(act_a.sem, 1)
                if tb is not None:
                    act.wait_ge(pe_b.sem, pe_b.after("w", tb))
                    act.wait_ge(dve_b.sem, dve_b.after("gm", tb - 1))
                    act.activation(sw[:], ps_w[:], ACT.Silu).then_inc(act_b.sem, 1)
                    for q in range(4):
                        act.wait_ge(pe_b.sem, pe_b.after(f"gu{q}", tb))
                        act.wait_ge(dve_b.sem, dve_b.after(f"h{q}", tb - 1))
                        for f in range(2):
                            fc = 2 * q + f
                            ins = act.activation(sg[:, fc * P:(fc + 1) * P], ps_gu[:, q % 2, f * P:(f + 1) * P], ACT.Silu,
                                                 bias=bg[:, fc:fc + 1])
                        ins.then_inc(act_b.sem, 1)
                    act.wait_ge(pe_b.sem, pe_b.after("gT", tb))
                    act.wait_ge(pe_b.sem, pe_b.after("y", tb - 1))
                    act.activation(gT[:, 0:BANK], ps_w[:, 0:BANK], ACT.Copy).then_inc(act_b.sem, 1)
                if ta is not None:
                    act.wait_ge(dve_a.sem, dve_a.after("t8", ta))
                    act.wait_ge(dve_m.sem, dve_m.after("sum8", ta - 2))
                    act.activation(e8[:, u], t8[:, u], ACT.Exp).then_inc(act_a.sem, 1)
                    act.wait_ge(gp_a.sem, gp_a.after("ss", ta))
                    act.wait_ge(dve_m.sem, dve_m.after(f"kept{HR - 1}", ta - 2))
                    act.activation(es[:, u], ss[:, u], ACT.Exp).then_inc(act_a.sem, 1)

            woven(act, NT, step)

        @block.vector
        def _(dve):
            for s in (dve_a, dve_m, dve_b):
                s.open(dve)
            dve.wait_ge(weights, n_loads)

            def search(t, u):
                def own(name):
                    dve.wait_ge(dve_a.sem, dve_a.after(name, t))

                dve.wait_ge(pe_a.sem, pe_a.after("sim", t))
                dve.wait_ge(gp_a.sem, gp_a.after("ss", t - 1))
                dve.tensor_copy(sim[:].rearrange("p q h n -> p (q h n)"), ps_s[:]).then_inc(dve_a.sem, 1)
                own("sim")
                dve.sem_inc(dve_a.sem, 1)
                for q in range(2):
                    for h in range(HR):
                        ins = dve.max(s8[:, q, h, :], sim[:, q, h, :])
                ins.then_inc(dve_a.sem, 1)
                own("s8")
                dve.tensor_tensor(top[:], s8[:, 0, :, 0], s8[:, 1, :, 0], ALU.add).then_inc(dve_a.sem, 1)
                own("top")
                dve.tensor_tensor(s8x[:], s8[:, 0], bc(top[:], [P, HR, TOP]), ALU.subtract).then_inc(dve_a.sem, 1)
                dve.tensor_tensor(simx[:], sim[:, 0, :, 0:NA], bc(top[:], [P, HR, NA]), ALU.subtract).then_inc(dve_a.sem, 1)
                own("s8x")
                dve.tensor_tensor(cand[:], s8x[:].unsqueeze(3).to_broadcast([P, HR, TOP, TOP]),
                                  s8[:, 1].unsqueeze(2).to_broadcast([P, HR, TOP, TOP]), ALU.add).then_inc(dve_a.sem, 1)
                own("cand")
                dve.sem_inc(dve_a.sem, 1)
                for h in range(HR):
                    ins = dve.max(t8[:, u, h, :], cand[:, h].rearrange("p a b -> p (a b)"))
                ins.then_inc(dve_a.sem, 1)

            def coefficients(t, u, h):
                def own(name):
                    dve.wait_ge(dve_m.sem, dve_m.after(name, t))

                if h == 0:
                    dve.wait_ge(act_a.sem, act_a.after("es", t))
                    dve.tensor_reduce(sum8[:], e8[:, u], AX, ALU.add).then_inc(dve_m.sem, 1)
                    own("sum8")
                    dve.reciprocal(rinv[:], sum8[:]).then_inc(dve_m.sem, 1)
                    own("rinv")
                else:
                    own(f"co{h - 1}")
                dve.sem_inc(dve_m.sem, 1)
                dve.scalar_tensor_tensor(kept[:], ss[:, u, h], t8[:, u, h, TOP - 1:TOP], es[:, u, h], ALU.is_ge, ALU.mult,
                                         accum_out=inside[:, h:h + 1]).then_inc(dve_m.sem, 1)
                own(f"kept{h}")
                if h == 0:
                    dve.tensor_scalar(co[:, u], kept[:], rinv[:, 0:1], None, ALU.mult).then_inc(dve_m.sem, 1)
                else:
                    dve.scalar_tensor_tensor(co[:, u], kept[:], rinv[:, h:h + 1], co[:, u], ALU.mult, ALU.add).then_inc(dve_m.sem, 1)
                if h == HR - 1:
                    dve.tensor_tensor(rest[:], sum8[:], inside[:], ALU.subtract).then_inc(dve_m.sem, 1)
                    own("rest")
                    dve.tensor_tensor(rest[:], rest[:], rinv[:], ALU.mult).then_inc(dve_m.sem, 1)
                    own("restr")
                    dve.tensor_reduce(rest1[:], rest[:], AX, ALU.add).then_inc(dve_m.sem, 1)
                    own("rest1")
                    dve.tensor_tensor(co[:, u, NE - 1:NE], co[:, u, NE - 1:NE], rest1[:], ALU.add).then_inc(dve_m.sem, 1)

            def hidden(t, u, q):
                dve.wait_ge(act_b.sem, act_b.after(f"sg{q}", t))
                if q == 0:
                    dve.wait_ge(pe_b.sem, pe_b.after("y", t - 1))
                for f in range(2):
                    fc = 2 * q + f
                    ins = dve.scalar_tensor_tensor(hT[:, fc * P:(fc + 1) * P], ps_gu[:, q % 2, (2 + f) * P:(3 + f) * P],
                                                   bu[:, fc:fc + 1], sg[:, fc * P:(fc + 1) * P], ALU.add, ALU.mult)
                ins.then_inc(dve_b.sem, 1)

            def step(ta, tm, tb, u):
                if ta is not None:
                    search(ta, u)
                if tb is not None:
                    dve.wait_ge(act_b.sem, act_b.after("sw", tb))
                    dve.wait_ge(dve_m.sem, dve_m.after("co", tb))
                    dve.wait_ge(pe_b.sem, pe_b.after("gT", tb - 1))
                    dve.tensor_tensor(gm[:], sw[:], co[:, u], ALU.mult).then_inc(dve_b.sem, 1)
                for q in range(4):
                    if tb is not None:
                        hidden(tb, u, q)
                    if tm is not None:
                        coefficients(tm, 1 - u, q)
                if tb is not None:
                    x_t = c["x"][:, bass.ds(tb, 1), :].rearrange("p a d -> p (a d)")
                    dve.wait_ge(pe_b.sem, pe_b.after("gT", tb))
                    dve.tensor_copy(gT[:, BANK:], ps_w[:, BANK:]).then_inc(dve_b.sem, 1)
                    dve.wait_ge(pe_b.sem, pe_b.after("y", tb))
                    dve.tensor_tensor(yb[:], ps_y[:, 0:D], bd[:], ALU.add).then_inc(dve_b.sem, 1)
                    dve.wait_ge(dve_b.sem, dve_b.after("yb", tb))
                    dve.tensor_tensor(x_t, x_t, yb[:], ALU.add).then_inc(dve_b.sem, 1)

            woven(dve, NT, step)


def routing(nc, ctx, layer):
    def sb(name, shape, dt=F32):
        return ctx.enter_context(nc.sbuf_tensor(f"{name}_{layer}", shape, dt))

    return {"logits": sb("logits", [P, NT, 16]), "wt": sb("wt", [P, 2, NT]), "slot": sb("slot", [P, 2, NT], U32),
            "slot_out": sb("slot_out", [P, 2, NT], U32), "tile_expert": sb("tile_expert", [P, N_SLOT_TILES[2]], I32),
            "acc": sb("acc", [P, NT, D])}


def clear_slots(nc, pool, xs_dram, n):
    with Phase(nc, pool) as ph:
        zero = ph.sb("zero", [P, D])
        zeroed, stored = ph.sem(), ph.sem()
        block = ph.stack.enter_context(nc.Block())

        @block.vector
        def _(dve):
            dve.memset(zero[:], 0.0).then_inc(zeroed, 1)

        @block.sync
        def _(sp):
            sp.wait_ge(zeroed, 1)
            sp.dma_start(xs_dram.rearrange("(t p) d -> p t d", p=P),
                         zero[:].unsqueeze(1).to_broadcast([P, n, D])).then_inc(stored, 16)
            sp.wait_ge(stored, 16)


def attention_store(nc, ctx, layer):
    def sb(name, shape, dt=F32):
        return ctx.enter_context(nc.sbuf_tensor(f"{name}_{layer}", shape, dt))

    return {
        "qo": sb("qo", [P, NT, NP, P]), "kT": sb("kT", [P, T]), "v": sb("v", [P, NT, DH]),
        "nk": sb("nk", [P, DH]), "nsn": sb("nsn", [P, NT, H]), "nv": sb("nv", [P, DH]), "km": sb("km", [P, B, S], BF16),
        "dm": sb("dm", [P, B * S], BF16),
    }


def constants(nc, ctx):
    def sb(name, shape, dt=F32):
        return ctx.enter_context(nc.sbuf_tensor(name, shape, dt))

    return {"x": sb("x_sb", [P, NT, D]), "cur": sb("cur_sb", [P, NT, D]), "ident": sb("ident_sb", [P, P]),
            "ident16": sb("ident16", [P, P], BF16), "ones": sb("ones_sb", [P, P]), "eps": sb("eps_sb", [P, 2])}


N_PHASE_SEMS = 40


def semaphore_pool(nc):
    sems = [nc.alloc_semaphore(f"phase{i}") for i in range(N_PHASE_SEMS)]
    return {"sems": sems, "n": 0, "first": sems[0].num}


def store_x(nc, pool, c, out):
    with Phase(nc, pool) as ph:
        stored = ph.sem()
        block = ph.stack.enter_context(nc.Block())

        @block.sync
        def _(sp):
            sp.dma_start(out.rearrange("b (t p) d -> p (b t) d", p=P), c["x"][:]).then_inc(stored, 16)
            sp.wait_ge(stored, 16)


def build(nc, a, out):
    with ExitStack() as ctx:
        rows_moved = {"sem": nc.alloc_semaphore("rows_moved"), "count": 0}
        bias_spread = nc.alloc_semaphore("bias_spread")
        pool = semaphore_pool(nc)
        c = constants(nc, ctx)
        n_rows = N_SLOT_TILES[2] * P
        xs_dram = nc.dram_tensor("slot_rows", (n_rows, D), F32, kind="Internal").ap()
        ys_dram = nc.dram_tensor("slot_outputs", (n_rows, D), F32, kind="Internal").ap()
        table_dram = nc.dram_tensor("bias_table", (H, S + P), F32, kind="Internal").ap()
        spread_dram = nc.dram_tensor("bias_by_partition", (H, P, S), F32, kind="Internal").ap()

        setup(nc, pool, c, a["x"])
        clear_slots(nc, pool, xs_dram, N_SLOT_TILES[2])
        bias_table_phase(nc, pool, c, {n: a["L2_cond_" + n] for n in ("w0", "b0", "g0", "w1", "b1", "g1", "w2", "b2")},
                         table_dram, spread_dram, bias_spread)

        def given_bias(h, qt):
            return a["fside_16xSxS_0"][bass.ds(h, 1), qt * P:(qt + 1) * P, 0:(qt + 1) * P].rearrange("a p j -> p (a j)")

        def relative_bias(h, qt):
            first = S - (qt + 1) * P
            return spread_dram[bass.ds(h, 1), :, first:S].rearrange("a p j -> p (a j)")

        def cond_moe(layer):
            w = {n: a[f"L{layer}_cond_" + n] for n in ("wt", "wg", "w_gate", "w_up", "w_down", "sw_gate", "sw_up", "sw_down")}
            logits_phase(nc, pool, c, r, c["x"], w["wt"], None, cond=(a["cond_64"], w["wg"]), halve=True,
                         shared=(w["sw_gate"], w["sw_up"], w["sw_down"]))
            choose_phase(nc, pool, c, r, 8, 2, c["x"], xs_dram, dma_done=rows_moved)
            glu_experts_phase(nc, pool, c, r, N_SLOT_TILES[2], w["w_gate"], w["w_up"], w["w_down"], xs_dram, ys_dram)
            combine_phase(nc, pool, c, r, 2, ys_dram, n_rows, c["cur"], base=r["acc"], dma_done=rows_moved)

        with ExitStack() as actx:
            att = attention_store(nc, actx, 0)
            null_phase(nc, pool, c, att, a["cond_64"], a["mask_BxS_bk0"])
            qkv_phase(nc, pool, c, att, a["L0_cond_g_in"], a["L0_cond_Wq"], a["L0_cond_Wkv"], a["L0_cond_null_attn_bias"])
            core_phase(nc, pool, c, att, given_bias)
            out_phase(nc, pool, c, att, a["L0_cond_Wo"], a["L0_cond_g_out"])
        with ExitStack() as rctx:
            r = routing(nc, rctx, 0)
            logits_phase(nc, pool, c, r, c["cur"], a["L0_ffn_Wg"], a["L0_ffn_bg"])
            choose_phase(nc, pool, c, r, 16, 1, c["cur"], xs_dram, capacity=T // 16, dma_done=rows_moved)
            mlp_experts_phase(nc, pool, c, r, 16, False, ACT.Relu, a["L0_ffn_W1"], a["L0_ffn_b1"], a["L0_ffn_W2"],
                              a["L0_ffn_b2"], xs_dram, ys_dram)
            combine_phase(nc, pool, c, r, 1, ys_dram, 16 * P, c["x"], base=c["x"], dma_done=rows_moved)

            cond_moe(1)
            logits_phase(nc, pool, c, r, c["cur"], a["L1_ffn_router_w"], None)
            choose_phase(nc, pool, c, r, 8, 2, c["cur"], xs_dram, softmax_all=False, dma_done=rows_moved)
            mlp_experts_phase(nc, pool, c, r, N_SLOT_TILES[2], True, ACT.Gelu, a["L1_ffn_w1"], a["L1_ffn_b1"],
                              a["L1_ffn_w2"], a["L1_ffn_b2"], xs_dram, ys_dram)
            combine_phase(nc, pool, c, r, 2, ys_dram, n_rows, c["x"], base=c["x"], dma_done=rows_moved)

        with ExitStack() as actx:
            att = attention_store(nc, actx, 2)
            null_phase(nc, pool, c, att, a["cond_64"], a["mask_BxS_bf1"], k_scale=a["L2_cond_k_scale"])
            qkv_phase(nc, pool, c, att, a["L2_cond_g_norm"], a["L2_cond_Wq"], a["L2_cond_Wkv"],
                      a["L2_cond_null_attn_bias"], q_scale=a["L2_cond_q_scale"], k_scale=a["L2_cond_k_scale"])
            core_phase(nc, pool, c, att, relative_bias, bias_made=bias_spread)
            out_phase(nc, pool, c, att, a["L2_cond_Wout"], a["L2_cond_g_out"])
        product_key_phase(nc, pool, c, {
            "Wq": a["L2_ffn_Wq"], "Wg": a["L2_ffn_Wg"], "Wu": a["L2_ffn_Wu"], "Wd": a["L2_ffn_Wd"],
            "downT": a["L2_ffn_down_embed"], "up": a["L2_ffn_up_embed"], "bgT": a["L2_ffn_bg"], "buT": a["L2_ffn_bu"],
            "bd": a["L2_ffn_bd"], "keysT": a["L2_ffn_keys"]})

        with ExitStack() as rctx:
            r = routing(nc, rctx, 3)
            cond_moe(3)
            logits_phase(nc, pool, c, r, c["cur"], a["L3_ffn_gate_w"], None, rms=a["L3_ffn_rms_w"])
            choose_phase(nc, pool, c, r, 8, 1, c["cur"], xs_dram, dma_done=rows_moved)
            mlp_experts_phase(nc, pool, c, r, N_SLOT_TILES[1], True, ACT.Silu, a["L3_ffn_W1"], a["L3_ffn_b1"],
                              a["L3_ffn_W2"], a["L3_ffn_b2"], xs_dram, ys_dram)
            combine_phase(nc, pool, c, r, 1, ys_dram, N_SLOT_TILES[1] * P, c["x"], base=c["x"], dma_done=rows_moved)
        store_x(nc, pool, c, out)


def _transposed(*axes):
    return lambda v: v.transpose(*axes)


def _by_partition(v):
    w = v.reshape(*v.shape[:-1], -1, P)
    return w.swapaxes(-1, -2)


_LAYOUT = {
    "L0_ffn_b1": _by_partition, "L1_ffn_b1": _by_partition, "L3_ffn_b1": _by_partition,
    "L1_cond_wt": _transposed(1, 0), "L1_cond_wg": _transposed(1, 0), "L3_cond_wt": _transposed(1, 0),
    "L3_cond_wg": _transposed(1, 0), "L1_ffn_router_w": _transposed(1, 0), "L3_ffn_gate_w": _transposed(1, 0),
    "L1_ffn_w1": _transposed(0, 2, 1), "L1_ffn_w2": _transposed(0, 2, 1),
    "L2_ffn_down_embed": _transposed(1, 0), "L2_ffn_bg": _by_partition, "L2_ffn_bu": _by_partition,
    "L2_ffn_keys": _transposed(2, 0, 3, 1),
}


def kernel(**inputs):
    import numpy as _np
    import concourse.bacc as _bacc
    from concourse import mybir as _mybir
    from concourse.bass_utils import run_bass_kernel_spmd as _run

    nc = _bacc.Bacc("TRN2", target_bir_lowering=False, num_devices=1)
    arrays, args = {}, {}
    for name, value in inputs.items():
        v = _np.asarray(value)
        v = _np.ascontiguousarray(_LAYOUT[name](v) if name in _LAYOUT else v)
        arrays[f"in_{name}_dram"] = v
        args[name] = nc.dram_tensor(f"in_{name}_dram", v.shape, _mybir.dt.from_np(v.dtype), kind="ExternalInput").ap()
    out = nc.dram_tensor("out_dram", (B, S, D), _mybir.dt.float32, kind="ExternalOutput").ap()
    build(nc, args, out)
    return _run(nc, [arrays], core_ids=[0]).results[0]["out_dram"]
```

```python
from contextlib import ExitStack

import concourse.bass as bass
from concourse import mybir

F32 = mybir.dt.float32
F32R = mybir.dt.float32r
BF16 = mybir.dt.bfloat16
U8 = mybir.dt.uint8
I32 = mybir.dt.int32
U32 = mybir.dt.uint32
ALU = mybir.AluOpType
ACT = mybir.ActivationFunctionType
AX = mybir.AxisListType.X

P = 128
B, S, D = 2, 1024, 256
T = B * S
NT = T // P
TB = S // P
KD = D // P
H, DH = 16, 64
NP = H // 2
INNER = H * DH
LN_EPS = 1e-5
RMS_EPS = 1e-6
NORM_FLOOR = 1e-12
MASKED = -1e38
BANK = 512


class Steps:

    def __init__(self, sem, names, ahead=4):
        self.sem, self.names, self.ahead = sem, names.split(), ahead

    def open(self, eng):
        eng.sem_inc(self.sem, self.ahead * len(self.names))

    def after(self, name, t):
        return (t + self.ahead) * len(self.names) + self.names.index(name) + 1


class Phase:

    def __init__(self, nc, pool):
        self.nc, self.pool, self.used, self.stack = nc, pool, 0, ExitStack()

    def __enter__(self):
        return self

    def sb(self, name, shape, dt=F32):
        return self.stack.enter_context(self.nc.sbuf_tensor(self.name(name), shape, dt))

    def ps(self, name, shape, dt=F32):
        return self.stack.enter_context(self.nc.psum_tensor(self.name(name), shape, dt))

    def name(self, name):
        self.pool["n"] += 1
        return f"{name}_{self.pool['n']}"

    def sem(self):
        self.used += 1
        return self.pool["sems"][self.used - 1]

    def steps(self, names, ahead=4):
        return Steps(self.sem(), names, ahead)

    def __exit__(self, kind, value, tb):
        self.stack.close()
        if kind is None:
            first = self.pool["first"]
            self.nc.all_engine_barrier(sems_to_clear=range(first, first + self.used))
        return False


def tiles(eng, n, body):
    with eng.Fori(0, n // 2) as i:
        body(i * 2, 0)
        body(i * 2 + 1, 1)


def skewed(eng, n, a, b, b_first=False):

    def pair(i, j):
        steps = [lambda: a(i, (j + 1) % 2), lambda: b(i - 1, j % 2)]
        for step in reversed(steps) if b_first else steps:
            step()

    a(0, 0)
    if n > 2:
        with eng.Fori(0, n // 2 - 1) as i:
            pair(i * 2 + 1, 0)
            pair(i * 2 + 2, 1)
    pair(n - 1, 0)
    b(n - 1, 1)


def pipeline(eng, n, unroll, *stages):
    for t in range(unroll):
        for lag, fn in stages:
            if t >= lag:
                fn(t - lag, t - lag)
    if n > unroll:
        with eng.Fori(1, n // unroll) as i:
            for v in range(unroll):
                for lag, fn in stages:
                    fn(i * unroll + (v - lag), (v - lag) % unroll)
    for t in range(n, n + max(lag for lag, _ in stages)):
        for lag, fn in stages:
            if t - lag < n:
                fn(t - lag, (t - lag) % unroll)


def row(ap, width, offset=0):
    return bass.AP(ap.tensor, ap.offset + offset, [[0, P], [1, width]])


def bc(ap, shape):
    return ap.unsqueeze(2).to_broadcast(shape)


def setup(nc, pool, c, x_in):
    with Phase(nc, pool) as ph:
        loaded, zeroed = ph.sem(), ph.sem()
        made = ph.sem()
        block = ph.stack.enter_context(nc.Block())

        @block.sync
        def _(sp):
            sp.dma_start(c["x"][:], x_in.rearrange("b (t p) d -> p (b t) d", p=P)).then_inc(loaded, 16)
            sp.wait_ge(loaded, 16)

        @block.gpsimd
        def _(pool_eng):
            pool_eng.memset(c["ident"][:], 0.0).then_inc(zeroed, 1)
            pool_eng.memset(c["ones"][:], 1.0).then_inc(zeroed, 1)
            pool_eng.memset(c["eps"][:, 0:1], LN_EPS).then_inc(zeroed, 1)
            pool_eng.memset(c["eps"][:, 1:2], RMS_EPS).then_inc(zeroed, 1)
            pool_eng.wait_ge(zeroed, 4)
            pool_eng.affine_select(out=c["ident"][:], in_=c["ident"][:], compare_op=ALU.not_equal, fill=1.0,
                                   base=0, pattern=[[-1, P]], channel_multiplier=1).then_inc(made, 1)
            pool_eng.wait_ge(made, 1)
            pool_eng.tensor_copy(c["ident16"][:], c["ident"][:]).then_inc(made, 1)


def qkv_phase(nc, pool, c, att, g, wq, wkv, null_bias, q_scale=None, k_scale=None):
    normal = q_scale is not None
    HN = H + 1
    QK = INNER + DH
    V, NULL, ALL = QK, QK + DH, QK + DH + H
    banks = ((0, BANK), (BANK, 2 * BANK), (2 * BANK, ALL))
    with Phase(nc, pool) as ph:
        w = ph.sb("w", [P, KD, NULL])
        wf = ph.sb("wf", [P, KD, ALL])
        gcol = ph.sb("gcol", [P, KD])
        ktab = ph.sb("ktab", [P, 4, DH])
        wnk = ph.sb("wnk", [P, KD, INNER])
        wnull = ph.sb("wnull", [P, KD, H])
        nb_row = ph.sb("nb_row", [P, H])
        stats = ph.sb("stats", [P, 4, 6])
        mv = ph.sb("mv", [P, 4, 2])
        sd = ph.sb("sd", [P, 4, 1])
        rstd = ph.sb("rstd", [P, 4, 1])
        xn = ph.sb("xn", [P, 2, D])
        xnT = ph.sb("xnT", [P, 2, KD, P])
        raw = ph.sb("raw", [P, 4, ALL])
        kk = ph.sb("kk", [P, 2, 2, DH])
        if normal:
            sq = ph.sb("sq", [P, 2, QK])
            qn = ph.sb("qn", [P, 2, INNER])
            n2 = ph.sb("n2", [P, HN])
            nr = ph.sb("nr", [P, HN])
            nf = ph.sb("nf", [P, HN])
            rn = ph.sb("rn", [P, 2, HN])
            nulln = ph.sb("nulln", [P, H])
        ps_x = ph.ps("ps_x", [P, 2, BANK])
        ps_q = ph.ps("ps_q", [P, 3 * BANK])
        ps_t = ph.ps("ps_t", [P, 3 * BANK])

        weights, tabled, folded = ph.sem(), ph.sem(), ph.sem()
        dve_0 = ph.steps("stats waited moments")
        act_0 = ph.steps("sd")
        dve_1 = ph.steps("rstd xn")
        pe_x = ph.steps("xT")
        act_x = ph.steps("xnT")
        pe_q = ph.steps("b0 b1 b2")
        act_r = ph.steps("b0 v")
        dve_r = ph.steps("b1 b2")
        act_s = ph.steps("sq")
        dve_n = ph.steps("sumsq floor rn")
        act_n = ph.steps("norm")
        gp_q = ph.steps("qn")
        dve_k = ph.steps("nulln k kdup null")
        pe_t = ph.steps("qT")
        act_t = ph.steps("qT")
        dve_t = ph.steps("khi klo")
        block = ph.stack.enter_context(nc.Block())

        loads = [(w[:, :, 0:INNER], wq.rearrange("(k p) n -> p k n", p=P)),
                 (w[:, :, INNER:], wkv.rearrange("(k p) n -> p k n", p=P)),
                 (gcol[:], g), (nb_row[:], row(null_bias, H))]
        if normal:
            loads += [(ktab[:, 0, :], row(q_scale, DH)), (ktab[:, 3, :], row(k_scale, DH))]

        @block.sync
        def _(sp):
            for dst, src in loads:
                sp.dma_start(dst, src).then_inc(weights, 16)

        @block.tensor
        def _(pe):
            for s in (pe_x, pe_q, pe_t):
                s.open(pe)
            pe.wait_ge(folded, 2 * KD)

            def transpose_x(t, u):
                pe.wait_ge(dve_1.sem, dve_1.after("xn", t))
                pe.wait_ge(act_x.sem, act_x.after("xnT", t - 2))
                for k in range(KD):
                    ins = pe.transpose(ps_x[:, u % 2, k * P:(k + 1) * P], xn[:, u % 2, k * P:(k + 1) * P], c["ident"][:])
                ins.then_inc(pe_x.sem, 1)

            def products(t, u):
                pe.wait_ge(act_x.sem, act_x.after("xnT", t))
                for m, (lo, hi) in enumerate(banks):
                    if m == 0:
                        pe.wait_ge(act_r.sem, act_r.after("b0", t - 1))
                    else:
                        pe.wait_ge(dve_r.sem, dve_r.after(f"b{m}", t - 1))
                    for k in range(KD):
                        ins = pe.matmul(ps_q[:, lo:hi], xnT[:, u % 2, k, :], wf[:, k, lo:hi], start=(k == 0),
                                        stop=(k == KD - 1))
                    ins.then_inc(pe_q.sem, 1)

            def transpose_qk(t, u):
                q_t = qn[:, u % 2] if normal else raw[:, u]
                if normal:
                    pe.wait_ge(gp_q.sem, gp_q.after("qn", t))
                pe.wait_ge(dve_k.sem, dve_k.after("kdup", t))
                pe.wait_ge(dve_t.sem, dve_t.after("klo", t - 1))
                pe.wait_ge(act_t.sem, act_t.after("qT", t - 1))
                for k in range(NP):
                    pe.transpose(ps_t[:, k * P:(k + 1) * P], q_t[:, k * P:(k + 1) * P], c["ident"][:])
                pe.transpose(ps_t[:, INNER:INNER + P], kk[:, u % 2].rearrange("p a n -> p (a n)"),
                             c["ident"][:]).then_inc(pe_t.sem, 1)

            pipeline(pe, NT, 4, (2, products), (4, transpose_qk), (1, transpose_x))

        @block.scalar
        def _(act):
            for s in (act_0, act_x, act_r, act_s, act_n, act_t):
                s.open(act)
            act.wait_ge(weights, 16 * len(loads))
            for k in range(KD):
                act.activation(wf[:, k, 0:NULL], w[:, k, :], ACT.Copy, scale=gcol[:, k:k + 1]).then_inc(folded, 1)

            def root(t, u):
                act.wait_ge(dve_0.sem, dve_0.after("moments", t))
                act.wait_ge(dve_1.sem, dve_1.after("rstd", t - 4))
                act.activation(sd[:, u, :], mv[:, u, 1:2], ACT.Sqrt, bias=c["eps"][:, 0:1]).then_inc(act_0.sem, 1)

            def transposed_x(t, u):
                act.wait_ge(pe_x.sem, pe_x.after("xT", t))
                act.wait_ge(pe_q.sem, pe_q.after("b2", t - 2))
                act.activation(xnT[:, u % 2].rearrange("p k n -> p (k n)"), ps_x[:, u % 2, 0:D], ACT.Copy).then_inc(act_x.sem, 1)

            def results(t, u):
                act.wait_ge(pe_q.sem, pe_q.after("b0", t))
                act.wait_ge(pe_t.sem, pe_t.after("qT", t - 4))
                act.activation(raw[:, u, 0:BANK], ps_q[:, 0:BANK], ACT.Copy).then_inc(act_r.sem, 1)
                act.wait_ge(dve_r.sem, dve_r.after("b2", t))
                act.activation(att["v"][:, bass.ds(t, 1), :], raw[:, u, V:V + DH].unsqueeze(1), ACT.Copy).then_inc(act_r.sem, 1)
                if normal:
                    act.wait_ge(act_r.sem, act_r.after("b0", t))
                    act.wait_ge(dve_n.sem, dve_n.after("sumsq", t - 2))
                    act.activation(sq[:, u % 2], raw[:, u, 0:QK], ACT.Square).then_inc(act_s.sem, 1)

            def norms(t, u):
                act.wait_ge(dve_n.sem, dve_n.after("sumsq", t))
                act.wait_ge(dve_n.sem, dve_n.after("floor", t - 1))
                act.activation(nr[:], n2[:], ACT.Sqrt).then_inc(act_n.sem, 1)

            def transposed_q(t, u):
                act.wait_ge(pe_t.sem, pe_t.after("qT", t))
                act.activation(att["qo"][:, bass.ds(t, 1)].rearrange("p a q n -> p (a q n)"), ps_t[:, 0:INNER],
                               ACT.Copy).then_inc(act_t.sem, 1)

            stages = [(0, root), (2, results), (4, transposed_q), (1, transposed_x)]
            pipeline(act, NT, 4, *([(3, norms)] if normal else []), *stages)

        @block.vector
        def _(dve):
            for s in (dve_0, dve_1, dve_r, dve_n, dve_k, dve_t):
                s.open(dve)
            dve.wait_ge(weights, 16 * len(loads))
            if normal:
                dve.tensor_scalar(ktab[:, 1, :], ktab[:, 0, :], 8.0, None, ALU.mult).then_inc(tabled, 1)
                dve.wait_ge(tabled, 1)
                dve.tensor_tensor(ktab[:, 0, :], ktab[:, 1, :], ktab[:, 3, :], ALU.mult).then_inc(tabled, 1)
            else:
                dve.memset(ktab[:, 0, :], DH ** -0.5).then_inc(tabled, 1)
                dve.memset(ktab[:, 1, :], DH ** -0.5).then_inc(tabled, 1)
            dve.wait_ge(tabled, 2)
            dve.tensor_tensor(ktab[:, 2, :], ktab[:, 1, :], att["nk"][:], ALU.mult).then_inc(tabled, 1)
            dve.wait_ge(tabled, 3)
            for k in range(KD):
                dve.tensor_tensor(wnk[:, k].rearrange("p (h n) -> p h n", n=DH),
                                  w[:, k, 0:INNER].rearrange("p (h n) -> p h n", n=DH),
                                  ktab[:, 2, :].unsqueeze(1).to_broadcast([P, H, DH]), ALU.mult).then_inc(tabled, 1)
            dve.wait_ge(tabled, 3 + KD)
            dve.tensor_reduce(wnull[:], wnk[:].rearrange("p k (h n) -> p k h n", n=DH), AX, ALU.add).then_inc(tabled, 1)
            dve.wait_ge(tabled, 4 + KD)
            for k in range(KD):
                dve.tensor_scalar(wf[:, k, NULL:ALL], wnull[:, k, :], gcol[:, k:k + 1], None, ALU.mult).then_inc(folded, 1)

            def x_at(t):
                return c["x"][:, bass.ds(t, 1), :].rearrange("p a d -> p (a d)")

            def moments(t, u):
                dve.bn_stats(stats[:, u, :], x_at(t)).then_inc(dve_0.sem, 1)
                dve.wait_ge(dve_0.sem, dve_0.after("stats", t))
                dve.sem_inc(dve_0.sem, 1)
                dve.bn_aggr(mv[:, u, :], stats[:, u, :]).then_inc(dve_0.sem, 1)

            def normalised(t, u):
                dve.wait_ge(act_0.sem, act_0.after("sd", t))
                dve.reciprocal(rstd[:, u, :], sd[:, u, :]).then_inc(dve_1.sem, 1)
                dve.wait_ge(dve_1.sem, dve_1.after("rstd", t))
                dve.wait_ge(pe_x.sem, pe_x.after("xT", t - 2))
                dve.tensor_scalar(xn[:, u % 2, :], x_at(t), mv[:, u, 0:1], rstd[:, u, 0:1], ALU.subtract,
                                  ALU.mult).then_inc(dve_1.sem, 1)

            def results(t, u):
                dve.wait_ge(pe_t.sem, pe_t.after("qT", t - 4))
                dve.wait_ge(act_r.sem, act_r.after("v", t - 4))
                for m in (1, 2):
                    lo, hi = banks[m]
                    dve.wait_ge(pe_q.sem, pe_q.after(f"b{m}", t))
                    dve.tensor_copy(raw[:, u, lo:hi], ps_q[:, lo:hi]).then_inc(dve_r.sem, 1)

            def norms(t, u):
                dve.wait_ge(act_s.sem, act_s.after("sq", t))
                dve.wait_ge(act_n.sem, act_n.after("norm", t - 1))
                dve.tensor_reduce(n2[:], sq[:, u % 2].rearrange("p (h n) -> p h n", n=DH), AX, ALU.add).then_inc(dve_n.sem, 1)

            def inverse_norms(t, u):
                dve.wait_ge(act_n.sem, act_n.after("norm", t))
                dve.tensor_scalar(nf[:], nr[:], NORM_FLOOR, None, ALU.max).then_inc(dve_n.sem, 1)
                dve.wait_ge(dve_n.sem, dve_n.after("floor", t))
                dve.wait_ge(gp_q.sem, gp_q.after("qn", t - 2))
                dve.reciprocal(rn[:, u % 2], nf[:]).then_inc(dve_n.sem, 1)
                dve.wait_ge(dve_n.sem, dve_n.after("rn", t))

            def keys(t, u):
                null = raw[:, u, NULL:ALL]
                if normal:
                    dve.tensor_tensor(nulln[:], null, rn[:, u % 2, 0:H], ALU.mult).then_inc(dve_k.sem, 1)
                else:
                    dve.wait_ge(dve_r.sem, dve_r.after("b2", t))
                    dve.sem_inc(dve_k.sem, 1)
                dve.wait_ge(pe_t.sem, pe_t.after("qT", t - 2))
                for i in range(2):
                    k_t = raw[:, u, INNER:QK]
                    if normal:
                        dve.scalar_tensor_tensor(kk[:, u % 2, i, :], k_t, rn[:, u % 2, H:HN], ktab[:, 0, :], ALU.mult,
                                                 ALU.mult).then_inc(dve_k.sem, 1)
                    else:
                        dve.tensor_tensor(kk[:, u % 2, i, :], k_t, ktab[:, 0, :], ALU.mult).then_inc(dve_k.sem, 1)
                dve.wait_ge(dve_k.sem, dve_k.after("nulln", t))
                dve.scalar_tensor_tensor(att["nsn"][:, bass.ds(t, 1), :].rearrange("p a h -> p (a h)"),
                                         nulln[:] if normal else null, -1.0, nb_row[:], ALU.mult,
                                         ALU.subtract).then_inc(dve_k.sem, 1)
                dve.wait_ge(dve_k.sem, dve_k.after("null", t))

            def transposed_k(t, u):
                k_hi = att["khi"][:, bass.ds(t * P, P)]
                dve.wait_ge(pe_t.sem, pe_t.after("qT", t))
                dve.tensor_copy(k_hi, ps_t[:, INNER:INNER + P]).then_inc(dve_t.sem, 1)
                dve.wait_ge(dve_t.sem, dve_t.after("khi", t))
                dve.tensor_tensor(att["klo"][:, bass.ds(t * P, P)], ps_t[:, INNER:INNER + P], k_hi.bitcast(F32),
                                  ALU.subtract).then_inc(dve_t.sem, 1)

            stages = [(0, moments), (1, normalised)]
            if normal:
                stages += [(3, norms), (2, results), (3, inverse_norms)]
            else:
                stages += [(2, results)]
            pipeline(dve, NT, 4, *stages, (3, keys), (4, transposed_k))

        if normal:
            @block.gpsimd
            def _(gp):
                gp_q.open(gp)

                def normalised(t, u):
                    gp.wait_ge(dve_n.sem, dve_n.after("rn", t))
                    gp.wait_ge(pe_t.sem, pe_t.after("qT", t - 2))
                    gp.tensor_tensor(qn[:, u % 2].rearrange("p (h n) -> p h n", n=DH),
                                     raw[:, u, 0:INNER].rearrange("p (h n) -> p h n", n=DH),
                                     bc(rn[:, u % 2, 0:H], [P, H, DH]), ALU.mult).then_inc(gp_q.sem, 1)

                pipeline(gp, NT, 4, (0, normalised))


def null_phase(nc, pool, c, att, null_kv, mask, k_scale=None):
    with Phase(nc, pool) as ph:
        m8 = ph.sb("m8", [P, B, S], U8)
        raw = ph.sb("raw", [P, DH])
        ks = ph.sb("ks", [P, DH])
        sq = ph.sb("sq", [P, DH])
        nrm = ph.sb("nrm", [P, 4])
        loaded, masked, step, rooted, triangle = (ph.sem() for _ in range(5))
        block = ph.stack.enter_context(nc.Block())
        normal = k_scale is not None
        n_loads = 16 * (4 if normal else 3)

        @block.sync
        def _(sp):
            sp.dma_start(m8[:].rearrange("p b s -> p (b s)"), row(mask, B * S)).then_inc(loaded, 16)
            sp.dma_start(raw[:], row(null_kv, DH)).then_inc(loaded, 16)
            sp.dma_start(att["nv"][:], row(null_kv, DH, DH)).then_inc(loaded, 16)
            if normal:
                sp.dma_start(ks[:], row(k_scale, DH)).then_inc(loaded, 16)
            sp.wait_ge(loaded, n_loads)

        @block.vector
        def _(dve):
            dve.wait_ge(loaded, n_loads)
            dve.tensor_scalar(att["km"][:], m8[:], -1.0, -MASKED, ALU.add, ALU.mult).then_inc(masked, 1)
            if normal:
                dve.tensor_tensor(sq[:], raw[:], raw[:], ALU.mult).then_inc(step, 1)
                dve.wait_ge(step, 1)
                dve.tensor_reduce(nrm[:, 0:1], sq[:], AX, ALU.add).then_inc(step, 1)
                dve.wait_ge(rooted, 1)
                dve.tensor_scalar(nrm[:, 2:3], nrm[:, 1:2], NORM_FLOOR, None, ALU.max).then_inc(step, 1)
                dve.wait_ge(step, 3)
                dve.reciprocal(nrm[:, 3:4], nrm[:, 2:3]).then_inc(step, 1)
                dve.wait_ge(step, 4)
                dve.scalar_tensor_tensor(att["nk"][:], raw[:], nrm[:, 3:4], ks[:], ALU.mult, ALU.mult).then_inc(step, 1)
            else:
                dve.tensor_copy(att["nk"][:], raw[:]).then_inc(step, 1)

        @block.scalar
        def _(act):
            if normal:
                act.wait_ge(step, 2)
                act.activation(nrm[:, 1:2], nrm[:, 0:1], ACT.Sqrt).then_inc(rooted, 1)

        @block.gpsimd
        def _(gp):
            gp.wait_ge(masked, 1)
            gp.affine_select(out=att["dm"][:].rearrange("p (m j) -> p m j", j=P),
                             in_=att["km"][:].rearrange("p b (m j) -> p (b m) j", j=P), compare_op=ALU.is_ge,
                             fill=MASKED, base=0, pattern=[[0, NT], [-1, P]], channel_multiplier=1).then_inc(triangle, 1)
            gp.wait_ge(triangle, 1)


def core_phase(nc, pool, c, att, bias_src, bias_made=None):
    G = NP // 2
    with Phase(nc, pool) as ph:
        stage = ph.sb("stage", [P, 4, B, P], F32R)
        bias = ph.sb("bias", [P, 4, S])
        prob = ph.sb("prob", [P, 2, S])
        pT = ph.sb("pT", [P, 2, S])
        nsn = ph.sb("nsn", [P, 2, 4])
        nmax = ph.sb("nmax", [P, 2, 4])
        rsum = ph.sb("rsum", [P, 2, 4])
        diff = ph.sb("diff", [P, 2, 4])
        p0 = ph.sb("p0", [P, 2, 4])
        nvp = ph.sb("nvp", [P, 2, 4, DH])
        tot = ph.sb("tot", [P, 4])
        rinv = ph.sb("rinv", [P, 4])
        ot = ph.sb("ot", [P, 4, DH])
        ps_s = ph.ps("ps_s", [P, 2, 2 * BANK])
        ps_pt = ph.ps("ps_pt", [P, 2, BANK])
        ps_o = ph.ps("ps_o", [P, 2, BANK])

        bias_in = [ph.sem() for _ in range(4)]
        gp_s = ph.steps("null hi0 waited0 lo0 hi1 waited1 lo1")
        pe_s = ph.steps("scores", 8)
        dve_s = ph.steps("waited neg", 8)
        act_s = ph.steps("exp", 8)
        pe_t = ph.steps("t0 t1", 8)
        act_t = ph.steps("pt0", 8)
        dve_t = ph.steps("pt1", 8)
        pe_v = ph.steps("pv", 8)
        dve_d = ph.steps("diff")
        act_d = ph.steps("p0")
        gp_d = ph.steps("nvp")
        dve_f = ph.steps("tot rinv ot o")
        block = ph.stack.enter_context(nc.Block())

        def units(eng, *stages):

            def step(qt, g, v):
                for lag, fn in stages:
                    q, gg, w = qt, g, v - lag
                    if w < 0:
                        w += 8
                        if isinstance(g, int) and g == 0:
                            q, gg = qt - 1, G - 1
                        else:
                            gg = g - 1
                    if isinstance(q, int) and 0 <= q < TB:
                        fn(q, gg, w, (gg + q * G) * 8 + w, (gg + q * G) * 2 + w // 4)

            deepest = max(lag for lag, _ in stages)
            for qt in range(TB):
                for v in range(8):
                    step(qt, 0, v)
                with eng.Fori(1, G) as g:
                    for v in range(8):
                        step(qt, g, v)
            for v in range(deepest):
                for lag, fn in stages:
                    if v < lag:
                        w = v - lag + 8
                        fn(TB - 1, G - 1, w, (TB * G - 1) * 8 + w, (TB * G - 1) * 2 + w // 4)

        def split(qt):
            return (qt + 2) // 2, qt + 1

        @block.sync
        def _(sp):
            if bias_made is not None:
                sp.wait_ge(bias_made, 16)
            for qt in range(TB):
                with sp.Fori(0, G) as g:
                    for h in range(4):
                        sp.wait_ge(dve_s.sem, dve_s.after("neg", (g + qt * G) * 8 + 2 * h + 1 - 8))
                        sp.dma_start(bias[:, h, 0:(qt + 1) * P], bias_src(g * 4 + h, qt)).then_inc(bias_in[h], 16)

        @block.gpsimd
        def _(gp):
            gp_s.open(gp)
            gp_d.open(gp)

            def queries(qt, g, r):
                pair = (g + qt * G) * 2 + r
                gp.wait_ge(dve_d.sem, dve_d.after("diff", pair - 2))
                gp.tensor_copy(nsn[:, r].rearrange("p (h b) -> p h b", b=B),
                               att["nsn"][:, qt:NT:TB, bass.ds(g * 4 + 2 * r, 2)].rearrange("p b h -> p h b")
                               ).then_inc(gp_s.sem, 1)
                for hp in range(2):
                    gp.wait_ge(pe_s.sem, pe_s.after("scores", pair * 4 + 2 * hp + 1 - 8))
                    own, other = slice(hp * DH, (hp + 1) * DH), slice((1 - hp) * DH, (2 - hp) * DH)
                    q_t = att["qo"][own, qt:NT:TB, bass.ds(g * 2 + r, 1), :].rearrange("d b a n -> d b (a n)")
                    gp.tensor_copy(stage[own, 2 * r + hp], q_t).then_inc(gp_s.sem, 1)
                    gp.wait_ge(gp_s.sem, gp_s.after(f"hi{hp}", pair))
                    gp.sem_inc(gp_s.sem, 1)
                    gp.tensor_tensor(stage[other, 2 * r + hp], q_t, stage[own, 2 * r + hp].bitcast(F32),
                                     ALU.subtract).then_inc(gp_s.sem, 1)
                    gp.wait_ge(gp_s.sem, gp_s.after(f"lo{hp}", pair))

            def null_values(r, pair):
                gp.wait_ge(act_d.sem, act_d.after("p0", pair))
                gp.wait_ge(dve_f.sem, dve_f.after("ot", pair - 2))
                gp.tensor_tensor(nvp[:, r], att["nv"][:].unsqueeze(1).to_broadcast([P, 4, DH]),
                                 bc(p0[:, r], [P, 4, DH]), ALU.mult).then_inc(gp_d.sem, 1)

            queries(0, 0, 0)
            for qt in range(TB):
                with gp.Fori(0, G - 1) as g:
                    queries(qt, g, 1)
                    null_values(0, (g + qt * G) * 2)
                    queries(qt, g + 1, 0)
                    null_values(1, (g + qt * G) * 2 + 1)
                queries(qt, G - 1, 1)
                null_values(0, (qt * G + G - 1) * 2)
                if qt + 1 < TB:
                    queries(qt + 1, 0, 0)
                null_values(1, (qt * G + G - 1) * 2 + 1)

        @block.tensor
        def _(pe):
            for s in (pe_s, pe_t, pe_v):
                s.open(pe)

            def scores(qt, g, v, n, pair):
                h, b, u = v // 2, v % 2, v % 2
                W = (qt + 1) * P
                pe.wait_ge(gp_s.sem, gp_s.after(f"lo{h % 2}", pair))
                pe.wait_ge(dve_s.sem, dve_s.after("neg", n - 2))
                for lo in range(0, W, BANK):
                    hi = min(lo + BANK, W)
                    last = min(hi, qt * P)
                    if last > lo:
                        pe.matmul(ps_s[:, u, lo:last], c["ident16"][:], att["km"][:, b, lo:last], start=True,
                                  stop=False, skip_group_check=True)
                    if hi == W:
                        pe.matmul(ps_s[:, u, W - P:W], c["ident16"][:], att["dm"][:, b * S + W - P:b * S + W],
                                  start=last <= lo, stop=False, skip_group_check=True)
                    for part in ("khi", "klo"):
                        ins = pe.matmul(ps_s[:, u, lo:hi], stage[:, h, b, :], att[part][:, b * S + lo:b * S + hi],
                                        start=False, stop=part == "klo", skip_group_check=True)
                ins.then_inc(pe_s.sem, 1)

            def transposes(qt, g, v, n, pair):
                u = v % 2
                first, n_blocks = split(qt)
                pe.wait_ge(act_s.sem, act_s.after("exp", n))
                pe.wait_ge(act_t.sem, act_t.after("pt0", n - 1))
                for k in range(first):
                    ins = pe.transpose(ps_pt[:, 0, k * P:(k + 1) * P], prob[:, u, k * P:(k + 1) * P], c["ident"][:])
                ins.then_inc(pe_t.sem, 1 if first < n_blocks else 2)
                if first < n_blocks:
                    pe.wait_ge(dve_t.sem, dve_t.after("pt1", n - 1))
                    for k in range(first, n_blocks):
                        ins = pe.transpose(ps_pt[:, 1, (k - first) * P:(k - first + 1) * P],
                                           prob[:, u, k * P:(k + 1) * P], c["ident"][:])
                    ins.then_inc(pe_t.sem, 1)

            def values(qt, g, v, n, pair):
                u, r, w = v % 2, v // 4, v % 4
                first, n_blocks = split(qt)
                pe.wait_ge(act_t.sem, act_t.after("pt0", n))
                if w == 0:
                    pe.wait_ge(dve_f.sem, dve_f.after("ot", pair - 2))
                for k in range(n_blocks):
                    if k == first:
                        pe.wait_ge(dve_t.sem, dve_t.after("pt1", n))
                    ins = pe.matmul(ps_o[:, r, w * DH:(w + 1) * DH], pT[:, u, k * P:(k + 1) * P],
                                    att["v"][:, (v % 2) * TB + k, :], start=(k == 0), stop=(k == n_blocks - 1))
                ins.then_inc(pe_v.sem, 1)

            units(pe, (0, scores), (1, transposes), (2, values))

        @block.vector
        def _(dve):
            for s in (dve_s, dve_t, dve_d, dve_f):
                s.open(dve)

            def negated(qt, g, v, n, pair):
                h, u, r, w = v // 2, v % 2, v // 4, v % 4
                W = (qt + 1) * P
                dve.wait_ge(gp_s.sem, gp_s.after("null", pair))
                dve.wait_ge(bias_in[h], (g + qt * G + 1) * 16)
                dve.wait_ge(pe_t.sem, pe_t.after("t1", n - 2))
                if w == 0:
                    dve.wait_ge(act_s.sem, act_s.after("exp", n - 5))
                dve.wait_ge(dve_s.sem, dve_s.after("neg", n - 1))
                dve.wait_ge(pe_s.sem, pe_s.after("scores", n))
                dve.sem_inc(dve_s.sem, 1)
                dve.tensor_tensor_reduce(out=prob[:, u, 0:W], in0=ps_s[:, u, 0:W], in1=bias[:, h, 0:W], scale=-1.0,
                                         scalar=nsn[:, r, w:w + 1], op0=ALU.add, op1=ALU.min,
                                         accum_out=nmax[:, r, w:w + 1]).then_inc(dve_s.sem, 1)

            def blocks(qt, g, v, n, pair):
                u, r = v % 2, v // 4
                first, n_blocks = split(qt)
                if v % 4 == 3:
                    dve.wait_ge(dve_s.sem, dve_s.after("neg", n))
                    dve.wait_ge(act_d.sem, act_d.after("p0", pair - 2))
                    dve.tensor_tensor(diff[:, r], nmax[:, r], nsn[:, r], ALU.subtract).then_inc(dve_d.sem, 1)
                if first < n_blocks:
                    dve.wait_ge(pe_t.sem, pe_t.after("t1", n))
                    dve.wait_ge(pe_v.sem, pe_v.after("pv", n - 2))
                    dve.tensor_copy(pT[:, u, first * P:n_blocks * P], ps_pt[:, 1, 0:(n_blocks - first) * P]
                                    ).then_inc(dve_t.sem, 1)
                else:
                    dve.sem_inc(dve_t.sem, 1)

            def outputs(qt, g, v, n, pair):
                r = v // 4
                if v % 4 != 3:
                    return
                dve.wait_ge(act_d.sem, act_d.after("p0", pair))
                dve.tensor_tensor(tot[:], rsum[:, r], p0[:, r], ALU.add).then_inc(dve_f.sem, 1)
                dve.wait_ge(dve_f.sem, dve_f.after("tot", pair))
                dve.reciprocal(rinv[:], tot[:]).then_inc(dve_f.sem, 1)
                dve.wait_ge(gp_d.sem, gp_d.after("nvp", pair))
                dve.wait_ge(pe_v.sem, pe_v.after("pv", n))
                dve.tensor_tensor(ot[:], ps_o[:, r, 0:4 * DH].rearrange("p (w n) -> p w n", n=DH), nvp[:, r],
                                  ALU.add).then_inc(dve_f.sem, 1)
                dve.wait_ge(dve_f.sem, dve_f.after("ot", pair))
                for hp in range(2):
                    ins = dve.tensor_tensor(att["qo"][:, qt:NT:TB, bass.ds(g * 2 + r, 1), hp * DH:(hp + 1) * DH]
                                            .rearrange("p b a n -> p b (a n)"), ot[:, 2 * hp:2 * hp + 2],
                                            bc(rinv[:, 2 * hp:2 * hp + 2], [P, 2, DH]), ALU.mult)
                ins.then_inc(dve_f.sem, 1)

            units(dve, (0, negated), (1, blocks), (3, outputs))
            dve.wait_ge(dve_f.sem, dve_f.after("o", TB * NP - 1))

        @block.scalar
        def _(act):
            for s in (act_s, act_t, act_d):
                s.open(act)

            def blocks(qt, g, v, n, pair):
                u = v % 2
                first, _ = split(qt)
                act.wait_ge(pe_t.sem, pe_t.after("t0", n))
                act.wait_ge(pe_v.sem, pe_v.after("pv", n - 2))
                act.activation(pT[:, u, 0:first * P], ps_pt[:, 0, 0:first * P], ACT.Copy).then_inc(act_t.sem, 1)

            def exponentials(qt, g, v, n, pair):
                u, r, w = v % 2, v // 4, v % 4
                W = (qt + 1) * P
                if w == 0:
                    act.wait_ge(dve_f.sem, dve_f.after("tot", pair - 2))
                act.wait_ge(dve_s.sem, dve_s.after("neg", n))
                act.activation(prob[:, u, 0:W], prob[:, u, 0:W], ACT.Exp, bias=nmax[:, r, w:w + 1], scale=-1.0,
                               accum_out=rsum[:, r, w:w + 1]).then_inc(act_s.sem, 1)

            def null_probability(qt, g, v, n, pair):
                r = v // 4
                if v % 4 == 3:
                    act.wait_ge(dve_d.sem, dve_d.after("diff", pair))
                    act.wait_ge(gp_d.sem, gp_d.after("nvp", pair - 2))
                    act.activation(p0[:, r], diff[:, r], ACT.Exp).then_inc(act_d.sem, 1)

            units(act, (1, blocks), (0, exponentials), (1, null_probability))


def out_phase(nc, pool, c, att, wo, g):
    with Phase(nc, pool) as ph:
        w = ph.sb("w", [P, NP, D])
        gt = ph.sb("gt", [P, D])
        o = ph.sb("o", [P, 2, INNER])
        oT = ph.sb("oT", [P, 2, INNER])
        stats = ph.sb("stats", [P, 2, 6])
        mv = ph.sb("mv", [P, 2, 2])
        sd = ph.sb("sd", [P, 2, 1])
        rstd = ph.sb("rstd", [P, 2, 1])
        yc = ph.sb("yc", [P, 2, D])
        ps_t = ph.ps("ps_t", [P, 2, 2 * BANK])
        ps_y = ph.ps("ps_y", [P, 2, BANK])
        weights = ph.sem()
        gp_a = ph.steps("o")
        pe_a = ph.steps("oT")
        act_a = ph.steps("oT")
        dve_a = ph.steps("oT")
        pe_b = ph.steps("y")
        dve_b = ph.steps("stats waited moments rstd centred y")
        act_b = ph.steps("sd")
        block = ph.stack.enter_context(nc.Block())

        @block.sync
        def _(sp):
            sp.dma_start(w[:], wo.rearrange("(k p) n -> p k n", p=P)).then_inc(weights, 16)
            sp.dma_start(gt[:], row(g, D)).then_inc(weights, 16)

        @block.gpsimd
        def _(gp):
            gp_a.open(gp)

            def stage(t, u):
                gp.wait_ge(pe_a.sem, pe_a.after("oT", t - 2))
                gp.tensor_copy(o[:, u, :], att["qo"][:, bass.ds(t, 1)].rearrange("p a q n -> p (a q n)")
                               ).then_inc(gp_a.sem, 1)

            tiles(gp, NT, stage)

        @block.tensor
        def _(pe):
            pe_a.open(pe)
            pe_b.open(pe)
            pe.wait_ge(weights, 32)

            def a(t, u):
                pe.wait_ge(gp_a.sem, gp_a.after("o", t))
                pe.wait_ge(act_a.sem, act_a.after("oT", t - 2))
                pe.wait_ge(dve_a.sem, dve_a.after("oT", t - 2))
                for k in range(NP):
                    ins = pe.transpose(ps_t[:, u, k * P:(k + 1) * P], o[:, u, k * P:(k + 1) * P], c["ident"][:])
                ins.then_inc(pe_a.sem, 1)

            def b(t, u):
                pe.wait_ge(act_a.sem, act_a.after("oT", t))
                pe.wait_ge(dve_a.sem, dve_a.after("oT", t))
                pe.wait_ge(dve_b.sem, dve_b.after("centred", t - 2))
                for k in range(NP):
                    ins = pe.matmul(ps_y[:, u, 0:D], oT[:, u, k * P:(k + 1) * P], w[:, k, :], start=(k == 0),
                                    stop=(k == NP - 1))
                ins.then_inc(pe_b.sem, 1)

            skewed(pe, NT, a, b)

        @block.vector
        def _(dve):
            dve_a.open(dve)
            dve_b.open(dve)
            dve.wait_ge(weights, 32)

            def a(t, u):
                dve.wait_ge(pe_a.sem, pe_a.after("oT", t))
                dve.wait_ge(pe_b.sem, pe_b.after("y", t - 2))
                dve.tensor_copy(oT[:, u, BANK:], ps_t[:, u, BANK:]).then_inc(dve_a.sem, 1)

            def b(t, u):
                dve.wait_ge(pe_b.sem, pe_b.after("y", t))
                dve.bn_stats(stats[:, u, :], ps_y[:, u, 0:D]).then_inc(dve_b.sem, 1)
                dve.wait_ge(dve_b.sem, dve_b.after("stats", t))
                dve.sem_inc(dve_b.sem, 1)
                dve.bn_aggr(mv[:, u, :], stats[:, u, :]).then_inc(dve_b.sem, 1)
                dve.wait_ge(act_b.sem, act_b.after("sd", t))
                dve.reciprocal(rstd[:, u, :], sd[:, u, :]).then_inc(dve_b.sem, 1)
                dve.wait_ge(dve_b.sem, dve_b.after("rstd", t))
                dve.tensor_scalar(yc[:, u, :], ps_y[:, u, 0:D], mv[:, u, 0:1], rstd[:, u, 0:1], ALU.subtract,
                                  ALU.mult).then_inc(dve_b.sem, 1)
                dve.wait_ge(dve_b.sem, dve_b.after("centred", t))
                dve.tensor_tensor(c["cur"][:, bass.ds(t, 1), :].rearrange("p a d -> p (a d)"), yc[:, u, :], gt[:],
                                  ALU.mult).then_inc(dve_b.sem, 1)

            skewed(dve, NT, a, b)

        @block.scalar
        def _(act):
            act_a.open(act)
            act_b.open(act)

            def a(t, u):
                act.wait_ge(pe_a.sem, pe_a.after("oT", t))
                act.wait_ge(pe_b.sem, pe_b.after("y", t - 2))
                act.activation(oT[:, u, 0:BANK], ps_t[:, u, 0:BANK], ACT.Copy).then_inc(act_a.sem, 1)

            def b(t, u):
                act.wait_ge(dve_b.sem, dve_b.after("moments", t))
                act.activation(sd[:, u, :], mv[:, u, 1:2], ACT.Sqrt, bias=c["eps"][:, 0:1]).then_inc(act_b.sem, 1)

            skewed(act, NT, a, b)

N_SLOT_TILES = {1: NT + 8, 2: 2 * NT + 8}


def interleaved(eng, n, a1, b, a2):

    def step(t, u):
        a1(t, u)
        b(t - 1, 1 - u)
        a2(t, u)

    a1(0, 0)
    a2(0, 0)
    with eng.Fori(0, n // 2 - 1) as i:
        step(i * 2 + 1, 1)
        step(i * 2 + 2, 0)
    step(n - 1, 1)
    b(n - 1, 1)


def loaded(t, u, n_dmas):
    return (t - u + 2) * (8 * n_dmas)


def at(buf, t):
    return buf[:, t] if isinstance(t, int) else buf[:, bass.ds(t, 1), :].rearrange("p a n -> p (a n)")


class Gather:

    def __init__(self, r, choices, ys_dram, n_slots, dst, base, rows_in):
        self.r, self.choices, self.ys_dram, self.n_slots, self.dst, self.base = r, choices, ys_dram, n_slots, dst, base
        self.sems, self.start = rows_in["sems"], rows_in["count"]
        rows_in["count"] += 16 * choices

    def rows(self, gp, yg):
        for t in range(NT):
            for k in range(self.choices):
                gp.indirect_dma_start(out=yg[:, k, t, :], out_offset=None, in_=self.ys_dram[0:self.n_slots, :],
                                      in_offset=bass.IndirectOffsetOnAxis(ap=self.r["slot"][:, k, t:t + 1], axis=0),
                                      bounds_check=self.n_slots - 1, oob_is_err=False).then_inc(self.sems[t], 16)

    def add(self, dve, t, yg, steps):
        dve.wait_ge(self.sems[t], self.start + 16 * self.choices)
        for k in range(self.choices):
            if k:
                dve.wait_ge(steps.sem, steps.after(f"y{k - 1}", t))
            dve.scalar_tensor_tensor(self.dst[:, t], yg[:, k, t], self.r["wt"][:, k, t:t + 1],
                                     self.dst[:, t] if k else self.base[:, t], ALU.mult, ALU.add).then_inc(steps.sem, 1)


def logits_phase(nc, pool, c, r, src, gate_w, bias, cond=None, halve=False, shared=None, rms=None, gather=None):
    E = gate_w.shape[1]
    with Phase(nc, pool) as ph:
        w = ph.sb("w", [P, KD, E])
        lb = ph.sb("lb", [P, B, E])
        xs = ph.sb("xs", [P, 2, D])
        xT = ph.sb("xT", [P, 2, KD, P])
        if cond is not None:
            cw = ph.sb("cw", [64, E])
            cg = ph.sb("cg", [64, B])
            cgb = ph.sb("cgb", [64, B, P])
        if shared is not None:
            wg = ph.sb("wg", [P, KD, D])
            wu = ph.sb("wu", [P, KD, D])
            wd = ph.sb("wd", [P, KD, D])
            small = ph.sb("small", [P, 2, D])
            lr = ph.sb("lr", [P, 2, D])
            hT = ph.sb("hT", [P, 2, D])
        if rms is not None:
            gt = ph.sb("gt", [P, D])
            sq = ph.sb("sq", [P, 2, D])
            ms = ph.sb("ms", [P, 2, 4])
        if gather:
            yg = ph.sb("yg", [P, gather.choices, NT, D])
        ps_x = ph.ps("ps_x", [P, 2, BANK])
        ps_l = ph.ps("ps_l", [P, 1, BANK])
        if shared is not None:
            ps_g = ph.ps("ps_g", [P, 2, BANK])
            ps_u = ph.ps("ps_u", [P, 2, BANK])
            ps_y = ph.ps("ps_y", [P, 1, BANK])

        weights, biased, cb, rep = ph.sem(), ph.sem(), ph.sem(), ph.sem()
        act_a = ph.steps("x")
        dve_g = ph.steps(" ".join(f"y{k}" for k in range(gather.choices)) if gather else "y0")
        pe_x = ph.steps("xT")
        act_x = ph.steps("xT")
        pe_l = ph.steps("logits")
        dve_l = ph.steps("logits")
        pe_s = ph.steps("gate up")
        act_s = ph.steps("hundredth")
        dve_s = ph.steps("leaky h")
        pe_y = ph.steps("y")
        act_y = ph.steps("y")
        act_n = ph.steps("ms root")
        dve_n = ph.steps("rinv scaled xn")
        block = ph.stack.enter_context(nc.Block())
        loads = [(w[:], gate_w.rearrange("(k p) n -> p k n", p=P))]
        if bias is not None:
            loads += [(lb[:, b, :], row(bias, E)) for b in range(B)]
        if cond is not None:
            loads += [(cw[:], cond[1])]
            loads += [(cg[:, b:b + 1], bass.AP(cond[0].tensor, cond[0].offset + 64 * b, [[1, 64], [1, 1]])) for b in range(B)]
        if shared is not None:
            loads += [(s[:], d.rearrange("(k p) n -> p k n", p=P)) for s, d in zip((wg, wu, wd), shared)]
        if rms is not None:
            loads += [(gt[:], row(rms, D))]

        @block.sync
        def _(sp):
            for dst, src_ in loads:
                sp.dma_start(dst, src_).then_inc(weights, 16)
            sp.wait_ge(weights, 16 * len(loads))

        unroll = NT if gather else 4
        late = 0 if rms is None else 1

        if gather:
            @block.gpsimd
            def _(gp):
                gather.rows(gp, yg)

        @block.tensor
        def _(pe):
            for s in (pe_x, pe_l, pe_s, pe_y):
                s.open(pe)
            pe.wait_ge(weights, 16 * len(loads))
            if cond is not None:
                pe.wait_ge(rep, 2)
                for b in range(B):
                    ins = pe.matmul(ps_l[:, 0, b * E:(b + 1) * E], cgb[:, b, :], cw[:], start=True, stop=True)
                ins.then_inc(cb, 1)
                pe.wait_ge(biased, 1)

            def a1(t, u):
                pe.wait_ge(act_a.sem, act_a.after("x", t))
                pe.wait_ge(act_x.sem, act_x.after("xT", t - 2))
                for k in range(KD):
                    ins = pe.transpose(ps_x[:, u % 2, k * P:(k + 1) * P], xs[:, u % 2, k * P:(k + 1) * P], c["ident"][:])
                ins.then_inc(pe_x.sem, 1)

            def a2(t, u):
                pe.wait_ge(act_x.sem, act_x.after("xT", t))
                pe.wait_ge(dve_l.sem, dve_l.after("logits", t - 1))
                for k in range(KD):
                    ins = pe.matmul(ps_l[:, 0, 0:E], xT[:, u % 2, k, :], w[:, k, :], start=(k == 0), stop=(k == KD - 1))
                ins.then_inc(pe_l.sem, 1)
                if shared is not None:
                    for ww, ps, used in ((wg, ps_g, "leaky"), (wu, ps_u, "h")):
                        pe.wait_ge(dve_s.sem, dve_s.after(used, t - 2))
                        for m in range(D // P):
                            for k in range(KD):
                                ins = pe.matmul(ps[:, u % 2, m * P:(m + 1) * P], ww[:, k, m * P:(m + 1) * P], xT[:, u % 2, k, :],
                                                start=(k == 0), stop=(k == KD - 1))
                        ins.then_inc(pe_s.sem, 1)

            def b(t, u):
                if shared is None:
                    return
                pe.wait_ge(dve_s.sem, dve_s.after("h", t))
                pe.wait_ge(act_y.sem, act_y.after("y", t - 1))
                for m in range(D // P):
                    ins = pe.matmul(ps_y[:, 0, 0:D], hT[:, u % 2, m * P:(m + 1) * P], wd[:, m, :], start=(m == 0),
                                    stop=(m == D // P - 1))
                ins.then_inc(pe_y.sem, 1)

            pipeline(pe, NT, unroll, (late, a1), (late + 3, b), (late + 1, a2))

        @block.scalar
        def _(act):
            for s in (act_a, act_x, act_s, act_y, act_n):
                s.open(act)

            def stage(t, u):
                act.wait_ge(pe_x.sem, pe_x.after("xT", t - 2))
                if rms is not None:
                    act.wait_ge(dve_n.sem, dve_n.after("xn", t))
                elif gather:
                    act.wait_ge(dve_g.sem, dve_g.after(f"y{gather.choices - 1}", t))
                act.activation(xs[:, u % 2, :], at(src, t), ACT.Copy).then_inc(act_a.sem, 1)

            def norm(t, u):
                if rms is None:
                    return
                act.wait_ge(dve_n.sem, dve_n.after("xn", t - 2))
                if gather:
                    act.wait_ge(dve_g.sem, dve_g.after(f"y{gather.choices - 1}", t))
                act.activation(sq[:, u % 2, :], at(src, t), ACT.Square,
                               scale=float(D) ** -0.5, accum_out=ms[:, u % 2, 0:1]).then_inc(act_n.sem, 1)
                act.wait_ge(act_n.sem, act_n.after("ms", t))
                act.activation(ms[:, u % 2, 1:2], ms[:, u % 2, 0:1], ACT.Sqrt, bias=c["eps"][:, 1:2]).then_inc(act_n.sem, 1)

            def xT_out(t, u):
                act.wait_ge(pe_x.sem, pe_x.after("xT", t))
                act.wait_ge(pe_l.sem, pe_l.after("logits", t - 2))
                if shared is not None:
                    act.wait_ge(pe_s.sem, pe_s.after("up", t - 2))
                act.activation(xT[:, u % 2].rearrange("p k n -> p (k n)"), ps_x[:, u % 2, 0:D], ACT.Copy).then_inc(act_x.sem, 1)

            def hundredth(t, u):
                act.wait_ge(pe_s.sem, pe_s.after("gate", t))
                act.wait_ge(dve_s.sem, dve_s.after("leaky", t - 2))
                act.activation(small[:, u % 2, :], ps_g[:, u % 2, 0:D], ACT.Copy, scale=0.01).then_inc(act_s.sem, 1)

            def y_out(t, u):
                act.wait_ge(pe_y.sem, pe_y.after("y", t))
                act.activation(r["acc"][:, bass.ds(t, 1), :], ps_y[:, 0:1, 0:D], ACT.Copy).then_inc(act_y.sem, 1)

            if shared is not None:
                pipeline(act, NT, unroll, (2, hundredth), (0, stage), (3, y_out), (1, xT_out))
            else:
                pipeline(act, NT, unroll, (0, norm), (late, stage), (late + 1, xT_out))

        @block.vector
        def _(dve):
            for s in (dve_g, dve_l, dve_s, dve_n):
                s.open(dve)
            dve.wait_ge(weights, 16 * len(loads))
            if cond is not None:
                for b in range(B):
                    dve.tensor_copy(cgb[:, b, :], cg[:, b:b + 1].to_broadcast([64, P])).then_inc(rep, 1)
                dve.wait_ge(cb, 1)
                dve.tensor_copy(lb[:].rearrange("p b e -> p (b e)"), ps_l[:, 0, 0:B * E]).then_inc(biased, 1)
                dve.wait_ge(biased, 1)

            def norm(t, u):
                if rms is None:
                    return
                x_t = at(src, t)
                dve.wait_ge(act_n.sem, act_n.after("root", t))
                dve.reciprocal(ms[:, u % 2, 2:3], ms[:, u % 2, 1:2]).then_inc(dve_n.sem, 1)
                dve.wait_ge(dve_n.sem, dve_n.after("rinv", t))
                dve.tensor_scalar(sq[:, u % 2, :], x_t, ms[:, u % 2, 2:3], None, ALU.mult).then_inc(dve_n.sem, 1)
                dve.wait_ge(dve_n.sem, dve_n.after("scaled", t))
                dve.tensor_tensor(x_t, sq[:, u % 2, :], gt[:], ALU.mult).then_inc(dve_n.sem, 1)

            def b(t, u):
                dve.wait_ge(pe_l.sem, pe_l.after("logits", t))
                l_t = at(r["logits"], t)[:, 0:E]
                dve.tensor_copy(l_t, ps_l[:, 0, 0:E]).then_inc(dve_l.sem, 1)
                if shared is not None:
                    dve.wait_ge(act_s.sem, act_s.after("hundredth", t))
                    dve.tensor_tensor(lr[:, u % 2, :], small[:, u % 2, :], ps_g[:, u % 2, 0:D], ALU.max).then_inc(dve_s.sem, 1)
                    dve.wait_ge(dve_s.sem, dve_s.after("leaky", t))
                    dve.wait_ge(pe_s.sem, pe_s.after("up", t))
                    dve.wait_ge(pe_y.sem, pe_y.after("y", t - 2))
                    dve.tensor_tensor(hT[:, u % 2, :], lr[:, u % 2, :], ps_u[:, u % 2, 0:D], ALU.mult).then_inc(dve_s.sem, 1)

            def combine(t, u):
                if gather:
                    gather.add(dve, t, yg, dve_g)

            pipeline(dve, NT, unroll, (0, combine), (0, norm), (late + 2, b))
            if bias is not None or cond is not None:
                dve.wait_ge(dve_l.sem, dve_l.after("logits", NT - 1))
                for b_ in range(B):
                    l_b = r["logits"][:, b_ * TB:(b_ + 1) * TB, 0:E]
                    dve.tensor_tensor(l_b, l_b, lb[:, b_, :].unsqueeze(1).to_broadcast([P, TB, E]), ALU.add).then_inc(biased, 1)
                if halve:
                    dve.wait_ge(biased, 3)
                    l_a = r["logits"][:, :, 0:E]
                    dve.tensor_scalar(l_a, l_a, 0.5, None, ALU.mult).then_inc(biased, 1)


def choose_phase(nc, pool, c, r, E, choices, dispatch_src, xs_dram, capacity=None, softmax_all=True, dma_done=None):
    n_slots = E * P if capacity else N_SLOT_TILES[choices] * P
    with Phase(nc, pool) as ph:
        L = r["logits"][:, :, 0:E]
        iota_i = ph.sb("iota_i", [P, NT, E], I32)
        iota = ph.sb("iota", [P, NT, E])
        far = ph.sb("far", [P, NT, E])
        mx = ph.sb("mx", [P, 2, NT])
        idx = ph.sb("idx", [P, 2, NT])
        oh = ph.sb("oh", [P, 2, NT, E])
        ex = ph.sb("ex", [P, NT, E])
        z = ph.sb("z", [P, 4, NT])
        m16 = ph.sb("m16", [P, NT * E], BF16)
        msum = ph.sb("msum", [P, NT, E])
        tri = ph.sb("tri", [P, P], BF16)
        ones16 = ph.sb("ones16", [P, P], BF16)
        cum = ph.sb("cum", [P, 2, NT + 1, E])
        rank = ph.sb("rank", [P, NT, E])
        cnt_i = ph.sb("cnt_i", [P, 2, E], I32)
        ends = ph.sb("ends", [P, 3, E + 1])
        sel = ph.sb("sel", [P, NT, E])
        slot_f = ph.sb("slot_f", [P, 4, NT])
        n_slot_tiles = n_slots // P
        tmap = ph.sb("tmap", [P, n_slot_tiles, E])
        tio_i = ph.sb("tio_i", [P, n_slot_tiles, E], I32)
        tio = ph.sb("tio", [P, n_slot_tiles, E])
        tsum = ph.sb("tsum", [P, n_slot_tiles])
        ps_r = ph.ps("ps_r", [P, BANK])
        ps_t = ph.ps("ps_t", [P, BANK])
        made, v, prefix, exped, slots_ready = (ph.sem() for _ in range(5))
        block = ph.stack.enter_context(nc.Block())
        count = {"v": 0}

        @block.gpsimd
        def _(gp):
            gp.iota(iota_i[:], pattern=[[0, NT], [1, E]], base=0, channel_multiplier=0).then_inc(made, 1)
            gp.iota(tio_i[:], pattern=[[1, n_slot_tiles], [0, E]], base=0, channel_multiplier=0).then_inc(made, 1)
            gp.memset(tri[:], 1.0).then_inc(made, 1)
            gp.memset(ones16[:], 1.0).then_inc(made, 1)
            gp.wait_ge(made, 4)
            gp.affine_select(out=tri[:], in_=tri[:], compare_op=ALU.is_gt, fill=0.0, base=0, pattern=[[1, P]],
                             channel_multiplier=-1).then_inc(made, 1)
            gp.wait_ge(slots_ready, 1)
            for t in range(NT):
                for k in range(choices):
                    gp.indirect_dma_start(out=xs_dram[0:n_slots, :],
                                          out_offset=bass.IndirectOffsetOnAxis(ap=r["slot_out"][:, k, t:t + 1], axis=0),
                                          in_=dispatch_src[:, t, :], in_offset=None, bounds_check=n_slots - 1,
                                          oob_is_err=False).then_inc(dma_done["sem"], 16)
            dma_done["count"] += 16 * NT * choices
            gp.wait_ge(dma_done["sem"], dma_done["count"])

        @block.tensor
        def _(pe):
            pe.wait_ge(made, 5)
            pe.wait_ge(prefix, 1)
            pe.matmul(ps_r[:, 0:NT * E], tri[:], m16[:], start=True, stop=True).then_inc(prefix, 1)
            pe.matmul(ps_t[:, 0:NT * E], ones16[:], m16[:], start=True, stop=True).then_inc(prefix, 1)

        @block.scalar
        def _(act):
            act.wait_ge(exped, 1)
            act.activation(ex[:], ex[:], ACT.Exp).then_inc(exped, 1)
            if choices == 2:
                act.activation(z[:, 1, :], z[:, 1, :], ACT.Exp).then_inc(exped, 1)

        @block.vector
        def _(dve):
            def then(ins):
                count["v"] += 1
                ins.then_inc(v, 1)
                dve.wait_ge(v, count["v"])

            wide = [P, NT, E]
            dve.wait_ge(made, 2)
            then(dve.tensor_copy(iota[:], iota_i[:]))
            then(dve.tensor_copy(tio[:], tio_i[:]))
            for k in range(choices):
                if k == 1:
                    then(dve.scalar_tensor_tensor(sel[:], oh[:, 0], -3e38, L, ALU.mult, ALU.add))
                Lk = L if k == 0 else sel[:]
                then(dve.tensor_reduce(mx[:, k, :], Lk, AX, ALU.max))
                then(dve.tensor_tensor(far[:], Lk, bc(mx[:, k, :], wide), ALU.is_lt))
                then(dve.scalar_tensor_tensor(far[:], far[:], float(E), iota[:], ALU.mult, ALU.add))
                then(dve.tensor_reduce(idx[:, k, :], far[:], AX, ALU.min))
                then(dve.tensor_tensor(oh[:, k], iota[:], bc(idx[:, k, :], wide), ALU.is_equal))
            then(dve.tensor_tensor(ex[:], L, bc(mx[:, 0, :], wide), ALU.subtract))
            if choices == 2:
                then(dve.tensor_tensor(z[:, 1, :], mx[:, 1, :], mx[:, 0, :], ALU.subtract))
            dve.sem_inc(exped, 1)
            if choices == 2:
                then(dve.tensor_tensor(msum[:], oh[:, 0], oh[:, 1], ALU.add))
                then(dve.tensor_copy(m16[:], msum[:].rearrange("p t e -> p (t e)")))
            else:
                then(dve.tensor_copy(m16[:], oh[:, 0].rearrange("p t e -> p (t e)")))
            dve.sem_inc(prefix, 1)
            dve.wait_ge(exped, choices + 1)
            if softmax_all:
                then(dve.tensor_reduce(z[:, 0, :], ex[:], AX, ALU.add))
            if choices == 1:
                then(dve.reciprocal(r["wt"][:, 0, :], z[:, 0, :]))
            else:
                if softmax_all:
                    then(dve.tensor_scalar(z[:, 2, :], z[:, 1, :], 1.0, None, ALU.add))
                    then(dve.scalar_tensor_tensor(z[:, 2, :], z[:, 0, :], 1e-20, z[:, 2, :], ALU.mult, ALU.add))
                else:
                    then(dve.tensor_scalar(z[:, 2, :], z[:, 1, :], 1.0, None, ALU.add))
                then(dve.reciprocal(r["wt"][:, 0, :], z[:, 2, :]))
                then(dve.tensor_tensor(r["wt"][:, 1, :], z[:, 1, :], r["wt"][:, 0, :], ALU.mult))
            dve.wait_ge(prefix, 3)
            then(dve.memset(cum[:, 0, 0, :], 0.0))
            then(dve.memset(cum[:, 1, 0, :], 0.0))
            then(dve.tensor_copy(cum[:, 0, 1:, :], ps_t[:, 0:NT * E].rearrange("p (t e) -> p t e", e=E)))
            at, shift = 0, 1
            while shift < NT:
                then(dve.tensor_copy(cum[:, 1 - at, 1:shift + 1, :], cum[:, at, 1:shift + 1, :]))
                then(dve.tensor_tensor(cum[:, 1 - at, shift + 1:, :], cum[:, at, shift + 1:, :],
                                       cum[:, at, 1:NT + 1 - shift, :], ALU.add))
                at, shift = 1 - at, shift * 2
            then(dve.tensor_tensor(rank[:], ps_r[:, 0:NT * E].rearrange("p (t e) -> p t e", e=E), cum[:, at, 0:NT, :], ALU.add))
            if capacity:
                then(dve.tensor_tensor(sel[:], oh[:, 0], rank[:], ALU.mult))
                then(dve.tensor_reduce(slot_f[:, 0, :], sel[:], AX, ALU.add))
                then(dve.tensor_scalar(slot_f[:, 1, :], slot_f[:, 0, :], float(capacity), None, ALU.is_lt))
                then(dve.tensor_tensor(r["wt"][:, 0, :], r["wt"][:, 0, :], slot_f[:, 1, :], ALU.mult))
                then(dve.tensor_scalar(slot_f[:, 0, :], slot_f[:, 0, :], float(capacity - 1), None, ALU.min))
                then(dve.scalar_tensor_tensor(slot_f[:, 0, :], idx[:, 0, :], float(P), slot_f[:, 0, :], ALU.mult, ALU.add))
                then(dve.tensor_copy(r["slot"][:, 0, :], slot_f[:, 0, :]))
                then(dve.tensor_scalar(slot_f[:, 2, :], slot_f[:, 1, :], -float(n_slots), float(n_slots), ALU.mult, ALU.add))
                then(dve.tensor_tensor(slot_f[:, 3, :], slot_f[:, 2, :], slot_f[:, 0, :], ALU.add))
                then(dve.tensor_copy(r["slot_out"][:, 0, :], slot_f[:, 3, :]))
                dve.sem_inc(slots_ready, 1)
                return
            then(dve.tensor_scalar(ends[:, 2, 0:E], cum[:, at, NT, :], float(P - 1), None, ALU.add))
            then(dve.tensor_copy(cnt_i[:, 0, :], ends[:, 2, 0:E]))
            then(dve.tensor_scalar(cnt_i[:, 1, :], cnt_i[:, 0, :], 7, None, ALU.arith_shift_right))
            then(dve.memset(ends[:, 0, 0:1], 0.0))
            then(dve.memset(ends[:, 1, 0:1], 0.0))
            then(dve.tensor_copy(ends[:, 0, 1:], cnt_i[:, 1, :]))
            a2, shift = 0, 1
            while shift < E:
                then(dve.tensor_copy(ends[:, 1 - a2, 1:shift + 1], ends[:, a2, 1:shift + 1]))
                then(dve.tensor_tensor(ends[:, 1 - a2, shift + 1:], ends[:, a2, shift + 1:], ends[:, a2, 1:E + 1 - shift], ALU.add))
                a2, shift = 1 - a2, shift * 2
            then(dve.tensor_scalar(ends[:, 2, 0:E], ends[:, a2, 0:E], float(P), None, ALU.mult))
            then(dve.tensor_tensor(rank[:], rank[:], ends[:, 2, 0:E].unsqueeze(1).to_broadcast(wide), ALU.add))
            for k in range(choices):
                then(dve.tensor_tensor(sel[:], oh[:, k], rank[:], ALU.mult))
                then(dve.tensor_reduce(slot_f[:, k, :], sel[:], AX, ALU.add))
                then(dve.tensor_copy(r["slot"][:, k, :], slot_f[:, k, :]))
                then(dve.tensor_copy(r["slot_out"][:, k, :], slot_f[:, k, :]))
            dve.sem_inc(slots_ready, 1)
            then(dve.tensor_tensor(tmap[:], tio[:], ends[:, a2, 1:].unsqueeze(1).to_broadcast([P, n_slot_tiles, E]), ALU.is_ge))
            then(dve.tensor_reduce(tsum[:], tmap[:], AX, ALU.add))
            then(dve.tensor_scalar(tsum[:], tsum[:], float(E - 1), None, ALU.min))
            then(dve.tensor_copy(r["tile_expert"][:, 0:n_slot_tiles], tsum[:]))


def loaded4(t, u, n_dmas):
    return (t - u + 4) * (4 * n_dmas)


def mlp_experts_phase(nc, pool, c, r, n_tiles, by_map, func, w, b2, xs_dram, ys_dram):
    E = w.shape[0]
    FC = w.shape[2] // (4 * P + 1)
    F = FC * P
    n_dmas = 3
    with Phase(nc, pool) as ph:
        xs = ph.sb("xs", [P, 4, D])
        ws = ph.sb("ws", [P, 4, 4 * F + FC])
        b2s = ph.sb("b2s", [P, 4, D])
        xT = ph.sb("xT", [P, 2, D])
        hT = ph.sb("hT", [P, 2, F])
        ys = ph.sb("ys", [P, 4, D])
        nbank = (F + BANK - 1) // BANK
        per = BANK // P
        ps_x = ph.ps("ps_x", [P, 2, BANK])
        ps_h = ph.ps("ps_h", [P, 4, BANK])
        ps_y = ph.ps("ps_y", [P, 2, BANK])
        loads = [ph.sem() for _ in range(4)]
        stores = [ph.sem() for _ in range(4)]
        banks = " ".join(f"h{m}" for m in range(nbank))
        pe_x = ph.steps("xT")
        dve_x = ph.steps("xT")
        pe_h = ph.steps(banks)
        act_h = ph.steps(banks)
        pe_y = ph.steps("y")
        dve_y = ph.steps("y")
        block = ph.stack.enter_context(nc.Block())

        @block.sync
        def _(sp):
            def load(t, u):
                sp.wait_ge(pe_y.sem, pe_y.after("y", t - 4))
                sp.wait_ge(dve_y.sem, dve_y.after("y", t - 4))
                e = sp.value_load(r["tile_expert"][0:1, bass.ds(t, 1)], min_val=0, max_val=E - 1) if by_map else t
                sp.dma_start(xs[:, u, :], xs_dram[bass.ds(t * P, P), :]).then_inc(loads[u], 16)
                sp.dma_start(ws[:, u], w[bass.ds(e, 1)].rearrange("a p f -> p (a f)")).then_inc(loads[u], 16)
                sp.dma_start(b2s[:, u, :], b2[bass.ds(e, 1), :].to_broadcast([P, D])).then_inc(loads[u], 16)

            def store(t, u):
                sp.wait_ge(dve_y.sem, dve_y.after("y", t))
                sp.dma_start(ys_dram[bass.ds(t * P, P), :], ys[:, u, :]).then_inc(stores[u], 16)

            for u in range(4):
                sp.sem_inc(stores[u], 16)
            pipeline(sp, n_tiles, 4, (4, store), (0, load))
            for u in range(4):
                sp.wait_ge(stores[u], 4 * n_tiles + 16)

        @block.tensor
        def _(pe):
            for s in (pe_x, pe_h, pe_y):
                s.open(pe)

            def transposes(t, u):
                pe.wait_ge(loads[u], loaded4(t, u, n_dmas))
                pe.wait_ge(dve_x.sem, dve_x.after("xT", t - 2))
                for k in range(KD):
                    ins = pe.transpose(ps_x[:, u % 2, k * P:(k + 1) * P], xs[:, u, k * P:(k + 1) * P], c["ident"][:])
                ins.then_inc(pe_x.sem, 1)

            def hidden(t, u):
                pe.wait_ge(dve_x.sem, dve_x.after("xT", t))
                for f in range(FC):
                    if f % per == 0:
                        pe.wait_ge(act_h.sem, act_h.after(f"h{f // per}", t - 2))
                    o = ps_h[:, (u % 2) * 2 + f // per, (f % per) * P:(f % per + 1) * P]
                    for k in range(KD):
                        ins = pe.matmul(o, ws[:, u, k * F + f * P:k * F + (f + 1) * P], xT[:, u % 2, k * P:(k + 1) * P],
                                        start=(k == 0), stop=(k == KD - 1))
                    if f % per == per - 1:
                        ins.then_inc(pe_h.sem, 1)

            def outputs(t, u):
                pe.wait_ge(dve_y.sem, dve_y.after("y", t - 2))
                w2 = KD * F + FC
                for f in range(FC):
                    if f % per == 0:
                        pe.wait_ge(act_h.sem, act_h.after(f"h{f // per}", t))
                    ins = pe.matmul(ps_y[:, u % 2, 0:D], hT[:, u % 2, f * P:(f + 1) * P],
                                    ws[:, u, w2 + f * D:w2 + (f + 1) * D], start=(f == 0), stop=(f == FC - 1))
                ins.then_inc(pe_y.sem, 1)

            pipeline(pe, n_tiles, 4, (0, transposes), (2, outputs), (1, hidden))

        @block.scalar
        def _(act):
            act_h.open(act)

            def hidden(t, u):
                act.wait_ge(pe_y.sem, pe_y.after("y", t - 2))
                for f in range(FC):
                    if f % per == 0:
                        act.wait_ge(pe_h.sem, pe_h.after(f"h{f // per}", t))
                    o = ps_h[:, (u % 2) * 2 + f // per, (f % per) * P:(f % per + 1) * P]
                    ins = act.activation(hT[:, u % 2, f * P:(f + 1) * P], o, func,
                                         bias=ws[:, u, KD * F + f:KD * F + f + 1])
                    if f % per == per - 1:
                        ins.then_inc(act_h.sem, 1)

            pipeline(act, n_tiles, 4, (0, hidden))

        @block.vector
        def _(dve):
            dve_x.open(dve)
            dve_y.open(dve)

            def transposed(t, u):
                dve.wait_ge(pe_x.sem, pe_x.after("xT", t))
                dve.wait_ge(pe_h.sem, pe_h.after(f"h{nbank - 1}", t - 2))
                dve.tensor_copy(xT[:, u % 2, :], ps_x[:, u % 2, 0:D]).then_inc(dve_x.sem, 1)

            def outputs(t, u):
                dve.wait_ge(pe_y.sem, pe_y.after("y", t))
                dve.wait_ge(stores[u], loaded4(t, u, 1))
                dve.tensor_tensor(ys[:, u, :], ps_y[:, u % 2, 0:D], b2s[:, u, :], ALU.add).then_inc(dve_y.sem, 1)

            pipeline(dve, n_tiles, 4, (0, transposed), (2, outputs))


def glu_experts_phase(nc, pool, c, r, n_tiles, w, xs_dram, ys_dram):
    E = w.shape[0]
    M = (w.shape[2] - D) // (2 * KD)
    n_dmas = 2
    with Phase(nc, pool) as ph:
        xs = ph.sb("xs", [P, 4, D])
        ws = ph.sb("ws", [P, 4, w.shape[2]])
        xT = ph.sb("xT", [P, 2, D])
        small = ph.sb("small", [P, 2, P])
        lr = ph.sb("lr", [P, 2, P])
        hT = ph.sb("hT", [P, 2, P])
        ys = ph.sb("ys", [P, 4, D])
        ps_x = ph.ps("ps_x", [P, 2, BANK])
        ps_g = ph.ps("ps_g", [P, 2, BANK])
        ps_u = ph.ps("ps_u", [P, 2, BANK])
        ps_y = ph.ps("ps_y", [P, 2, BANK])
        loads = [ph.sem() for _ in range(4)]
        stores = [ph.sem() for _ in range(4)]
        pe_x = ph.steps("xT")
        act_x = ph.steps("xT")
        pe_h = ph.steps("gate up")
        act_h = ph.steps("hundredth")
        dve_h = ph.steps("leaky h")
        pe_y = ph.steps("y")
        act_y = ph.steps("y")
        block = ph.stack.enter_context(nc.Block())

        @block.sync
        def _(sp):
            def load(t, u):
                sp.wait_ge(pe_y.sem, pe_y.after("y", t - 4))
                e = sp.value_load(r["tile_expert"][0:1, bass.ds(t, 1)], min_val=0, max_val=E - 1)
                sp.dma_start(xs[:, u, :], xs_dram[bass.ds(t * P, P), :]).then_inc(loads[u], 16)
                sp.dma_start(ws[:, u], w[bass.ds(e, 1)].rearrange("a p f -> p (a f)")).then_inc(loads[u], 16)

            def store(t, u):
                sp.wait_ge(act_y.sem, act_y.after("y", t))
                sp.dma_start(ys_dram[bass.ds(t * P, P), :], ys[:, u, :]).then_inc(stores[u], 16)

            for u in range(4):
                sp.sem_inc(stores[u], 16)
            pipeline(sp, n_tiles, 4, (0, load), (4, store))
            for u in range(4):
                sp.wait_ge(stores[u], 4 * n_tiles + 16)

        @block.tensor
        def _(pe):
            for s in (pe_x, pe_h, pe_y):
                s.open(pe)

            def transposes(t, u):
                pe.wait_ge(loads[u], loaded4(t, u, n_dmas))
                pe.wait_ge(act_x.sem, act_x.after("xT", t - 2))
                for k in range(KD):
                    ins = pe.transpose(ps_x[:, u % 2, k * P:(k + 1) * P], xs[:, u, k * P:(k + 1) * P], c["ident"][:])
                ins.then_inc(pe_x.sem, 1)

            def hidden(t, u):
                pe.wait_ge(act_x.sem, act_x.after("xT", t))
                for m, (ps, freed) in enumerate(((ps_g, "leaky"), (ps_u, "h"))):
                    pe.wait_ge(dve_h.sem, dve_h.after(freed, t - 2))
                    for k in range(KD):
                        at = (m * KD + k) * M
                        ins = pe.matmul(ps[:, u % 2, 0:P], ws[:, u, at:at + M], xT[:, u % 2, k * P:(k + 1) * P],
                                        start=(k == 0), stop=(k == KD - 1))
                    ins.then_inc(pe_h.sem, 1)

            def outputs(t, u):
                pe.wait_ge(dve_h.sem, dve_h.after("h", t))
                pe.wait_ge(act_y.sem, act_y.after("y", t - 2))
                pe.matmul(ps_y[:, u % 2, 0:D], hT[:, u % 2, :], ws[:, u, 2 * KD * M:], start=True,
                          stop=True).then_inc(pe_y.sem, 1)

            pipeline(pe, n_tiles, 4, (0, transposes), (2, outputs), (1, hidden))

        @block.scalar
        def _(act):
            for s in (act_x, act_h, act_y):
                s.open(act)

            def transposed(t, u):
                act.wait_ge(pe_x.sem, pe_x.after("xT", t))
                act.wait_ge(pe_h.sem, pe_h.after("up", t - 2))
                act.activation(xT[:, u % 2, :], ps_x[:, u % 2, 0:D], ACT.Copy).then_inc(act_x.sem, 1)

            def hundredth(t, u):
                act.wait_ge(pe_h.sem, pe_h.after("gate", t))
                act.wait_ge(dve_h.sem, dve_h.after("leaky", t - 2))
                act.activation(small[:, u % 2, :], ps_g[:, u % 2, 0:P], ACT.Copy, scale=0.01).then_inc(act_h.sem, 1)

            def outputs(t, u):
                act.wait_ge(pe_y.sem, pe_y.after("y", t))
                act.wait_ge(stores[u], loaded4(t, u, 1))
                act.activation(ys[:, u, :], ps_y[:, u % 2, 0:D], ACT.Copy).then_inc(act_y.sem, 1)

            pipeline(act, n_tiles, 4, (0, transposed), (2, outputs), (1, hundredth))

        @block.vector
        def _(dve):
            dve_h.open(dve)

            def hidden(t, u):
                dve.wait_ge(act_h.sem, act_h.after("hundredth", t))
                dve.tensor_tensor(lr[:, u % 2, :], small[:, u % 2, :], ps_g[:, u % 2, 0:P], ALU.max).then_inc(dve_h.sem, 1)
                dve.wait_ge(dve_h.sem, dve_h.after("leaky", t))
                dve.wait_ge(pe_h.sem, pe_h.after("up", t))
                dve.wait_ge(pe_y.sem, pe_y.after("y", t - 2))
                dve.tensor_tensor(hT[:, u % 2, :], lr[:, u % 2, :], ps_u[:, u % 2, 0:P], ALU.mult).then_inc(dve_h.sem, 1)

            pipeline(dve, n_tiles, 4, (0, hidden))


def combine_phase(nc, pool, c, gather, out=None):
    G = 4
    with Phase(nc, pool) as ph:
        yg = ph.sb("yg", [P, gather.choices, NT, D])
        dve_g = ph.steps(" ".join(f"y{k}" for k in range(gather.choices)))
        stored = ph.sem()
        block = ph.stack.enter_context(nc.Block())

        @block.gpsimd
        def _(gp):
            gather.rows(gp, yg)

        @block.vector
        def _(dve):
            dve_g.open(dve)
            for t in range(NT):
                gather.add(dve, t, yg, dve_g)

        if out is not None:
            @block.sync
            def _(sp):
                for t in range(0, NT, G):
                    sp.wait_ge(dve_g.sem, dve_g.after(f"y{gather.choices - 1}", t + G - 1))
                    sp.dma_start(out.rearrange("b (t p) d -> p (b t) d", p=P)[:, t:t + G, :],
                                 gather.dst[:, t:t + G, :]).then_inc(stored, 16)
                sp.wait_ge(stored, 16 * (NT // G))


def bias_table_phase(nc, pool, c, w, table_dram, spread_dram, spread_done):
    NTP = S // P
    with Phase(nc, pool) as ph:
        pos_i = ph.sb("pos_i", [P, NTP], I32)
        pos = ph.sb("pos", [P, NTP])
        rows = {n: ph.sb(n, [P, D]) for n in ("w0", "b0", "g0", "b1", "g1")}
        w1 = ph.sb("w1", [P, KD, D])
        w2 = ph.sb("w2", [P, KD, H])
        b2 = ph.sb("b2", [H, 1])
        h = ph.sb("h", [P, NTP, D])
        hT = ph.sb("hT", [P, KD, S])
        stats = ph.sb("stats", [P, NTP, 6])
        mv = ph.sb("mv", [P, NTP, 2])
        sd = ph.sb("sd", [P, NTP])
        rstd = ph.sb("rstd", [P, NTP])
        table = ph.sb("table", [H, S + P])
        ps_t = ph.ps("ps_t", [P, KD, S])
        ps_h = ph.ps("ps_h", [P, NTP, D])
        loaded, made, v, spread, moments, rooted, normed, silued, turned, out_t, product, stored = (ph.sem() for _ in range(12))
        block = ph.stack.enter_context(nc.Block())
        n_loads = 16 * 8
        count = {"v": 0}

        @block.sync
        def _(sp):
            for n in rows:
                sp.dma_start(rows[n][:], row(w[n], D)).then_inc(loaded, 16)
            sp.dma_start(w1[:], w["w1"].rearrange("(k p) n -> p k n", p=P)).then_inc(loaded, 16)
            sp.dma_start(w2[:], w["w2"].rearrange("(k p) n -> p k n", p=P)).then_inc(loaded, 16)
            sp.dma_start(b2[:], w["b2"].rearrange("(h a) -> h a", a=1)).then_inc(loaded, 16)
            sp.wait_ge(product, 2)
            sp.wait_ge(v, 1)
            sp.dma_start(table_dram, table[:]).then_inc(stored, 16)
            sp.wait_ge(stored, 16)
            sp.dma_start(spread_dram, bass.AP(table_dram.tensor, table_dram.offset + P - 1,
                                              [[S + P, H], [-1, P], [1, S]])).then_inc(spread_done, 16)

        @block.gpsimd
        def _(gp):
            gp.iota(pos_i[:], pattern=[[-P, NTP]], base=S - 1, channel_multiplier=-1).then_inc(made, 1)

        @block.vector
        def _(dve):
            def then(ins):
                count["v"] += 1
                ins.then_inc(v, 1)
                dve.wait_ge(v, count["v"])

            def norm(gain, n):
                for t in range(NTP):
                    ins = dve.bn_stats(stats[:, t, :], h[:, t, :])
                then(ins)
                for t in range(NTP):
                    ins = dve.bn_aggr(mv[:, t, :], stats[:, t, :])
                ins.then_inc(moments, 1)
                dve.wait_ge(rooted, n)
                then(dve.reciprocal(rstd[:], sd[:]))
                for t in range(NTP):
                    ins = dve.tensor_scalar(h[:, t, :], h[:, t, :], mv[:, t, 0:1], rstd[:, t:t + 1], ALU.subtract, ALU.mult)
                then(ins)
                dve.tensor_tensor(h[:], h[:], rows[gain][:].unsqueeze(1).to_broadcast([P, NTP, D]),
                                  ALU.mult).then_inc(normed, 1)

            then(dve.memset(table[:, S:], 0.0))
            dve.wait_ge(made, 1)
            then(dve.tensor_copy(pos[:], pos_i[:]))
            dve.wait_ge(loaded, n_loads)
            for t in range(NTP):
                ins = dve.scalar_tensor_tensor(h[:, t, :], rows["w0"][:], pos[:, t:t + 1], rows["b0"][:], ALU.mult, ALU.add)
            then(ins)
            norm("g0", 1)
            dve.wait_ge(turned, 1)
            dve.tensor_copy(hT[:, 1, :], ps_t[:, 1, :]).then_inc(out_t, 1)
            dve.wait_ge(product, 1)
            then(dve.tensor_tensor(h[:], ps_h[:], rows["b1"][:].unsqueeze(1).to_broadcast([P, NTP, D]), ALU.add))
            norm("g1", 2)
            dve.wait_ge(turned, 2)
            dve.tensor_copy(hT[:, 1, :], ps_t[:, 1, :]).then_inc(out_t, 1)

        @block.scalar
        def _(act):
            for n in (1, 2):
                act.wait_ge(moments, n)
                act.activation(sd[:], mv[:, :, 1], ACT.Sqrt, bias=c["eps"][:, 0:1]).then_inc(rooted, 1)
                act.wait_ge(normed, n)
                act.activation(h[:], h[:], ACT.Silu).then_inc(silued, 1)
                act.wait_ge(turned, n)
                act.activation(hT[:, 0, :], ps_t[:, 0, :], ACT.Copy).then_inc(out_t, 1)
            act.wait_ge(spread, 1)
            act.wait_ge(loaded, n_loads)
            act.activation(table[:, 0:S], ps_h[0:H].rearrange("p a d -> p (a d)")[:, 0:S], ACT.Identity,
                           bias=b2[:, 0:1]).then_inc(product, 1)

        @block.tensor
        def _(pe):
            pe.wait_ge(loaded, n_loads)
            for n in (1, 2):
                pe.wait_ge(silued, n)
                for k in range(KD):
                    for t in range(NTP):
                        ins = pe.transpose(ps_t[:, k, t * P:(t + 1) * P], h[:, t, k * P:(k + 1) * P], c["ident"][:])
                ins.then_inc(turned, 1)
                pe.wait_ge(out_t, 2 * n)
                if n == 1:
                    for t in range(NTP):
                        for k in range(KD):
                            ins = pe.matmul(ps_h[:, t, :], hT[:, k, t * P:(t + 1) * P], w1[:, k, :], start=(k == 0),
                                            stop=(k == KD - 1))
                    ins.then_inc(product, 1)
                else:
                    flat = ps_h[0:H].rearrange("p a d -> p (a d)")
                    for lo in range(0, S, BANK):
                        for k in range(KD):
                            ins = pe.matmul(flat[:, lo:lo + BANK], w2[:, k, :], hT[:, k, lo:lo + BANK], start=(k == 0),
                                            stop=(k == KD - 1))
                    ins.then_inc(spread, 1)


def product_key_phase(nc, pool, c, w):
    HR, NK, TOP = 4, 64, 8
    NE = 1024
    NA = NE // NK
    FC = NE // P
    with Phase(nc, pool) as ph:
        wq = ph.sb("wq", [P, KD, 4 * P])
        kbd = ph.sb("kbd", [P, 4, P])
        wg = ph.sb("wg", [P, KD, NE])
        wu = ph.sb("wu", [P, KD, NE])
        wd = ph.sb("wd", [P, FC, D])
        down = ph.sb("down", [P, KD, NE])
        up = ph.sb("up", [P, FC, D])
        bg = ph.sb("bg", [P, FC])
        bu = ph.sb("bu", [P, FC])
        bd = ph.sb("bd", [P, D])
        xs = ph.sb("xs", [P, 2, D])
        xT = ph.sb("xT", [P, 4, KD, P])
        qT = ph.sb("qT", [P, 4 * P])
        sim = ph.sb("sim", [P, 2, HR, NK])
        s8 = ph.sb("s8", [P, 2, HR, TOP])
        top = ph.sb("top", [P, HR])
        s8x = ph.sb("s8x", [P, HR, TOP])
        simx = ph.sb("simx", [P, HR, NA])
        cand = ph.sb("cand", [P, HR, TOP, TOP])
        t8 = ph.sb("t8", [P, 2, HR, TOP])
        e8 = ph.sb("e8", [P, 2, HR, TOP])
        ss = ph.sb("ss", [P, 2, HR, NE])
        es = ph.sb("es", [P, 2, HR, NE])
        sum8 = ph.sb("sum8", [P, HR])
        rinv = ph.sb("rinv", [P, HR])
        kept = ph.sb("kept", [P, NE])
        inside = ph.sb("inside", [P, HR])
        rest = ph.sb("rest", [P, HR])
        rest1 = ph.sb("rest1", [P, 1])
        co = ph.sb("co", [P, NE])
        sw = ph.sb("sw", [P, NE])
        gm = ph.sb("gm", [P, NE])
        gT = ph.sb("gT", [P, NE])
        sg = ph.sb("sg", [P, NE])
        hT = ph.sb("hT", [P, NE])
        yb = ph.sb("yb", [P, D])
        ps_x = ph.ps("ps_x", [P, BANK])
        ps_q = ph.ps("ps_q", [P, BANK])
        ps_s = ph.ps("ps_s", [P, BANK])
        ps_w = ph.ps("ps_w", [P, 2 * BANK])
        ps_gu = ph.ps("ps_gu", [P, 2, BANK])
        ps_y = ph.ps("ps_y", [P, BANK])

        weights, zeroed = ph.sem(), ph.sem()
        gp_x = ph.steps("x")
        pe_x = ph.steps("xT")
        act_x = ph.steps("xT")
        pe_q = ph.steps("q")
        act_q = ph.steps("qT")
        pe_s = ph.steps("sim")
        dve_a = ph.steps("sim ready s8 top s8x simx cand ready2 t8")
        gp_a = ph.steps("ss")
        act_e = ph.steps("e8 es")
        dve_m = ph.steps("sum8 rinv " + " ".join(f"wait{h} kept{h} co{h}" for h in range(HR)) + " rest restr rest1 co")
        pe_b = ph.steps("w gu0 gu1 gu2 gu3 gT")
        act_b = ph.steps("sw sg0 sg1 sg2 sg3 gT")
        dve_b = ph.steps("gm h0 h1 h2 h3 gT")
        pe_y = ph.steps("y")
        dve_y = ph.steps("yb x")
        block = ph.stack.enter_context(nc.Block())
        loads = [(wq[:], w["Wq"].rearrange("(k p) n -> p k n", p=P)), (wg[:], w["Wg"].rearrange("(k p) n -> p k n", p=P)),
                 (wu[:], w["Wu"].rearrange("(k p) n -> p k n", p=P)), (wd[:], w["Wd"].rearrange("(k p) n -> p k n", p=P)),
                 (down[:], w["downT"].rearrange("(k p) n -> p k n", p=P)), (up[:], w["up"].rearrange("(k p) n -> p k n", p=P)),
                 (bg[:], w["bgT"]), (bu[:], w["buT"]), (bd[:], row(w["bd"], D))]
        for q in range(2):
            for h in range(HR):
                half = slice((h % 2) * NK, (h % 2 + 1) * NK)
                loads.append((kbd[half, q * 2 + h // 2, half], w["keysT"][q, h]))
        n_loads = 16 * len(loads)

        @block.sync
        def _(sp):
            sp.wait_ge(zeroed, 1)
            for dst, src in loads:
                sp.dma_start(dst, src).then_inc(weights, 16)
            sp.wait_ge(weights, n_loads)

        @block.gpsimd
        def _(gp):
            gp_x.open(gp)
            gp_a.open(gp)
            gp.memset(kbd[:], 0.0).then_inc(zeroed, 1)

            def stage(t, u):
                gp.wait_ge(pe_x.sem, pe_x.after("xT", t - 2))
                gp.tensor_copy(xs[:, u % 2, :], at(c["cur"], t)).then_inc(gp_x.sem, 1)

            def sums(t, u):
                gp.wait_ge(dve_a.sem, dve_a.after("simx", t))
                gp.wait_ge(dve_m.sem, dve_m.after(f"kept{HR - 1}", t - 2))
                gp.wait_ge(act_e.sem, act_e.after("es", t - 2))
                gp.tensor_tensor(ss[:, u % 2].rearrange("p h (a b) -> p h a b", b=NK),
                                 simx[:].unsqueeze(3).to_broadcast([P, HR, NA, NK]),
                                 sim[:, 1].unsqueeze(2).to_broadcast([P, HR, NA, NK]), ALU.add).then_inc(gp_a.sem, 1)

            pipeline(gp, NT, 4, (0, stage), (1, sums))

        @block.tensor
        def _(pe):
            for s in (pe_x, pe_q, pe_s, pe_b, pe_y):
                s.open(pe)
            pe.wait_ge(weights, n_loads)

            def transposes(t, u):
                pe.wait_ge(gp_x.sem, gp_x.after("x", t))
                pe.wait_ge(act_x.sem, act_x.after("xT", t - 1))
                for k in range(KD):
                    ins = pe.transpose(ps_x[:, k * P:(k + 1) * P], xs[:, u % 2, k * P:(k + 1) * P], c["ident"][:])
                ins.then_inc(pe_x.sem, 1)

            def queries(t, u):
                pe.wait_ge(act_x.sem, act_x.after("xT", t))
                pe.wait_ge(act_q.sem, act_q.after("qT", t - 1))
                for m in range(4):
                    for k in range(KD):
                        ins = pe.matmul(ps_q[:, m * P:(m + 1) * P], wq[:, k, m * P:(m + 1) * P], xT[:, u, k, :],
                                        start=(k == 0), stop=(k == KD - 1))
                ins.then_inc(pe_q.sem, 1)

            def similarities(t, u):
                pe.wait_ge(act_q.sem, act_q.after("qT", t))
                pe.wait_ge(dve_a.sem, dve_a.after("sim", t - 1))
                for m in range(4):
                    ins = pe.matmul(ps_s[:, m * P:(m + 1) * P], qT[:, m * P:(m + 1) * P], kbd[:, m, :], start=True, stop=True)
                ins.then_inc(pe_s.sem, 1)

            def retrieval(t, u):
                pe.wait_ge(act_b.sem, act_b.after("gT", t - 1))
                pe.wait_ge(dve_b.sem, dve_b.after("gT", t - 1))
                for lo in range(0, NE, BANK):
                    for k in range(KD):
                        ins = pe.matmul(ps_w[:, lo:lo + BANK], xT[:, u, k, :], down[:, k, lo:lo + BANK],
                                        start=(k == 0), stop=(k == KD - 1))
                ins.then_inc(pe_b.sem, 1)

            def hidden(t, u):
                for q in range(4):
                    pe.wait_ge(dve_b.sem, dve_b.after(f"h{(q + 2) % 4}", t - 1 if q < 2 else t))
                    for j, ww in enumerate((wg, wu)):
                        for f in range(2):
                            fc = 2 * q + f
                            for k in range(KD):
                                ins = pe.matmul(ps_gu[:, q % 2, (2 * j + f) * P:(2 * j + f + 1) * P],
                                                ww[:, k, fc * P:(fc + 1) * P], xT[:, u, k, :], start=(k == 0),
                                                stop=(k == KD - 1))
                    ins.then_inc(pe_b.sem, 1)
                pe.wait_ge(dve_b.sem, dve_b.after("gm", t))
                for k in range(FC):
                    ins = pe.transpose(ps_w[:, k * P:(k + 1) * P], gm[:, k * P:(k + 1) * P], c["ident"][:])
                ins.then_inc(pe_b.sem, 1)

            def outputs(t, u):
                pe.wait_ge(dve_b.sem, dve_b.after("h3", t))
                pe.wait_ge(dve_y.sem, dve_y.after("yb", t - 1))
                for k in range(FC):
                    pe.matmul(ps_y[:, 0:D], hT[:, k * P:(k + 1) * P], wd[:, k, :], start=(k == 0), stop=False)
                pe.wait_ge(act_b.sem, act_b.after("gT", t))
                pe.wait_ge(dve_b.sem, dve_b.after("gT", t))
                for k in range(FC):
                    ins = pe.matmul(ps_y[:, 0:D], gT[:, k * P:(k + 1) * P], up[:, k, :], start=False, stop=(k == FC - 1))
                ins.then_inc(pe_y.sem, 1)

            pipeline(pe, NT, 4, (0, transposes), (3, outputs), (0, queries), (2, retrieval), (0, similarities), (2, hidden))

        @block.scalar
        def _(act):
            for s in (act_x, act_q, act_e, act_b):
                s.open(act)
            act.wait_ge(weights, n_loads)

            def transposed(t, u):
                act.wait_ge(pe_x.sem, pe_x.after("xT", t))
                act.wait_ge(pe_b.sem, pe_b.after("gu3", t - 4))
                act.activation(xT[:, u].rearrange("p k n -> p (k n)"), ps_x[:, 0:D], ACT.Copy).then_inc(act_x.sem, 1)

            def exponentials(t, u):
                act.wait_ge(dve_a.sem, dve_a.after("t8", t))
                act.wait_ge(dve_m.sem, dve_m.after("sum8", t - 2))
                act.activation(e8[:, u % 2], t8[:, u % 2], ACT.Exp).then_inc(act_e.sem, 1)
                act.wait_ge(gp_a.sem, gp_a.after("ss", t))
                act.wait_ge(dve_m.sem, dve_m.after(f"kept{HR - 1}", t - 2))
                act.activation(es[:, u % 2], ss[:, u % 2], ACT.Exp).then_inc(act_e.sem, 1)

            def queries(t, u):
                act.wait_ge(pe_q.sem, pe_q.after("q", t))
                act.wait_ge(pe_s.sem, pe_s.after("sim", t - 1))
                act.activation(qT[:], ps_q[:], ACT.Copy).then_inc(act_q.sem, 1)

            def hidden(t, u):
                act.wait_ge(pe_b.sem, pe_b.after("w", t))
                act.wait_ge(dve_b.sem, dve_b.after("gm", t - 1))
                act.activation(sw[:], ps_w[:], ACT.Silu).then_inc(act_b.sem, 1)
                for q in range(4):
                    act.wait_ge(pe_b.sem, pe_b.after(f"gu{q}", t))
                    act.wait_ge(dve_b.sem, dve_b.after(f"h{q}", t - 1))
                    for f in range(2):
                        fc = 2 * q + f
                        ins = act.activation(sg[:, fc * P:(fc + 1) * P], ps_gu[:, q % 2, f * P:(f + 1) * P], ACT.Silu,
                                             bias=bg[:, fc:fc + 1])
                    ins.then_inc(act_b.sem, 1)
                act.wait_ge(pe_b.sem, pe_b.after("gT", t))
                act.wait_ge(pe_y.sem, pe_y.after("y", t - 1))
                act.activation(gT[:, 0:BANK], ps_w[:, 0:BANK], ACT.Copy).then_inc(act_b.sem, 1)

            pipeline(act, NT, 4, (0, transposed), (1, exponentials), (0, queries), (2, hidden))

        @block.vector
        def _(dve):
            for s in (dve_a, dve_m, dve_b, dve_y):
                s.open(dve)
            dve.wait_ge(weights, n_loads)

            def search(t, u):
                def own(name):
                    dve.wait_ge(dve_a.sem, dve_a.after(name, t))

                dve.wait_ge(pe_s.sem, pe_s.after("sim", t))
                dve.wait_ge(gp_a.sem, gp_a.after("ss", t - 1))
                dve.tensor_copy(sim[:].rearrange("p q h n -> p (q h n)"), ps_s[:]).then_inc(dve_a.sem, 1)
                own("sim")
                dve.sem_inc(dve_a.sem, 1)
                for q in range(2):
                    for h in range(HR):
                        ins = dve.max(s8[:, q, h, :], sim[:, q, h, :])
                ins.then_inc(dve_a.sem, 1)

            def search_sums(t, u):
                def own(name):
                    dve.wait_ge(dve_a.sem, dve_a.after(name, t))

                own("s8")
                dve.tensor_tensor(top[:], s8[:, 0, :, 0], s8[:, 1, :, 0], ALU.add).then_inc(dve_a.sem, 1)
                own("top")
                dve.tensor_tensor(s8x[:], s8[:, 0], bc(top[:], [P, HR, TOP]), ALU.subtract).then_inc(dve_a.sem, 1)
                dve.tensor_tensor(simx[:], sim[:, 0, :, 0:NA], bc(top[:], [P, HR, NA]), ALU.subtract).then_inc(dve_a.sem, 1)
                own("s8x")
                dve.tensor_tensor(cand[:], s8x[:].unsqueeze(3).to_broadcast([P, HR, TOP, TOP]),
                                  s8[:, 1].unsqueeze(2).to_broadcast([P, HR, TOP, TOP]), ALU.add).then_inc(dve_a.sem, 1)
                own("cand")
                dve.sem_inc(dve_a.sem, 1)
                for h in range(HR):
                    ins = dve.max(t8[:, u % 2, h, :], cand[:, h].rearrange("p a b -> p (a b)"))
                ins.then_inc(dve_a.sem, 1)

            def coefficients(t, u, h):
                def own(name):
                    dve.wait_ge(dve_m.sem, dve_m.after(name, t))

                if h == 0:
                    dve.wait_ge(act_e.sem, act_e.after("es", t))
                    dve.tensor_reduce(sum8[:], e8[:, u % 2], AX, ALU.add).then_inc(dve_m.sem, 1)
                    own("sum8")
                    dve.reciprocal(rinv[:], sum8[:]).then_inc(dve_m.sem, 1)
                    own("rinv")
                else:
                    own(f"co{h - 1}")
                dve.sem_inc(dve_m.sem, 1)
                dve.scalar_tensor_tensor(kept[:], ss[:, u % 2, h], t8[:, u % 2, h, TOP - 1:TOP], es[:, u % 2, h], ALU.is_ge, ALU.mult,
                                         accum_out=inside[:, h:h + 1]).then_inc(dve_m.sem, 1)
                own(f"kept{h}")
                if h == 0:
                    dve.wait_ge(dve_b.sem, dve_b.after("gm", t - 1))
                    dve.tensor_scalar(co[:], kept[:], rinv[:, 0:1], None, ALU.mult).then_inc(dve_m.sem, 1)
                else:
                    dve.scalar_tensor_tensor(co[:], kept[:], rinv[:, h:h + 1], co[:], ALU.mult, ALU.add).then_inc(dve_m.sem, 1)
                if h == HR - 1:
                    dve.tensor_tensor(rest[:], sum8[:], inside[:], ALU.subtract).then_inc(dve_m.sem, 1)
                    own("rest")
                    dve.tensor_tensor(rest[:], rest[:], rinv[:], ALU.mult).then_inc(dve_m.sem, 1)
                    own("restr")
                    dve.tensor_reduce(rest1[:], rest[:], AX, ALU.add).then_inc(dve_m.sem, 1)
                    own("rest1")
                    dve.tensor_tensor(co[:, NE - 1:NE], co[:, NE - 1:NE], rest1[:], ALU.add).then_inc(dve_m.sem, 1)

            def hidden(t, u, q):
                dve.wait_ge(act_b.sem, act_b.after(f"sg{q}", t))
                if q == 0:
                    dve.wait_ge(pe_y.sem, pe_y.after("y", t - 1))
                for f in range(2):
                    fc = 2 * q + f
                    ins = dve.scalar_tensor_tensor(hT[:, fc * P:(fc + 1) * P], ps_gu[:, q % 2, (2 + f) * P:(3 + f) * P],
                                                   bu[:, fc:fc + 1], sg[:, fc * P:(fc + 1) * P], ALU.add, ALU.mult)
                ins.then_inc(dve_b.sem, 1)

            def all_coefficients(t, u):
                for h in range(HR):
                    coefficients(t, u, h)

            def weighed(t, u):
                dve.wait_ge(act_b.sem, act_b.after("sw", t))
                dve.wait_ge(dve_m.sem, dve_m.after("co", t))
                dve.wait_ge(pe_b.sem, pe_b.after("gT", t - 1))
                dve.tensor_tensor(gm[:], sw[:], co[:], ALU.mult).then_inc(dve_b.sem, 1)

            def first_hidden(t, u):
                hidden(t, u, 0)
                hidden(t, u, 1)

            def last_hidden(t, u):
                hidden(t, u, 2)
                hidden(t, u, 3)
                dve.wait_ge(pe_b.sem, pe_b.after("gT", t))
                dve.tensor_copy(gT[:, BANK:], ps_w[:, BANK:]).then_inc(dve_b.sem, 1)

            def outputs(t, u):
                x_t = at(c["x"], t)
                dve.wait_ge(pe_y.sem, pe_y.after("y", t))
                dve.tensor_tensor(yb[:], ps_y[:, 0:D], bd[:], ALU.add).then_inc(dve_y.sem, 1)
                dve.wait_ge(dve_y.sem, dve_y.after("yb", t))
                dve.tensor_tensor(x_t, x_t, yb[:], ALU.add).then_inc(dve_y.sem, 1)

            pipeline(dve, NT, 4, (2, all_coefficients), (3, outputs), (2, weighed), (0, search), (2, first_hidden),
                     (0, search_sums), (2, last_hidden))


def routing(nc, ctx, layer):
    def sb(name, shape, dt=F32):
        return ctx.enter_context(nc.sbuf_tensor(f"{name}_{layer}", shape, dt))

    return {"logits": sb("logits", [P, NT, 16]), "wt": sb("wt", [P, 2, NT]), "slot": sb("slot", [P, 2, NT], U32),
            "slot_out": sb("slot_out", [P, 2, NT], U32), "tile_expert": sb("tile_expert", [P, N_SLOT_TILES[2]], I32),
            "acc": sb("acc", [P, NT, D])}


def clear_slots(nc, pool, xs_dram, n):
    with Phase(nc, pool) as ph:
        zero = ph.sb("zero", [P, D])
        zeroed, stored = ph.sem(), ph.sem()
        block = ph.stack.enter_context(nc.Block())

        @block.vector
        def _(dve):
            dve.memset(zero[:], 0.0).then_inc(zeroed, 1)

        @block.sync
        def _(sp):
            sp.wait_ge(zeroed, 1)
            sp.dma_start(xs_dram.rearrange("(t p) d -> p t d", p=P),
                         zero[:].unsqueeze(1).to_broadcast([P, n, D])).then_inc(stored, 16)
            sp.wait_ge(stored, 16)


def attention_store(nc, ctx, layer):
    def sb(name, shape, dt=F32):
        return ctx.enter_context(nc.sbuf_tensor(f"{name}_{layer}", shape, dt))

    return {
        "qo": sb("qo", [P, NT, NP, P]), "khi": sb("khi", [P, T], F32R), "klo": sb("klo", [P, T], F32R), "v": sb("v", [P, NT, DH]),
        "nk": sb("nk", [P, DH]), "nsn": sb("nsn", [P, NT, H]), "nv": sb("nv", [P, DH]), "km": sb("km", [P, B, S], BF16),
        "dm": sb("dm", [P, B * S], BF16),
    }


def constants(nc, ctx):
    def sb(name, shape, dt=F32):
        return ctx.enter_context(nc.sbuf_tensor(name, shape, dt))

    return {"x": sb("x_sb", [P, NT, D]), "cur": sb("cur_sb", [P, NT, D]), "ident": sb("ident_sb", [P, P]),
            "ident16": sb("ident16", [P, P], BF16), "ones": sb("ones_sb", [P, P]), "eps": sb("eps_sb", [P, 2])}


N_PHASE_SEMS = 40


def semaphore_pool(nc):
    sems = [nc.alloc_semaphore(f"phase{i}") for i in range(N_PHASE_SEMS)]
    return {"sems": sems, "n": 0, "first": sems[0].num}


def build(nc, a, out):
    with ExitStack() as ctx:
        rows_moved = {"sem": nc.alloc_semaphore("rows_moved"), "count": 0}
        rows_in = {"sems": [nc.alloc_semaphore(f"rows_in{t}") for t in range(NT)], "count": 0}
        bias_spread = nc.alloc_semaphore("bias_spread")
        pool = semaphore_pool(nc)
        c = constants(nc, ctx)
        n_rows = N_SLOT_TILES[2] * P
        xs_dram = nc.dram_tensor("slot_rows", (n_rows, D), F32, kind="Internal").ap()
        ys_dram = nc.dram_tensor("slot_outputs", (n_rows, D), F32, kind="Internal").ap()
        table_dram = nc.dram_tensor("bias_table", (H, S + P), F32, kind="Internal").ap()
        spread_dram = nc.dram_tensor("bias_by_partition", (H, P, S), F32, kind="Internal").ap()

        setup(nc, pool, c, a["x"])
        clear_slots(nc, pool, xs_dram, N_SLOT_TILES[2])
        bias_table_phase(nc, pool, c, {n: a["L2_cond_" + n] for n in ("w0", "b0", "g0", "w1", "b1", "g1", "w2", "b2")},
                         table_dram, spread_dram, bias_spread)

        def given_bias(h, qt):
            return a["fside_16xSxS_0"][bass.ds(h, 1), qt * P:(qt + 1) * P, 0:(qt + 1) * P].rearrange("a p j -> p (a j)")

        def relative_bias(h, qt):
            first = S - (qt + 1) * P
            return spread_dram[bass.ds(h, 1), :, first:S].rearrange("a p j -> p (a j)")

        def slots_to(choices, dst, base, n_tiles=None):
            return Gather(r, choices, ys_dram, (n_tiles or N_SLOT_TILES[choices]) * P, dst, base, rows_in)

        def cond_moe(layer, gather=None):
            w = {n: a[f"L{layer}_cond_" + n] for n in ("wt", "wg", "sw_gate", "sw_up", "sw_down")}
            logits_phase(nc, pool, c, r, c["x"], w["wt"], None, cond=(a["cond_64"], w["wg"]), halve=True,
                         shared=(w["sw_gate"], w["sw_up"], w["sw_down"]), gather=gather)
            choose_phase(nc, pool, c, r, 8, 2, c["x"], xs_dram, dma_done=rows_moved)
            glu_experts_phase(nc, pool, c, r, N_SLOT_TILES[2], a[f"L{layer}_cond_experts"], xs_dram, ys_dram)

        with ExitStack() as actx:
            att = attention_store(nc, actx, 0)
            null_phase(nc, pool, c, att, a["cond_64"], a["mask_BxS_bk0"])
            qkv_phase(nc, pool, c, att, a["L0_cond_g_in"], a["L0_cond_Wq"], a["L0_cond_Wkv"], a["L0_cond_null_attn_bias"])
            core_phase(nc, pool, c, att, given_bias)
            out_phase(nc, pool, c, att, a["L0_cond_Wo"], a["L0_cond_g_out"])
        with ExitStack() as rctx:
            r = routing(nc, rctx, 0)
            logits_phase(nc, pool, c, r, c["cur"], a["L0_ffn_Wg"], a["L0_ffn_bg"])
            choose_phase(nc, pool, c, r, 16, 1, c["cur"], xs_dram, capacity=T // 16, dma_done=rows_moved)
            mlp_experts_phase(nc, pool, c, r, 16, False, ACT.Relu, a["L0_ffn_experts"],
                              a["L0_ffn_b2"], xs_dram, ys_dram)
            cond_moe(1, gather=slots_to(1, c["x"], c["x"], 16))
            logits_phase(nc, pool, c, r, c["cur"], a["L1_ffn_router_w"], None,
                         gather=slots_to(2, c["cur"], r["acc"]))
            choose_phase(nc, pool, c, r, 8, 2, c["cur"], xs_dram, softmax_all=False, dma_done=rows_moved)
            mlp_experts_phase(nc, pool, c, r, N_SLOT_TILES[2], True, ACT.Gelu, a["L1_ffn_experts"],
                              a["L1_ffn_b2"], xs_dram, ys_dram)
            combine_phase(nc, pool, c, slots_to(2, c["x"], c["x"]))

        with ExitStack() as actx:
            att = attention_store(nc, actx, 2)
            null_phase(nc, pool, c, att, a["cond_64"], a["mask_BxS_bf1"], k_scale=a["L2_cond_k_scale"])
            qkv_phase(nc, pool, c, att, a["L2_cond_g_norm"], a["L2_cond_Wq"], a["L2_cond_Wkv"],
                      a["L2_cond_null_attn_bias"], q_scale=a["L2_cond_q_scale"], k_scale=a["L2_cond_k_scale"])
            core_phase(nc, pool, c, att, relative_bias, bias_made=bias_spread)
            out_phase(nc, pool, c, att, a["L2_cond_Wout"], a["L2_cond_g_out"])
        product_key_phase(nc, pool, c, {
            "Wq": a["L2_ffn_Wq"], "Wg": a["L2_ffn_Wg"], "Wu": a["L2_ffn_Wu"], "Wd": a["L2_ffn_Wd"],
            "downT": a["L2_ffn_down_embed"], "up": a["L2_ffn_up_embed"], "bgT": a["L2_ffn_bg"], "buT": a["L2_ffn_bu"],
            "bd": a["L2_ffn_bd"], "keysT": a["L2_ffn_keys"]})

        with ExitStack() as rctx:
            r = routing(nc, rctx, 3)
            cond_moe(3)
            logits_phase(nc, pool, c, r, c["cur"], a["L3_ffn_gate_w"], None, rms=a["L3_ffn_rms_w"],
                         gather=slots_to(2, c["cur"], r["acc"]))
            choose_phase(nc, pool, c, r, 8, 1, c["cur"], xs_dram, dma_done=rows_moved)
            mlp_experts_phase(nc, pool, c, r, N_SLOT_TILES[1], True, ACT.Silu, a["L3_ffn_experts"],
                              a["L3_ffn_b2"], xs_dram, ys_dram)
            combine_phase(nc, pool, c, slots_to(1, c["x"], c["x"]), out=out)


def _transposed(*axes):
    return lambda v: v.transpose(*axes)


def _by_partition(v):
    w = v.reshape(*v.shape[:-1], -1, P)
    return w.swapaxes(-1, -2)


_LAYOUT = {
    "L0_cond_g_in": _by_partition, "L2_cond_g_norm": _by_partition,
    "L1_cond_wt": _transposed(1, 0), "L1_cond_wg": _transposed(1, 0), "L3_cond_wt": _transposed(1, 0),
    "L3_cond_wg": _transposed(1, 0), "L1_ffn_router_w": _transposed(1, 0), "L3_ffn_gate_w": _transposed(1, 0),
    "L2_ffn_down_embed": _transposed(1, 0), "L2_ffn_bg": _by_partition, "L2_ffn_bu": _by_partition,
    "L2_ffn_keys": _transposed(2, 0, 3, 1),
}


def _rows_by_partition(v):
    E, R, N = v.shape
    return v.reshape(E, R // P, P, N).transpose(0, 2, 1, 3).reshape(E, P, -1)


_TOGETHER = {
    "L0_ffn_experts": [("L0_ffn_W1", _rows_by_partition), ("L0_ffn_b1", _by_partition), ("L0_ffn_W2", _rows_by_partition)],
    "L1_ffn_experts": [("L1_ffn_w1", lambda v: _rows_by_partition(v.transpose(0, 2, 1))), ("L1_ffn_b1", _by_partition),
                       ("L1_ffn_w2", lambda v: _rows_by_partition(v.transpose(0, 2, 1)))],
    "L3_ffn_experts": [("L3_ffn_W1", _rows_by_partition), ("L3_ffn_b1", _by_partition), ("L3_ffn_W2", _rows_by_partition)],
    "L1_cond_experts": [(f"L1_cond_w_{n}", _rows_by_partition) for n in ("gate", "up", "down")],
    "L3_cond_experts": [(f"L3_cond_w_{n}", _rows_by_partition) for n in ("gate", "up", "down")],
}


def kernel(**inputs):
    import numpy as _np
    import concourse.bacc as _bacc
    from concourse import mybir as _mybir
    from concourse.bass_utils import run_bass_kernel_spmd as _run

    nc = _bacc.Bacc("TRN2", target_bir_lowering=False, num_devices=1)
    arrays, args = {}, {}
    laid_out = {name: _np.asarray(value) for name, value in inputs.items()}
    for name, parts in _TOGETHER.items():
        laid_out[name] = _np.concatenate([layout(laid_out.pop(part)) for part, layout in parts], axis=-1)
    for name, v in laid_out.items():
        v = _np.ascontiguousarray(_LAYOUT[name](v) if name in _LAYOUT else v)
        arrays[f"in_{name}_dram"] = v
        args[name] = nc.dram_tensor(f"in_{name}_dram", v.shape, _mybir.dt.from_np(v.dtype), kind="ExternalInput").ap()
    out = nc.dram_tensor("out_dram", (B, S, D), _mybir.dt.float32, kind="ExternalOutput").ap()
    build(nc, args, out)
    return _run(nc, [arrays], core_ids=[0]).results[0]["out_dram"]
```
